# Optimizing a Trainium2 kernel written in Bass

```python
import numpy as np
import jax
import jax.numpy as jnp

def _softmax(x, axis=-1):
    return jax.nn.softmax(x, axis=axis)

def _gelu(x):
    return jax.nn.gelu(x, approximate=True)

def _silu(x):
    return jax.nn.silu(x)

def _sigmoid(x):
    return jax.nn.sigmoid(x)

def _layernorm(x, axis=-1, eps=1e-05):
    m = jnp.mean(x, axis=axis, keepdims=True)
    v = jnp.var(x, axis=axis, keepdims=True)
    return (x - m) / jnp.sqrt(v + eps)

def _scatter_add(tgt, idx, src, axis=0):
    return tgt.at[idx].add(src)

def _segment_sum(src, seg, n):
    return jax.ops.segment_sum(src, seg, n)
kernel_name = 'mk_xattn_ffn_d1_seqx_r4_6cc75c'

def setup_inputs(seed: int=0):
    np.random.seed(seed)
    _w = jnp.asarray

    def _rec_inputs():
        import jax
        import jax.numpy as jnp
        _rk = jax.random.key(seed)
        x = -0.000125 + 0.9999 * jax.random.normal(jax.random.fold_in(_rk, 1), (4, 512, 512), jnp.float32)
        _lenS = 512 - jax.random.randint(jax.random.fold_in(_rk, 7), (4,), 0, max(1, 512 // 4) + 1, jnp.int32)
        _lenS2 = 1601 - jax.random.randint(jax.random.fold_in(_rk, 8), (4,), 0, max(1, 1601 // 4) + 1, jnp.int32)
        _ctx_2048P = jax.random.normal(jax.random.fold_in(_rk, 11), (4, 16, 512), jnp.float32)
        _ctx_2048c = jax.random.dirichlet(jax.random.fold_in(_rk, 511), 0.3 * jnp.ones((16,), jnp.float32), (4, 1601))
        _ctx_2048t = jnp.einsum('bsk,bkd->bsd', _ctx_2048c, _ctx_2048P)
        _ctx_2048t = _ctx_2048t * jax.lax.rsqrt(jnp.mean(jnp.square(_ctx_2048t)) + 1e-12) * 0.953939
        ctx_2048 = 1.72703e-05 + 1.00003 * (_ctx_2048t + 0.3 * jax.random.normal(jax.random.fold_in(_rk, 611), (4, 1601, 512), jnp.float32))
        return (x, ctx_2048)
    x, ctx_2048 = _rec_inputs()

    def _L0_xattn_setup():
        import jax, jax.numpy as jnp
        import numpy as np
        DIM = 512
        NH = 16
        HD = DIM // NH
        EPS = 1e-06
        IMG_LEN = 257

        def rms_norm(x, w, eps=EPS):
            xf = x.astype(jnp.float32)
            y = xf * jax.lax.rsqrt(jnp.mean(xf * xf, axis=-1, keepdims=True) + eps)
            return y.astype(x.dtype) * w

        def linear(x, w, b):
            return jnp.einsum('blc,oc->blo', x, w) + b

        def attention(q, k, v):
            scale = 1.0 / jnp.sqrt(jnp.asarray(HD, q.dtype))
            scores = jnp.einsum('bqhd,bkhd->bhqk', q, k) * scale
            probs = jax.nn.softmax(scores, axis=-1)
            return jnp.einsum('bhqk,bkhd->bqhd', probs, v)
        key = jax.random.key(seed)
        ks = jax.random.split(key, 12)
        B, L = (2, 2048)
        s = 0.02
        inp = {'x': jax.random.normal(ks[0], (B, L, DIM), jnp.float32), 'context': jax.random.normal(ks[1], (B, 769, DIM), jnp.float32), 'q_w': jax.random.normal(ks[2], (DIM, DIM), jnp.float32) * s, 'q_b': jnp.zeros((DIM,), jnp.float32), 'k_w': jax.random.normal(ks[3], (DIM, DIM), jnp.float32) * s, 'k_b': jnp.zeros((DIM,), jnp.float32), 'v_w': jax.random.normal(ks[4], (DIM, DIM), jnp.float32) * s, 'v_b': jnp.zeros((DIM,), jnp.float32), 'k_img_w': jax.random.normal(ks[5], (DIM, DIM), jnp.float32) * s, 'k_img_b': jnp.zeros((DIM,), jnp.float32), 'v_img_w': jax.random.normal(ks[6], (DIM, DIM), jnp.float32) * s, 'v_img_b': jnp.zeros((DIM,), jnp.float32), 'o_w': jax.random.normal(ks[7], (DIM, DIM), jnp.float32) * s, 'o_b': jnp.zeros((DIM,), jnp.float32), 'norm_q_w': jnp.ones((DIM,), jnp.float32), 'norm_k_w': jnp.ones((DIM,), jnp.float32), 'norm_k_img_w': jnp.ones((DIM,), jnp.float32)}
        return inp
    _L0_xattn_all = _L0_xattn_setup()
    _L0_xattn_in = {k: v for k, v in _L0_xattn_all.items() if k in ('q_w', 'q_b', 'k_w', 'k_b', 'v_w', 'v_b', 'k_img_w', 'k_img_b', 'v_img_w', 'v_img_b', 'o_w', 'o_b', 'norm_q_w', 'norm_k_w', 'norm_k_img_w')}
    del _L0_xattn_all

    def _L0_ffn_setup():
        import math
        import jax, jax.numpy as jnp
        import numpy as np
        from jax import lax
        D = 512
        I = 256
        E = 32
        K = 4
        NG = 8
        TKG = 3
        NSH = 2
        SCALE = 2.5
        CF = 1.25
        B, S = (2, 512)

        def _router(x, router_w, e_bias):
            scores = jax.nn.sigmoid(x @ router_w.T)
            sc = scores + e_bias[None, :]
            T = x.shape[0]
            gs = sc.reshape(T, NG, E // NG)
            group_scores = lax.top_k(gs, 2)[0].sum(-1)
            _, gidx = lax.top_k(group_scores, TKG)
            gmask = jnp.zeros((T, NG), sc.dtype).at[jnp.arange(T)[:, None], gidx].set(1.0)
            smask = jnp.repeat(gmask, E // NG, axis=1)
            masked = jnp.where(smask > 0, sc, 0.0)
            _, topk_idx = lax.top_k(masked, K)
            topk_w = jnp.take_along_axis(scores, topk_idx, axis=1)
            topk_w = topk_w / (topk_w.sum(-1, keepdims=True) + 1e-20)
            topk_w = topk_w * SCALE
            return (topk_idx.astype(jnp.int32), topk_w)

        def _moe_forward(hidden_states, router_w, e_bias, W_gate, W_up, W_down, shared_gate, shared_up, shared_down):
            b, s, d = hidden_states.shape
            T = b * s
            C = int(math.ceil(CF * T / E))
            EC = E * C
            x = hidden_states.reshape(T, d)
            topk_idx, topk_w = _router(x, router_w, e_bias)
            expert_flat = topk_idx.reshape(-1)
            w_flat = topk_w.reshape(-1)
            tok_flat = jnp.repeat(jnp.arange(T, dtype=jnp.int32), K)
            sort_ix = jnp.argsort(expert_flat)
            e_sorted = expert_flat[sort_ix]
            tok_s = tok_flat[sort_ix]
            w_s = w_flat[sort_ix]
            counts = jnp.zeros(E, jnp.int32).at[e_sorted].add(1)
            group_start = jnp.concatenate([jnp.zeros(1, jnp.int32), jnp.cumsum(counts)[:-1].astype(jnp.int32)])
            pos = jnp.arange(T * K, dtype=jnp.int32) - group_start[e_sorted]
            valid = pos < C
            dest = e_sorted * C + jnp.where(valid, pos, 0)
            slots_token = jnp.zeros(EC, jnp.int32).at[dest].add(jnp.where(valid, tok_s, 0))
            slots_w = jnp.zeros(EC, w_s.dtype).at[dest].add(jnp.where(valid, w_s, 0.0))
            Xp = x[slots_token].reshape(E, C, d)
            G = jnp.einsum('ecd,edi->eci', Xp, W_gate)
            U = jnp.einsum('ecd,edi->eci', Xp, W_up)
            Y = jnp.einsum('eci,eid->ecd', jax.nn.silu(G) * U, W_down)
            Yf = Y.reshape(EC, d) * slots_w[:, None]
            out = jnp.zeros((T, d), x.dtype).at[slots_token].add(Yf)
            shared = jax.nn.silu(x @ shared_gate.T) * (x @ shared_up.T) @ shared_down.T
            return (out + shared).reshape(b, s, d)
        key = jax.random.key(seed)
        ks = jax.random.split(key, 8)

        def rn(k, shape, scale=0.02):
            return jax.random.normal(k, shape, jnp.float32) * scale
        return {'hidden_states': jax.random.normal(ks[0], (B, S, D), jnp.float32), 'router_w': rn(ks[1], (E, D)), 'e_bias': jnp.zeros((E,), jnp.float32), 'W_gate': rn(ks[2], (E, D, I)), 'W_up': rn(ks[3], (E, D, I)), 'W_down': rn(ks[4], (E, I, D)), 'shared_gate': rn(ks[5], (I * NSH, D)), 'shared_up': rn(ks[6], (I * NSH, D)), 'shared_down': rn(ks[7], (D, I * NSH))}
    _L0_ffn_all = _L0_ffn_setup()
    _L0_ffn_in = {k: v for k, v in _L0_ffn_all.items() if k in ('router_w', 'e_bias', 'W_gate', 'W_up', 'W_down', 'shared_gate', 'shared_up', 'shared_down')}
    del _L0_ffn_all
    return {'x': x, 'ctx_2048': ctx_2048, 'L0_xattn_q_w': _L0_xattn_in['q_w'], 'L0_xattn_q_b': _L0_xattn_in['q_b'], 'L0_xattn_k_w': _L0_xattn_in['k_w'], 'L0_xattn_k_b': _L0_xattn_in['k_b'], 'L0_xattn_v_w': _L0_xattn_in['v_w'], 'L0_xattn_v_b': _L0_xattn_in['v_b'], 'L0_xattn_k_img_w': _L0_xattn_in['k_img_w'], 'L0_xattn_k_img_b': _L0_xattn_in['k_img_b'], 'L0_xattn_v_img_w': _L0_xattn_in['v_img_w'], 'L0_xattn_v_img_b': _L0_xattn_in['v_img_b'], 'L0_xattn_o_w': _L0_xattn_in['o_w'], 'L0_xattn_o_b': _L0_xattn_in['o_b'], 'L0_xattn_norm_q_w': _L0_xattn_in['norm_q_w'], 'L0_xattn_norm_k_w': _L0_xattn_in['norm_k_w'], 'L0_xattn_norm_k_img_w': _L0_xattn_in['norm_k_img_w'], 'L0_ffn_router_w': _L0_ffn_in['router_w'], 'L0_ffn_e_bias': _L0_ffn_in['e_bias'], 'L0_ffn_W_gate': _L0_ffn_in['W_gate'], 'L0_ffn_W_up': _L0_ffn_in['W_up'], 'L0_ffn_W_down': _L0_ffn_in['W_down'], 'L0_ffn_shared_gate': _L0_ffn_in['shared_gate'], 'L0_ffn_shared_up': _L0_ffn_in['shared_up'], 'L0_ffn_shared_down': _L0_ffn_in['shared_down']}

def reference(x, ctx_2048, L0_xattn_q_w, L0_xattn_q_b, L0_xattn_k_w, L0_xattn_k_b, L0_xattn_v_w, L0_xattn_v_b, L0_xattn_k_img_w, L0_xattn_k_img_b, L0_xattn_v_img_w, L0_xattn_v_img_b, L0_xattn_o_w, L0_xattn_o_b, L0_xattn_norm_q_w, L0_xattn_norm_k_w, L0_xattn_norm_k_img_w, L0_ffn_router_w, L0_ffn_e_bias, L0_ffn_W_gate, L0_ffn_W_up, L0_ffn_W_down, L0_ffn_shared_gate, L0_ffn_shared_up, L0_ffn_shared_down):
    import jax
    import jax.numpy as jnp

    def _L0_xattn_ref(x, context, q_w, q_b, k_w, k_b, v_w, v_b, k_img_w, k_img_b, v_img_w, v_img_b, o_w, o_b, norm_q_w, norm_k_w, norm_k_img_w):
        import jax, jax.numpy as jnp
        import numpy as np
        DIM = 512
        NH = 16
        HD = DIM // NH
        EPS = 1e-06
        IMG_LEN = 257

        def rms_norm(x, w, eps=EPS):
            xf = x.astype(jnp.float32)
            y = xf * jax.lax.rsqrt(jnp.mean(xf * xf, axis=-1, keepdims=True) + eps)
            return y.astype(x.dtype) * w

        def linear(x, w, b):
            return jnp.einsum('blc,oc->blo', x, w) + b

        def attention(q, k, v):
            scale = 1.0 / jnp.sqrt(jnp.asarray(HD, q.dtype))
            scores = jnp.einsum('bqhd,bkhd->bhqk', q, k) * scale
            probs = jax.nn.softmax(scores, axis=-1)
            return jnp.einsum('bhqk,bkhd->bqhd', probs, v)
        B, L, _ = x.shape
        ctx_img = context[:, :IMG_LEN]
        ctx_txt = context[:, IMG_LEN:]
        q = rms_norm(linear(x, q_w, q_b), norm_q_w).reshape(B, L, NH, HD)
        k = rms_norm(linear(ctx_txt, k_w, k_b), norm_k_w).reshape(B, -1, NH, HD)
        v = linear(ctx_txt, v_w, v_b).reshape(B, -1, NH, HD)
        k_img = rms_norm(linear(ctx_img, k_img_w, k_img_b), norm_k_img_w).reshape(B, -1, NH, HD)
        v_img = linear(ctx_img, v_img_w, v_img_b).reshape(B, -1, NH, HD)
        img_x = attention(q, k_img, v_img)
        txt_x = attention(q, k, v)
        out = (txt_x + img_x).reshape(B, L, DIM)
        return linear(out, o_w, o_b)

    def _L0_ffn_ref(hidden_states, router_w, e_bias, W_gate, W_up, W_down, shared_gate, shared_up, shared_down):
        import math
        import jax, jax.numpy as jnp
        import numpy as np
        from jax import lax
        D = 512
        I = 256
        E = 32
        K = 4
        NG = 8
        TKG = 3
        NSH = 2
        SCALE = 2.5
        CF = 1.25
        B, S = (2, 512)

        def _router(x, router_w, e_bias):
            scores = jax.nn.sigmoid(x @ router_w.T)
            sc = scores + e_bias[None, :]
            T = x.shape[0]
            gs = sc.reshape(T, NG, E // NG)
            group_scores = lax.top_k(gs, 2)[0].sum(-1)
            _, gidx = lax.top_k(group_scores, TKG)
            gmask = jnp.zeros((T, NG), sc.dtype).at[jnp.arange(T)[:, None], gidx].set(1.0)
            smask = jnp.repeat(gmask, E // NG, axis=1)
            masked = jnp.where(smask > 0, sc, 0.0)
            _, topk_idx = lax.top_k(masked, K)
            topk_w = jnp.take_along_axis(scores, topk_idx, axis=1)
            topk_w = topk_w / (topk_w.sum(-1, keepdims=True) + 1e-20)
            topk_w = topk_w * SCALE
            return (topk_idx.astype(jnp.int32), topk_w)

        def _moe_forward(hidden_states, router_w, e_bias, W_gate, W_up, W_down, shared_gate, shared_up, shared_down):
            b, s, d = hidden_states.shape
            T = b * s
            C = int(math.ceil(CF * T / E))
            EC = E * C
            x = hidden_states.reshape(T, d)
            topk_idx, topk_w = _router(x, router_w, e_bias)
            expert_flat = topk_idx.reshape(-1)
            w_flat = topk_w.reshape(-1)
            tok_flat = jnp.repeat(jnp.arange(T, dtype=jnp.int32), K)
            sort_ix = jnp.argsort(expert_flat)
            e_sorted = expert_flat[sort_ix]
            tok_s = tok_flat[sort_ix]
            w_s = w_flat[sort_ix]
            counts = jnp.zeros(E, jnp.int32).at[e_sorted].add(1)
            group_start = jnp.concatenate([jnp.zeros(1, jnp.int32), jnp.cumsum(counts)[:-1].astype(jnp.int32)])
            pos = jnp.arange(T * K, dtype=jnp.int32) - group_start[e_sorted]
            valid = pos < C
            dest = e_sorted * C + jnp.where(valid, pos, 0)
            slots_token = jnp.zeros(EC, jnp.int32).at[dest].add(jnp.where(valid, tok_s, 0))
            slots_w = jnp.zeros(EC, w_s.dtype).at[dest].add(jnp.where(valid, w_s, 0.0))
            Xp = x[slots_token].reshape(E, C, d)
            G = jnp.einsum('ecd,edi->eci', Xp, W_gate)
            U = jnp.einsum('ecd,edi->eci', Xp, W_up)
            Y = jnp.einsum('eci,eid->ecd', jax.nn.silu(G) * U, W_down)
            Yf = Y.reshape(EC, d) * slots_w[:, None]
            out = jnp.zeros((T, d), x.dtype).at[slots_token].add(Yf)
            shared = jax.nn.silu(x @ shared_gate.T) * (x @ shared_up.T) @ shared_down.T
            return (out + shared).reshape(b, s, d)
        return _moe_forward(hidden_states, router_w, e_bias, W_gate, W_up, W_down, shared_gate, shared_up, shared_down)
    x = x + _L0_xattn_ref(_layernorm(x, axis=-1), ctx_2048, L0_xattn_q_w, L0_xattn_q_b, L0_xattn_k_w, L0_xattn_k_b, L0_xattn_v_w, L0_xattn_v_b, L0_xattn_k_img_w, L0_xattn_k_img_b, L0_xattn_v_img_w, L0_xattn_v_img_b, L0_xattn_o_w, L0_xattn_o_b, L0_xattn_norm_q_w, L0_xattn_norm_k_w, L0_xattn_norm_k_img_w)
    x = x + _L0_ffn_ref(_layernorm(x, axis=-1), L0_ffn_router_w, L0_ffn_e_bias, L0_ffn_W_gate, L0_ffn_W_up, L0_ffn_W_down, L0_ffn_shared_gate, L0_ffn_shared_up, L0_ffn_shared_down)
    return x

_drawn_inputs = setup_inputs


def setup_inputs(seed=0):
    import zlib

    import numpy as np

    out = dict(_drawn_inputs(seed))
    spreads = {'L0_xattn_q_b': (0.0, 0.651),
     'L0_xattn_k_b': (0.0, 0.8),
     'L0_xattn_v_b': (0.0, 0.1),
     'L0_xattn_k_img_b': (0.0, 0.8),
     'L0_xattn_v_img_b': (0.0, 0.1),
     'L0_xattn_o_b': (0.0, 0.1),
     'L0_xattn_norm_q_w': (1.0, 0.6),
     'L0_xattn_norm_k_w': (1.0, 0.6),
     'L0_xattn_norm_k_img_w': (1.0, 0.6),
     'L0_ffn_e_bias': (0.0, 0.336)}
    factors = {'L0_ffn_router_w': 3.084,
     'L0_ffn_W_gate': 2.881,
     'L0_ffn_W_up': 2.832,
     'L0_ffn_W_down': 2.833}
    for name, (base, spread) in spreads.items():
        noise = np.random.default_rng([zlib.crc32(name.encode()), seed]).standard_normal(out[name].shape)
        drawn = base * np.exp(spread * noise) if base else spread * noise
        out[name] = jnp.asarray(drawn.astype(out[name].dtype))
    for name, factor in factors.items():
        out[name] = (out[name] * factor).astype(out[name].dtype)
    return out
```

```python
from contextlib import ExitStack

import numpy as np

import concourse.bass as bass
from concourse import mybir

ALU = mybir.AluOpType
ACT = mybir.ActivationFunctionType
F32 = mybir.dt.float32
F16 = mybir.dt.float16
U32 = mybir.dt.uint32

P = 128
B, L, D = 4, 512, 512
T = B * L
NC = D // P
HEADS, HD = 16, 32
NG = HEADS // 4
TXT, IMG = 1344, 257
KT = 13
KPAD = KT * P
MIX = TXT // P
SPLIT = TXT - MIX * P
LAST = TXT + IMG - (KT - 1) * P
QT = L // P
POS = KT + QT
WS = 256.0
STK = 3 * HD
SHIFT = 16.0
SCALE = 1.0 / float(np.sqrt(HD))


class Event:

    def __init__(self, ctx, nc, name, ahead=0):
        self.sem = ctx.enter_context(nc.semaphore(name))
        self.ahead = ahead

    def wait(self, eng, n):
        if not (isinstance(n, int) and n + self.ahead <= 0):
            eng.wait_ge(self.sem, n + self.ahead)


def attention_program(nc, d, x1_dram):
    with ExitStack() as ctx:
        def sb(name, shape, dt):
            return ctx.enter_context(nc.sbuf_tensor(name, shape, dt))

        def event(name, ahead=0):
            e = Event(ctx, nc, name, ahead)
            events.append(e)
            return e

        s_apart = ctx.enter_context(nc.semaphore("s_apart"))

        def apart(eng):
            eng.sem_inc(s_apart, 1)

        events = []
        wts = sb("wts", [P, 6, 2, NC * D], F16)
        WQ, WK, WV, WKI, WVI, WO = range(6)
        vec = sb("vec", [P, 12, D], F32)
        KB, KW, VB = 0, 3, 6
        QB, QW, OB = 9, 10, 11
        keys = sb("keys", [P, HEADS, KPAD], F16)
        vals = sb("vals", [P, KT, D], F32)
        quer = sb("quer", [P, HEADS, L], F16)
        vgrp = sb("vgrp", [P, KT, P], F32)
        attn = sb("attn", [P, 2, NG, L], F16)
        xres = sb("xres", [P, 2, D], F32)
        work = sb("work", [P, 11 * D], F32)
        ident = sb("ident", [P, P], F16)
        ones = sb("ones", [P, HD], F32)
        small = sb("small", [P, 24], F32)
        ps = ctx.enter_context(nc.psum_tensor("ps", [P, 8, 512], F32))

        raw = [work[:, i * D:(i + 1) * D] for i in range(2)]
        hl = [work[:, (2 + i) * D:(3 + i) * D].bitcast(F16).rearrange("p (s n) -> p s n", s=2) for i in range(2)]
        kraw = work[:, 4 * D:5 * D]
        knorm = work[:, 5 * D:6 * D]
        xnorm = work[:, 6 * D:7 * D]
        xs = work[:, 7 * D:8 * D].bitcast(F16).rearrange("p (s n) -> p s n", s=2)
        stw = HEADS * STK // 2
        stack = [work[:, 8 * D + i * stw:8 * D + (i + 1) * stw].bitcast(F16).rearrange("p (h r) -> p h r", h=HEADS)
                 for i in range(2)]
        prob = work[:, 0:8 * D].rearrange("p (s h q) -> p s h q", s=2, h=4)
        rden = work[:, 8 * D:9 * D]
        oimg = work[:, 9 * D:10 * D]
        mx = work[:, 8 * D:8 * D + P].rearrange("p (s h t) -> p s h t", s=2, h=HEADS)
        mh = work[:, 9 * D:9 * D + P // 2].bitcast(F16)
        mrow = work[:, 10 * D:10 * D + P // 2].bitcast(F16)
        wstage = [work[:, i * 4 * D:(i + 1) * 4 * D] for i in range(2)]
        ssq, rin, rtmp, st6, mv, rs, rs2 = (small[:, 0:1], small[:, 1:2], small[:, 2:3], small[:, 4:10],
                                            small[:, 10:12], small[:, 12:13], small[:, 13:14])
        mhalf = small[:, 14:15]

        turned = ps[:, 4:6, :].rearrange("p a n -> p (a n)").bitcast(F16).rearrange("p (h k) -> p h k", h=HEADS)
        xturned = ps[:, 6, :].bitcast(F16)
        NUM_T, DEN_T, NUM_I, DEN_I = 4, 5, 6, 7

        s_w = [ctx.enter_context(nc.semaphore(f"s_w{i}")) for i in range(2)]
        s_c = ctx.enter_context(nc.semaphore("s_c"))
        s_in = [ctx.enter_context(nc.semaphore(f"s_in{i}")) for i in range(2)]
        s_x = [ctx.enter_context(nc.semaphore(f"s_x{i}")) for i in range(2)]
        s_st = [ctx.enter_context(nc.semaphore(f"s_st{i}")) for i in range(2)]
        s_mx = ctx.enter_context(nc.semaphore("s_mx"))
        s_i0 = event("s_i0")
        s_const = event("s_const")
        whi, wlo = event("whi"), event("wlo")
        e_hi = event("e_hi")
        e_hl = event("e_hl")
        e_pv = event("e_pv", 2)
        e_pk = event("e_pk", 2)
        e_kr = event("e_kr")
        e_ssq = event("e_ssq")
        e_rt = event("e_rt")
        e_rin = event("e_rin")
        e_kn = event("e_kn")
        e_c0 = event("e_c0")
        e_c1 = event("e_c1", 1)
        e_lo = event("e_lo")
        e_t = event("e_t", 2)
        e_td = event("e_td", 1)
        e_ta = event("e_ta", 1)
        e_v = event("e_v", 2)
        e_st = event("e_st")
        e_mv = event("e_mv")
        e_rv = event("e_rv")
        e_rs = event("e_rs")
        e_xn = event("e_xn")
        e_xs = event("e_xs")
        e_xt = event("e_xt")
        e_ms = event("e_ms")
        e_mt, e_mi = event("e_mt"), event("e_mi", 2)
        e_mh = event("e_mh")
        e_mr = event("e_mr")
        e_mc = event("e_mc")
        e_vg = event("e_vg", 1)
        e_s = event("e_s")
        e_e = event("e_e", 2)
        e_av = event("e_av", 13)
        e_ri = event("e_ri")
        e_oi = event("e_oi", 1)
        e_rt2 = event("e_rt2")
        e_ot = event("e_ot", 1)
        e_os = event("e_os")
        e_oh = event("e_oh")
        e_at = event("e_at", 1)
        e_po = event("e_po")
        e_ob = event("e_ob")
        e_x1 = event("e_x1", 2)
        e_b = event("e_b", 1)

        block = ctx.enter_context(nc.Block())

        def kind(pos):
            return 0 if pos < MIX else 1 if pos == MIX else 2

        def is_q(pos):
            return pos >= KT

        def slots(b, pos):
            return (b * ((POS + 1) // 2) if pos % 2 == 0 else b * (POS // 2)) + pos // 2 + 1

        PAIRS = 4

        @block.sync
        def _(sp):
            for e in events:
                if e.ahead:
                    sp.sem_inc(e.sem, e.ahead)
            for i in range(6):
                if i >= 2:
                    wlo.wait(sp, i - 1)
                sp.dma_start(wstage[i % 2], d["w6"][i]).then_inc(s_w[i % 2], 16)
            srcs = [(k, d[n]) for k, n in ((KB, "kb"), (KW, "kw"), (VB, "vb"))]
            irng = {KB: "kib", KW: "kiw", VB: "vib"}
            for k, txt in srcs:
                img = d[irng[k]]
                sp.dma_start(vec[:, k, :], txt.partition_broadcast(P)).then_inc(s_c, 16)
                sp.dma_start(vec[0:SPLIT, k + 1, :], txt.partition_broadcast(SPLIT)).then_inc(s_c, 16)
                sp.dma_start(vec[SPLIT:P, k + 1, :], img.partition_broadcast(P - SPLIT)).then_inc(s_c, 16)
                sp.dma_start(vec[:, k + 2, :], img.partition_broadcast(P)).then_inc(s_c, 16)
            for k, n in ((QB, "qb"), (QW, "qw"), (OB, "ob")):
                sp.dma_start(vec[:, k, :], d[n].partition_broadcast(P)).then_inc(s_c, 16)
            for h in range(HEADS):
                sp.dma_start(keys[STK:P, h, :], d["mark"]).then_inc(s_c, 16)
            wlo.wait(sp, 6)

            with sp.Fori(0, B) as b:
                e_b.wait(sp, b)

                def load(b, pos, q_tile=None, key_tile=None):
                    if q_tile is not None:
                        src = d["x"][bass.ds(b * L + q_tile * P, P), :]
                    else:
                        src = d["ctx"][bass.ds(b * KT + key_tile, 1)].rearrange("a p n -> (a p) n")
                    sp.dma_start(raw[pos % 2], src).then_inc(s_in[pos % 2], 16)

                load(b, 0, key_tile=0)
                load(b, 1, key_tile=1)
                with sp.Fori(0, PAIRS) as i:
                    for u in range(2):
                        e_hl.wait(sp, b * POS + i * 2 + u + 1)
                        load(b, u, key_tile=i * 2 + u + 2)
                for pos in range(2 * PAIRS, POS - 2):
                    if is_q(pos):
                        e_xn.wait(sp, b * QT + pos - KT + 1)
                    else:
                        e_hl.wait(sp, b * POS + pos + 1)
                    nxt = pos + 2
                    load(b, nxt, **({"q_tile": nxt - KT} if is_q(nxt) else {"key_tile": nxt}))
                e_mc.wait(sp, b + 1)
                for k in range(2):
                    sp.dma_start(quer[STK + k:STK + k + 1, :, :].rearrange("p h (t q) -> p (h t) q", q=P),
                                 mrow[k * (P // 2):(k + 1) * (P // 2), :]).then_inc(s_mx, 16)
                for j in range(QT):
                    if j >= 2:
                        sp.wait_ge(s_st[j % 2], b * 32 + 16 * (j // 2))
                    sp.dma_start(xres[:, j % 2, :], d["x"][bass.ds(b * L + j * P, P), :]).then_inc(s_x[j % 2], 16)
                    if j >= 1:
                        e_x1.wait(sp, b * QT + j)
                        sp.dma_start(x1_dram[bass.ds(b * L + (j - 1) * P, P), :],
                                     xres[:, (j - 1) % 2, :]).then_inc(s_st[(j - 1) % 2], 16)
                e_x1.wait(sp, b * QT + QT)
                sp.dma_start(x1_dram[bass.ds(b * L + (QT - 1) * P, P), :],
                             xres[:, (QT - 1) % 2, :]).then_inc(s_st[(QT - 1) % 2], 16)
                for s in s_st:
                    sp.wait_ge(s, b * 32 + 32)
                sp.sem_inc(e_b.sem, 1)

        @block.gpsimd
        def _(pool):
            pool.memset(ident[:, :], 0.0).then_inc(s_i0.sem, 1)
            s_i0.wait(pool, 1)
            pool.affine_select(out=ident[:, :], in_=ident[:, :], pattern=[[-1, P]], compare_op=ALU.not_equal, fill=1.0,
                               base=0, channel_multiplier=1).then_inc(s_const.sem, 1)
            pool.memset(mhalf, -0.5).then_inc(s_const.sem, 1)
            s_const.wait(pool, 4)

            def rinv(n):
                e_ssq.wait(pool, n)
                apart(pool)
                pool.tensor_scalar(rtmp, ssq, 1.0 / D, 1e-6, ALU.mult, ALU.add).then_inc(e_rt.sem, 1)
                e_rt.wait(pool, n)
                pool.tensor_tensor(rin, rtmp, mhalf, ALU.pow).then_inc(e_rin.sem, 1)

            def rstd(m):
                e_mv.wait(pool, m)
                apart(pool)
                pool.tensor_scalar(rs2, mv[:, 1:2], 1.0, 1e-5, ALU.mult, ALU.add).then_inc(e_rv.sem, 1)
                e_rv.wait(pool, m)
                pool.tensor_tensor(rs, rs2, mhalf, ALU.pow).then_inc(e_rs.sem, 1)

            with pool.Fori(0, B) as b:
                with pool.Fori(0, 2 * PAIRS) as i:
                    rinv(b * POS + i + 1)
                for pos in range(2 * PAIRS, POS):
                    if pos + 1 < POS and is_q(pos + 1):
                        rstd(b * QT + pos + 1 - KT + 1)
                    rinv(b * POS + pos + 1)
                e_v.wait(pool, b * KT + KT)
                apart(pool)
                with pool.Fori(0, NG) as g:
                    gg = pool.snap(b * NG + g)
                    for n, t in enumerate(ORDER):
                        e_av.wait(pool, gg * KT + n + 1 - KT)
                        pool.tensor_copy(vgrp[:, t, :], vals[:, t, bass.ds(g * P, P)]).then_inc(e_vg.sem, 1)

        @block.scalar
        def _(act):
            for i in range(6):
                act.wait_ge(s_w[i % 2], 16 * (i // 2 + 1))
                act.activation(wts[:, i, 0, :], wstage[i % 2], ACT.Copy, scale=WS).then_inc(whi.sem, 1)

            def high(n, pos, b):
                if is_q(pos):
                    e_xn.wait(act, b * QT + pos - KT + 1)
                    act.copy(xs[:, 0, :], xnorm).then_inc(e_hi.sem, 1)
                else:
                    act.wait_ge(s_in[pos % 2], 16 * slots_of(pos, n, b))
                    e_pk.wait(act, n - 2)
                    act.copy(hl[pos % 2][:, 0, :], raw[pos % 2]).then_inc(e_hi.sem, 1)

            def store_turned(n, tile, q):
                e_t.wait(act, n)
                dst = quer if q else keys
                act.copy(dst[0:STK, 0:8, bass.ds(tile * P, P)], turned[0:STK, 0:8, :]).then_inc(e_ta.sem, 1)

            def turn(n, pos, b, tile, prev):
                if pos + 1 < POS:
                    high(n + 1, pos + 1, b)
                e_kr.wait(act, n)
                act.activation(ps[:, 7, :], kraw, ACT.Square, accum_out=ssq).then_inc(e_ssq.sem, 1)
                if prev is not None:
                    store_turned(n - 1, *prev)
                e_kn.wait(act, n)
                e_t.wait(act, n - 2)
                st = stack[pos % 2]
                kn = knorm.rearrange("p (h d) -> p h d", h=HEADS)
                second = 2 if is_q(pos) else 1
                act.copy(st[:, :, 0:HD], kn).then_inc(e_c0.sem, 1)
                act.copy(st[:, :, second * HD:(second + 1) * HD], kn).then_inc(e_c1.sem, 1)

            def slots_of(pos, n, b):
                return slots(b, pos) if not isinstance(pos, tuple) else None

            with act.Fori(0, B) as b:
                act.wait_ge(s_in[0], 16 * slots(b, 0))
                e_pk.wait(act, b * POS - 1)
                act.copy(hl[0][:, 0, :], raw[0]).then_inc(e_hi.sem, 1)
                turn(b * POS + 1, 0, b, 0, None)
                with act.Fori(0, PAIRS) as i:
                    for u in range(2):
                        n = act.snap(b * POS + i * 2 + u + 2)
                        s = (u + 2) % 2
                        act.wait_ge(s_in[s], 16 * (slots(b, s) + i + (1 if u == 0 else 1)))
                        e_pk.wait(act, n - 1)
                        act.copy(hl[s][:, 0, :], raw[s]).then_inc(e_hi.sem, 1)
                        e_kr.wait(act, n)
                        act.activation(ps[:, 7, :], kraw, ACT.Square, accum_out=ssq).then_inc(e_ssq.sem, 1)
                        store_turned(n - 1, i * 2 + u, False)
                        e_kn.wait(act, n)
                        e_t.wait(act, n - 2)
                        kn = knorm.rearrange("p (h d) -> p h d", h=HEADS)
                        act.copy(stack[1 - u][:, :, 0:HD], kn).then_inc(e_c0.sem, 1)
                        act.copy(stack[1 - u][:, :, HD:2 * HD], kn).then_inc(e_c1.sem, 1)
                for pos in range(2 * PAIRS + 1, POS):
                    q = pos - 1 >= KT
                    turn(b * POS + pos + 1, pos, b, None, (pos - 1 - KT if q else pos - 1, q))
                store_turned(b * POS + POS, QT - 1, True)
                with act.Fori(0, NG) as g:
                    gg = act.snap(b * NG + g)
                    for n, t in enumerate(ORDER):
                        rows = LAST if t == KT - 1 else P
                        for half in range(2):
                            e_s.wait(act, gg * 2 * KT + 2 * n + half + 1)
                            e_av.wait(act, gg * KT + n - 1)
                            act.activation(prob[0:rows, n % 2, 2 * half:2 * half + 2, :],
                                           ps[0:rows, 2 * half:2 * half + 2, :], ACT.Exp,
                                           scale=SCALE).then_inc(e_e.sem, 1)

        @block.vector
        def _(dve):
            dve.memset(ones[:, :], 1.0).then_inc(s_const.sem, 1)
            dve.memset(quer[STK:P, :, :], 0.0).then_inc(s_const.sem, 1)
            for i in range(6):
                whi.wait(dve, i + 1)
                dve.scalar_tensor_tensor(wts[:, i, 1, :], wstage[i % 2], WS, wts[:, i, 0, :], ALU.mult,
                                         ALU.subtract).then_inc(wlo.sem, 1)
            dve.wait_ge(s_c, 16 * (12 + 3 + HEADS))

            def low(s, n, count):
                e_hi.wait(dve, n)
                dve.tensor_tensor(hl[s][:, 1, :], raw[s], hl[s][:, 0, :], ALU.subtract).then_inc(e_hl.sem, 1)

            def norm_x(pos, n, b):
                m = dve.snap(b * QT + pos - KT + 1)
                dve.wait_ge(s_in[pos % 2], 16 * slots(b, pos))
                dve.bn_stats(st6, raw[pos % 2]).then_inc(e_st.sem, 1)
                e_st.wait(dve, m)
                apart(dve)
                dve.bn_aggr(mv, st6).then_inc(e_mv.sem, 1)
                e_rs.wait(dve, m)
                dve.tensor_scalar(xnorm, raw[pos % 2], mv[:, 0:1], rs, ALU.subtract, ALU.mult).then_inc(e_xn.sem, 1)
                e_hi.wait(dve, n)
                dve.tensor_tensor(xs[:, 1, :], xnorm, xs[:, 0, :], ALU.subtract).then_inc(e_xs.sem, 1)

            def tile(n, s, bias, weight, value, prep, prev, after):
                prep()
                e_pk.wait(dve, n)
                dve.scalar_tensor_tensor(kraw, ps[:, s, :], 1.0 / WS, vec[:, bias, :], ALU.mult,
                                         ALU.add).then_inc(e_kr.sem, 1)
                if value is not None:
                    vb, t, m = value
                    dve.scalar_tensor_tensor(vals[:, bass.ds(t, 1), :].rearrange("p a n -> p (a n)"), ps[:, 2 + s, :],
                                             1.0 / WS, vec[:, vb, :], ALU.mult, ALU.add).then_inc(e_v.sem, 1)
                after()
                if prev is not None:
                    store_turned(n - 1, *prev)
                e_rin.wait(dve, n)
                e_c1.wait(dve, n - 1)
                dve.scalar_tensor_tensor(knorm, kraw, rin, vec[:, weight, :], ALU.mult, ALU.mult).then_inc(e_kn.sem, 1)
                e_c0.wait(dve, n)
                st = stack[s]
                kn = knorm.rearrange("p (h d) -> p h d", h=HEADS)
                third = 1 if value is None else 2
                dve.tensor_tensor(st[:, :, third * HD:(third + 1) * HD], kn, st[:, :, 0:HD],
                                  ALU.subtract).then_inc(e_lo.sem, 1)

            def store_turned(n, tile, q):
                e_t.wait(dve, n)
                dst = quer if q else keys
                dve.tensor_copy(dst[0:STK, 8:16, bass.ds(tile * P, P)], turned[0:STK, 8:16, :]).then_inc(e_td.sem, 1)

            def nothing():
                pass

            with dve.Fori(0, B) as b:
                e_vg.wait(dve, b * NG * KT)
                low(0, b * POS + 1, None)
                tile(b * POS + 1, 0, KB, KW, (VB, 0, None), lambda: low(1, b * POS + 2, None), None, nothing)
                with dve.Fori(0, PAIRS) as i:
                    for u in range(2):
                        n = dve.snap(b * POS + i * 2 + u + 2)
                        tile(n, 1 - u, KB, KW, (VB, i * 2 + u + 1, None), lambda: low(u, n + 1, None),
                             (i * 2 + u, False), nothing)
                for pos in range(2 * PAIRS + 1, POS):
                    n = dve.snap(b * POS + pos + 1)
                    nxt = pos + 1
                    prep, after = nothing, nothing
                    if nxt < POS and is_q(nxt):
                        prep = lambda: norm_x(nxt, n + 1, b)

                        def after():
                            e_xt.wait(dve, b * QT + nxt - KT + 1)
                            e_pk.wait(dve, n - 1)
                            dve.tensor_copy(hl[nxt % 2].rearrange("p s n -> p (s n)"), xturned).then_inc(e_hl.sem, 1)
                    elif nxt < POS:
                        prep = lambda: low(nxt % 2, n + 1, None)
                    q = pos - 1 >= KT
                    prev = (pos - 1 - KT if q else pos - 1, q)
                    if is_q(pos):
                        tile(n, pos % 2, QB, QW, None, prep, prev, after)
                    else:
                        k = kind(pos)
                        tile(n, pos % 2, KB + k, KW + k, (VB + k, pos, None), prep, prev, after)
                store_turned(b * POS + POS, QT - 1, True)
                with dve.Fori(0, HEADS) as h:
                    for t in range(QT):
                        k = dve.snap(b * HEADS * QT + h * QT + t + 1)
                        bank = 4 * (t % 2)
                        e_ms.wait(dve, k)
                        for kd, (a, z, e) in enumerate(((0, TXT, e_mt), (1536, 1536 + IMG, e_mi))):
                            dve.tensor_reduce(mx[:, kd, bass.ds(h, 1), t],
                                              ps[:, bank:bank + 4, :].rearrange("p a n -> p (a n)")[:, a:z],
                                              mybir.AxisListType.X, ALU.max).then_inc(e.sem, 1)
                e_mt.wait(dve, b * HEADS * QT + HEADS * QT)
                e_mi.wait(dve, b * HEADS * QT + HEADS * QT)
                dve.tensor_scalar(mh, mx.rearrange("p s h t -> p (s h t)"), -1.0 / SHIFT, None,
                                  ALU.mult).then_inc(e_mh.sem, 1)
                e_mr.wait(dve, b + 1)
                dve.tensor_copy(mrow, ps[:, 0, 0:P // 2].bitcast(F16)).then_inc(e_mc.sem, 1)
                with dve.Fori(0, NG) as g:
                    gg = dve.snap(b * NG + g + 1)
                    e_av.wait(dve, gg * KT + ORDER.index(MIX) + 1 - KT)
                    e_at.wait(dve, gg - 1)
                    dve.reciprocal(rden, ps[:, DEN_I, :]).then_inc(e_ri.sem, 1)
                    e_ri.wait(dve, gg)
                    dve.tensor_tensor(oimg, ps[:, NUM_I, :], rden, ALU.mult).then_inc(e_oi.sem, 1)
                    e_av.wait(dve, gg * KT)
                    e_oi.wait(dve, gg)
                    dve.reciprocal(rden, ps[:, DEN_T, :]).then_inc(e_rt2.sem, 1)
                    e_rt2.wait(dve, gg)
                    dve.tensor_tensor(rden, ps[:, NUM_T, :], rden, ALU.mult).then_inc(e_ot.sem, 1)
                    e_ot.wait(dve, gg)
                    dve.tensor_tensor(rden, rden, oimg, ALU.add).then_inc(e_os.sem, 1)
                    e_os.wait(dve, gg)
                    dve.tensor_copy(attn[:, 0, bass.ds(g, 1), :].rearrange("p a n -> p (a n)"),
                                    rden).then_inc(e_oh.sem, 1)
                    e_oh.wait(dve, gg)
                    dve.tensor_tensor(attn[:, 1, bass.ds(g, 1), :].rearrange("p a n -> p (a n)"), rden,
                                      attn[:, 0, bass.ds(g, 1), :].rearrange("p a n -> p (a n)"),
                                      ALU.subtract).then_inc(e_at.sem, 1)
                for j in range(QT):
                    m = b * QT + j + 1
                    e_po.wait(dve, m)
                    e_x1.wait(dve, m - 1)
                    dve.scalar_tensor_tensor(oimg, ps[:, j % 2, :], 1.0 / WS, vec[:, OB, :], ALU.mult,
                                             ALU.add).then_inc(e_ob.sem, 1)
                    e_ob.wait(dve, m)
                    dve.wait_ge(s_x[j % 2], 16 * (b * 2 + j // 2 + 1))
                    dve.tensor_tensor(xres[:, j % 2, :], xres[:, j % 2, :], oimg, ALU.add).then_inc(e_x1.sem, 1)

        @block.tensor
        def _(pe):
            s_const.wait(pe, 4)
            wlo.wait(pe, 6)

            def product(out, lhs, w, cols=slice(0, P)):
                steps = [(c, a, z) for c in range(NC) for a, z in ((0, 0), (0, 1), (1, 0))]
                for k, (c, a, z) in enumerate(steps):
                    mm = pe.matmul(out, lhs(a, c)[:, cols], wts[:, w, z, c * D:(c + 1) * D],
                                   start=(k == 0), stop=(k == len(steps) - 1))
                return mm

            def project(n, s, pos):
                e_hl.wait(pe, n)
                lhs = lambda a, c: hl[s][:, a, c * P:(c + 1) * P]
                if is_q(pos):
                    product(ps[:, s, :], lhs, WQ).then_inc(e_pk.sem, 1)
                elif kind(pos) == 1:
                    lo, hi = slice(0, SPLIT), slice(SPLIT, P)
                    product(ps[0:SPLIT, 2 + s, :], lhs, WV, lo)
                    product(ps[SPLIT:P, 2 + s, :], lhs, WVI, hi).then_inc(e_pv.sem, 1)
                    product(ps[0:SPLIT, s, :], lhs, WK, lo)
                    product(ps[SPLIT:P, s, :], lhs, WKI, hi).then_inc(e_pk.sem, 1)
                else:
                    txt = kind(pos) == 0
                    product(ps[:, 2 + s, :], lhs, WV if txt else WVI).then_inc(e_pv.sem, 1)
                    product(ps[:, s, :], lhs, WK if txt else WKI).then_inc(e_pk.sem, 1)

            def turn_stacks(n, s):
                e_lo.wait(pe, n)
                e_c1.wait(pe, n)
                e_td.wait(pe, n - 1)
                e_ta.wait(pe, n - 1)
                for h in range(HEADS):
                    tr = pe.transpose(turned[0:STK, h, :], stack[s][:, h, :], ident[:, :])
                tr.then_inc(e_t.sem, 1)

            def turn_x(m):
                e_xs.wait(pe, m)
                for a in range(2):
                    for c in range(NC):
                        tr = pe.transpose(xturned[:, (a * NC + c) * P:(a * NC + c + 1) * P],
                                          xs[:, a, c * P:(c + 1) * P], ident[:, :])
                tr.then_inc(e_xt.sem, 1)

            with pe.Fori(0, B) as b:
                e_ot.wait(pe, b * NG)
                e_x1.wait(pe, b * QT)
                project(b * POS + 1, 0, 0)
                with pe.Fori(0, PAIRS) as i:
                    for u in range(2):
                        n = pe.snap(b * POS + i * 2 + u + 2)
                        project(n, 1 - u, 0)
                        turn_stacks(n - 1, u)
                for pos in range(2 * PAIRS + 1, POS):
                    n = pe.snap(b * POS + pos + 1)
                    project(n, pos % 2, pos)
                    if pos + 1 < POS and is_q(pos + 1):
                        turn_x(b * QT + pos + 1 - KT + 1)
                    turn_stacks(n - 1, (pos - 1) % 2)
                turn_stacks(b * POS + POS, (POS - 1) % 2)
                e_td.wait(pe, b * POS + POS)
                e_ta.wait(pe, b * POS + POS)
                apart(pe)
                with pe.Fori(0, HEADS) as h:
                    for t in range(QT):
                        k = pe.snap(b * HEADS * QT + h * QT + t + 1)
                        bank = 4 * (t % 2)
                        e_mi.wait(pe, k - 2)
                        for c, (a, z) in enumerate(((0, 512), (512, 1024), (1024, TXT), (TXT, TXT + IMG))):
                            mm = pe.matmul(ps[:, bank + c, 0:z - a],
                                           quer[0:STK, bass.ds(h, 1), t * P:(t + 1) * P].rearrange("p a n -> p (a n)"),
                                           keys[0:STK, bass.ds(h, 1), a:z].rearrange("p a n -> p (a n)"),
                                           start=True, stop=True)
                        mm.then_inc(e_ms.sem, 1)
                e_mh.wait(pe, b + 1)
                pe.transpose(ps[:, 0, 0:P // 2].bitcast(F16), mh, ident[:, :]).then_inc(e_mr.sem, 1)
                pe.wait_ge(s_mx, b * 32 + 32)
                apart(pe)

                with pe.Fori(0, NG) as g:
                    gg = pe.snap(b * NG + g)

                    def scores(n, half):
                        t = ORDER[n]
                        rows = LAST if t == KT - 1 else P
                        e_e.wait(pe, gg * 2 * KT + 2 * n + half - 1)
                        for h in range(2 * half, 2 * half + 2):
                            mm = pe.matmul(ps[0:rows, h, :],
                                           keys[:, bass.ds(g * 4 + h, 1), t * P:t * P + rows].rearrange("p a n -> p (a n)"),
                                           quer[:, bass.ds(g * 4 + h, 1), :].rearrange("p a n -> p (a n)"),
                                           start=True, stop=True)
                        mm.then_inc(e_s.sem, 1)

                    def sums(n, what):
                        t = ORDER[n]
                        parts = {KT - 1: [(0, LAST, 1)], MIX: [(SPLIT, P, 1), (0, SPLIT, 0)]}.get(
                            t, [(0, P, 1 if t > MIX else 0)])
                        for a, z, img in parts:
                            bank = (NUM_I if img else NUM_T) + what
                            first = n == 0 if img else t == MIX
                            last = t == MIX if img else n == KT - 1
                            for h in range(4):
                                w = ones[a:z, :] if what else vgrp[a:z, t, h * HD:(h + 1) * HD]
                                mm = pe.matmul(ps[h * HD:(h + 1) * HD, bank, :], w, prob[a:z, n % 2, h, :],
                                               start=first, stop=last)
                        return mm

                    scores(0, 0)
                    scores(0, 1)
                    for n in range(KT):
                        if n + 1 < KT:
                            scores(n + 1, 0)
                        e_vg.wait(pe, gg * KT + n + 1)
                        e_e.wait(pe, gg * 2 * KT + 2 * n + 2)
                        if n == 0:
                            e_oi.wait(pe, gg)
                        if ORDER[n] == MIX:
                            e_ot.wait(pe, gg)
                            apart(pe)
                        sums(n, 0)
                        if n + 1 < KT:
                            scores(n + 1, 1)
                        sums(n, 1).then_inc(e_av.sem, 1)
                e_at.wait(pe, b * NG + NG)
                for j in range(QT):
                    if j >= 2:
                        e_ob.wait(pe, b * QT + j - 1)
                    product(ps[:, j % 2, :], lambda a, c: attn[:, a, c, j * P:(j + 1) * P], WO).then_inc(e_po.sem, 1)


ORDER = [KT - 2, KT - 1, MIX] + list(range(MIX))


_ORDER_OF_W = ("q_w", "k_w", "v_w", "k_img_w", "v_img_w", "o_w")


def lay_attention(inputs):
    a = {k[len("L0_xattn_"):]: np.asarray(v) for k, v in inputs.items() if k.startswith("L0_xattn_")}
    w6 = np.stack([a[n].T.reshape(NC, P, D).transpose(1, 0, 2).reshape(P, NC * D) for n in _ORDER_OF_W])
    c = np.asarray(inputs["ctx_2048"])
    c = np.concatenate([c[:, IMG:], c[:, :IMG], np.zeros((B, KPAD - TXT - IMG, D), c.dtype)], axis=1)
    c = c.reshape(B, KT, P, NC, P).transpose(0, 1, 4, 3, 2).reshape(B * KT, P, D)
    mark = np.zeros((P - STK, KPAD), np.float16)
    mark[0, :TXT] = SHIFT
    mark[1, TXT:TXT + IMG] = SHIFT
    return {
        "x": np.asarray(inputs["x"]).reshape(T, D), "ctx": c, "w6": w6, "mark": mark,
        "kb": a["k_b"], "kw": a["norm_k_w"], "vb": a["v_b"], "kib": a["k_img_b"], "kiw": a["norm_k_img_w"],
        "vib": a["v_img_b"], "qb": a["q_b"], "qw": a["norm_q_w"], "ob": a["o_b"],
    }


E, TOPK, CAP, I = 32, 4, 80, 256
GRP, TOPG = 8, 3
NT = T // P
I2 = 512
NI = I2 // P
TROW = D + E
DUMMY = P
BIG = 1000.0
RING = 4
RSCALE = 2.5
N_CONST = 14


def ffn_program(nc, d, x1_dram, table, arow, out):
    with ExitStack() as ctx:
        def sb(name, shape, dt):
            return ctx.enter_context(nc.sbuf_tensor("f_" + name, shape, dt))

        s_apart = ctx.enter_context(nc.semaphore("f_s_apart"))

        def apart(eng):
            eng.sem_inc(s_apart, 1)

        events = []

        def event(name, ahead=0):
            e = Event(ctx, nc, "f_" + name, ahead)
            events.append(e)
            return e

        def dma_sem(name):
            return ctx.enter_context(nc.semaphore("f_" + name))

        x1s = sb("x1s", [P, NT, D], F32)
        x2t = sb("x2t", [P, 2, NC, T], F16)
        swt = sb("swt", [P, 3, 2, NC * D], F16)
        SG, SU, SD = range(3)
        rwt = sb("rwt", [P, 2, NC * E], F16)
        rraw = sb("rraw", [P, NC * E], F32)
        xn = sb("xn", [P, 2, D], F32)
        xs = sb("xs", [P, 2, 2, D], F16)
        stat = sb("stat", [P, 2, 16], F32)
        mhalf = sb("mhalf", [P, 1], F32)
        ident = sb("ident", [P, P], F16)
        identf = sb("identf", [P, P], F32)
        zero = sb("zero", [P, TROW], F32)
        wring = sb("wring", [P, RING, 3 * 2 * D], F32)
        ex = sb("ex", [P, D], F32)
        rc = sb("rc", [P, D], F32)
        hs = sb("hs", [P, 2, NI, D], F16)
        ebias = sb("ebias", [P, E], F32)
        rt = [sb(f"rt{i}", [P, NT, E], F32) for i in range(6)]
        gt = [sb(f"gt{i}", [P, NT, GRP], F32) for i in range(6)]
        gidx = sb("gidx", [P, NT, 8], U32)
        top8 = sb("top8", [P, NT, 8], F32)
        io8 = sb("io8", [P, GRP], F32)
        io32 = sb("io32", [P, E], F32)
        m16 = sb("m16", [P, NT, E], F16)
        c16 = sb("c16", [P, NT, E], F16)
        pv16 = sb("pv16", [P, NT, E], F16)
        wsum = sb("wsum", [P, NT], F32)
        before = sb("before", [P, P], F16)
        ones16 = sb("ones16", [P, P], F16)
        ioS = sb("ioS", [P, CAP, E], F16)
        oneh = sb("oneh", [P, 2, CAP, E], F16)
        tok = sb("tok", [P, NT], F16)
        arow_sb = oneh[0:1, :, :, :].rearrange("p a s e -> p (a s e)").bitcast(F32)
        ia = sb("ia", [CAP, E], F32)
        ib = sb("ib", [CAP, E], F32)
        sio = sb("sio", [P, 1], F32)
        idx = sb("idx", [CAP, E], U32)
        idc = [sb(f"idc{i}", [CAP, 1], U32) for i in range(2)]
        xg = [sb(f"xg{i}", [CAP, TROW], F32) for i in range(2)]
        xgt = [sb(f"xgt{i}", [P, NC, CAP], F32) for i in range(2)]
        wc = [sb(f"wc{i}", [CAP, 1], F32) for i in range(2)]
        eg, hh = ex[0:CAP, 0:I], rc[0:CAP, 0:I]
        ht = [sb(f"ht{i}", [P, 2, CAP], F32) for i in range(2)]
        yf = [sb(f"yf{i}", [CAP, D], F32) for i in range(2)]
        ps = ctx.enter_context(nc.psum_tensor("f_ps", [P, 8, 512], F32))
        wst = [wring[:, i, 0:NC * D] for i in range(2)]

        s_w = [dma_sem(f"s_w{i}") for i in range(2)]
        s_r, s_z, s_tab, s_o, s_a, s_ia, s_wt = (dma_sem(n) for n in ("s_r", "s_z", "s_tab", "s_o", "s_a", "s_ia", "s_wt"))
        s_xl = [dma_sem(f"s_xl{i}") for i in range(4)]
        s_xt = [dma_sem(f"s_xt{i}") for i in range(2)]
        s_ring = [dma_sem(f"s_ring{i}") for i in range(RING)]
        s_g = [dma_sem(f"s_g{i}") for i in range(2)]
        s_sc = dma_sem("s_sc")
        s_i0, s_const = event("s_i0"), event("s_const")
        whi, wlo = event("whi"), event("wlo")
        e_st, e_mv, e_rv, e_rs = event("e_st"), event("e_mv"), event("e_rv"), event("e_rs")
        e_xn, e_hi, e_xs, e_xt, e_x2 = event("e_xn"), event("e_hi"), event("e_xs", 2), event("e_xt", 2), event("e_x2", 2)
        e_r = event("e_r")
        e_ez = event("e_ez")
        link = event("link")
        e_m16, e_pos, e_pv, e_oh, e_a, e_ar, e_wv, e_idx = (event(n) for n in (
            "e_m16", "e_pos", "e_pv", "e_oh", "e_a", "e_ar", "e_wv", "e_idx"))
        e_a2 = event("e_a2")
        f_gu, f_e, f_1, f_r, f_t, f_h, f_hi, f_lo = (event(n, a) for n, a in (
            ("f_gu", 0), ("f_e", 0), ("f_1", 0), ("f_r", 0), ("f_t", 0), ("f_h", 1), ("f_hi", 0), ("f_lo", 2)))
        f_dn, f_ac = event("f_dn"), event("f_ac", 2)
        m_ix, m_xt, m_xc, m_gu, m_e, m_1, m_r, m_t, m_h, m_ht, m_hc, m_y, m_w, m_yf = (event(n, a) for n, a in (
            ("m_ix", 0), ("m_xt", 0), ("m_xc", 1), ("m_gu", 0), ("m_e", 0), ("m_1", 0), ("m_r", 0), ("m_t", 0),
            ("m_h", 2), ("m_ht", 0), ("m_hc", 1), ("m_y", 2), ("m_w", 0), ("m_yf", 2)))

        block = ctx.enter_context(nc.Block())

        def x1_rows(j, k=1):
            return x1_dram[j * P:(j + k) * P, :].rearrange("(k p) n -> p k n", p=P)

        @block.sync
        def _(sp):
            for e in events:
                if e.ahead:
                    sp.sem_inc(e.sem, e.ahead)
            sp.dma_start(rraw[:, :], d["rw"]).then_inc(s_r, 16)
            for k in range(4):
                sp.dma_start(x1s[:, 4 * k:4 * k + 4, :], x1_rows(4 * k, 4)).then_inc(s_xl[k], 16)
            sp.dma_start(ebias[:, :], d["ebias"].partition_broadcast(P)).then_inc(s_r, 16)
            for i in range(3):
                if i >= 2:
                    wlo.wait(sp, i - 1)
                sp.dma_start(wst[i % 2], d["w3"][i]).then_inc(s_w[i % 2], 16)
            s_const.wait(sp, N_CONST)
            sp.dma_start(table[T:T + DUMMY, :], zero[:, :]).then_inc(s_tab, 16)
            sp.dma_start(out[T:T + DUMMY, :], zero[:, 0:D]).then_inc(s_o, 16)
            with sp.Fori(0, NT // 2) as i:
                for u in range(2):
                    e_xn.wait(sp, i * 2 + u + 1)
                    sp.dma_start(table[bass.ds((i * 2 + u) * P, P), 0:D], xn[:, u, :]).then_inc(s_xt[u], 16)
            wlo.wait(sp, 3)
            for e in range(RING):
                sp.dma_start(wring[:, e, :], d["wx"][e]).then_inc(s_ring[e], 16)
            e_wv.wait(sp, 1)
            sp.dma_start(table[0:T, D:TROW].rearrange("(j p) n -> p j n", p=P), rt[5][:, :, :]).then_inc(s_wt, 16)
            e_ar.wait(sp, 1)
            sp.dma_start(arow, arow_sb).then_inc(s_a, 16)
            sp.wait_ge(s_a, 16)
            sp.dma_start(ia[:, :], arow.rearrange("a (s e) -> (a s) e", e=E)).then_inc(s_ia, 16)
            with sp.Fori(0, NT // 4) as bk:
                for q in range(4):
                    j = bk * 4 + q
                    f_ac.wait(sp, j + 1)
                    sp.dma_start(out[bass.ds(j * P, P), :], x1s[:, bass.ds(j, 1), :].rearrange("p a n -> p (a n)")).then_inc(s_o, 16)
            with sp.Fori(0, E // RING - 1) as o:
                for k in range(RING):
                    m_y.wait(sp, o * RING + k + 1)
                    sp.dma_start(wring[:, k, :], d["wx"][bass.ds((o + 1) * RING + k, 1)].rearrange("a p n -> (a p) n")).then_inc(s_ring[k], 16)
            sp.wait_ge(s_o, 16 * (NT + 1))
            sp.wait_ge(s_sc, 16 * E)


        @block.gpsimd
        def _(pool):
            c = s_const.sem
            pool.memset(ident[:, :], 0.0).then_inc(s_i0.sem, 1)
            pool.memset(identf[:, :], 0.0).then_inc(s_i0.sem, 1)
            pool.memset(before[:, :], 1.0).then_inc(s_i0.sem, 1)
            s_i0.wait(pool, 3)
            for t in (ident, identf):
                pool.affine_select(out=t[:, :], in_=t[:, :], pattern=[[-1, P]], compare_op=ALU.not_equal, fill=1.0,
                                   base=0, channel_multiplier=1).then_inc(c, 1)
            pool.affine_select(out=before[:, :], in_=before[:, :], pattern=[[1, P]], compare_op=ALU.is_gt, fill=0.0,
                               base=0, channel_multiplier=-1).then_inc(c, 1)
            pool.memset(mhalf[:, :], -0.5).then_inc(c, 1)
            pool.memset(zero[:, :], 0.0).then_inc(c, 1)
            pool.memset(ones16[:, :], 1.0).then_inc(c, 1)
            pool.iota(io8[:, :], [[1, GRP]], base=0, channel_multiplier=0, allow_small_or_imprecise_dtypes=True).then_inc(c, 1)
            pool.iota(io32[:, :], [[1, E]], base=0, channel_multiplier=0, allow_small_or_imprecise_dtypes=True).then_inc(c, 1)
            pool.iota(ioS[:, :, :], [[1, CAP], [0, E]], base=0, channel_multiplier=0, allow_small_or_imprecise_dtypes=True).then_inc(c, 1)
            pool.iota(tok[:, :], [[P, NT]], base=-T, channel_multiplier=1, allow_small_or_imprecise_dtypes=True).then_inc(c, 1)
            pool.iota(sio[:, :], [[1, 1]], base=0, channel_multiplier=1, allow_small_or_imprecise_dtypes=True).then_inc(c, 1)
            pool.memset(c16[:, 0, :], 0.0).then_inc(c, 1)
            s_const.wait(pool, N_CONST)
            with pool.Fori(0, NT // 2) as i:
                for u in range(2):
                    m = i * 2 + u + 1
                    e_mv.wait(pool, m)
                    apart(pool)
                    pool.tensor_scalar(stat[:, u, 9:10], stat[:, u, 7:8], 1.0, 1e-5, ALU.mult, ALU.add).then_inc(e_rv.sem, 1)
                    e_rv.wait(pool, m)
                    pool.tensor_tensor(stat[:, u, 8:9], stat[:, u, 9:10], mhalf[:, :], ALU.pow).then_inc(e_rs.sem, 1)
            e_idx.wait(pool, 1)
            pool.wait_ge(s_tab, 16)
            pool.wait_ge(s_wt, 16)
            for s in s_xt:
                pool.wait_ge(s, 16 * (NT // 2))

            def gather(n, u, e):
                pool.tensor_copy(idc[u][:, :], idx[:, bass.ds(e, 1)]).then_inc(m_ix.sem, 1)
                m_ix.wait(pool, n)
                apart(pool)
                pool.indirect_dma_start(out=xg[u][:, :], out_offset=None, in_=table[:, :],
                                        in_offset=bass.IndirectOffsetOnAxis(ap=idc[u][:, 0:1], axis=0)).then_inc(s_g[u], 16)

            def scatter(n, u):
                m_yf.wait(pool, n)
                apart(pool)
                pool.indirect_dma_start(out=out[:, :], out_offset=bass.IndirectOffsetOnAxis(ap=idc[u][:, 0:1], axis=0),
                                        in_=yf[u][:, :], in_offset=None, compute_op=ALU.add).then_inc(s_sc, 16)
                pool.wait_ge(s_sc, 16 * n)

            gather(1, 0, 0)
            pool.wait_ge(s_o, 16 * (NT + 1))

            def pair(n, e, last):
                for u in range(2):
                    if not (last and u == 1):
                        m_xc.wait(pool, n + u - 1)
                        m_yf.wait(pool, n + u - 1)
                        gather(n + u + 1, 1 - u, e + u + 1)
                    scatter(n + u, u)

            with pool.Fori(0, E // 2 - 1) as i:
                pair(i * 2 + 1, i * 2, False)
            pair(E - 1, E - 2, True)

        @block.scalar
        def _(act):
            act.wait_ge(s_r, 32)
            act.activation(rwt[:, 0, :], rraw[:, :], ACT.Copy, scale=WS).then_inc(whi.sem, 1)
            for i in range(3):
                act.wait_ge(s_w[i % 2], 16 * (i // 2 + 1))
                act.activation(swt[:, i, 0, :], wst[i % 2], ACT.Copy, scale=WS).then_inc(whi.sem, 1)
            with act.Fori(0, NT // 2) as i:
                for u in range(2):
                    m = act.snap(i * 2 + u + 1)
                    e_xn.wait(act, m)
                    e_xt.wait(act, m - 2)
                    act.copy(xs[:, u, 0, :], xn[:, u, :]).then_inc(e_hi.sem, 1)
            e_r.wait(act, 1)
            act.activation(rt[0].rearrange("p j e -> p (j e)"), ps[:, 2, :], ACT.Exp, scale=-1.0 / WS).then_inc(e_ez.sem, 1)
            e_a.wait(act, 1)
            for k in range(CAP * E // 512):
                cp = act.copy(arow_sb[:, k * 512:(k + 1) * 512], ps[0:1, 3 + k, :])
            cp.then_inc(e_ar.sem, 1)
            with act.Fori(0, NT // 4) as bk:
                for it in range(NI):
                    n = act.snap(bk * NI + it + 1)
                    f_gu.wait(act, n)
                    f_1.wait(act, n - 1)
                    act.activation(ex[:, :], ps[:, it % 2, :], ACT.Exp, scale=-1.0 / WS).then_inc(f_e.sem, 1)
                    f_h.wait(act, n)
                    act.copy(hs[:, 0, it, :], rc[:, :]).then_inc(f_hi.sem, 1)

            def turn(n, u):
                m_gu.wait(act, n)
                m_1.wait(act, n - 1)
                act.activation(eg, ps[0:CAP, 7 if u == 0 else 0, 0:I], ACT.Exp, scale=-1.0).then_inc(m_e.sem, 1)
                m_y.wait(act, n)
                m_w.wait(act, n)
                if not isinstance(n, int):
                    act.wait_ge(s_sc, (n - 2) * 16)
                act.activation(yf[u][:, :], ps[0:CAP, 2 + u, :], ACT.Copy, scale=wc[u][:, 0:1]).then_inc(m_yf.sem, 1)

            for u in range(2):
                turn(u + 1, u)
            with act.Fori(1, E // 2) as i:
                for u in range(2):
                    turn(act.snap(i * 2 + u + 1), u)

        @block.vector
        def _(dve):
            count = [0]

            def chain(ins):
                count[0] += 1
                ins.then_inc(link.sem, 1)
                link.wait(dve, count[0])

            dve.memset(stat[:, :, :], 0.0).then_inc(s_const.sem, 1)
            dve.memset(ia[:, :], 0.0).then_inc(s_const.sem, 1)
            s_const.wait(dve, N_CONST)
            whi.wait(dve, 1)
            chain(dve.scalar_tensor_tensor(rwt[:, 1, :], rraw[:, :], WS, rwt[:, 0, :], ALU.mult, ALU.subtract))
            for i in range(3):
                whi.wait(dve, i + 2)
                dve.scalar_tensor_tensor(swt[:, i, 1, :], wst[i % 2], WS, swt[:, i, 0, :], ALU.mult,
                                         ALU.subtract).then_inc(wlo.sem, 1)

            for k in range(4):
                dve.wait_ge(s_xl[k], 16)

            def norm(m, u, j):
                xj = x1s[:, bass.ds(j, 1), :].rearrange("p a n -> p (a n)")
                e_xs.wait(dve, m - 2)
                dve.bn_stats(stat[:, u, 0:6], xj).then_inc(e_st.sem, 1)
                e_st.wait(dve, m)
                apart(dve)
                dve.bn_aggr(stat[:, u, 6:8], stat[:, u, 0:6]).then_inc(e_mv.sem, 1)

            def apply(m, u, j, stored):
                xj = x1s[:, bass.ds(j, 1), :].rearrange("p a n -> p (a n)")
                e_rs.wait(dve, m)
                if stored is not None:
                    dve.wait_ge(s_xt[u], stored)
                dve.tensor_scalar(xn[:, u, :], xj, stat[:, u, 6:7], stat[:, u, 8:9], ALU.subtract, ALU.mult).then_inc(e_xn.sem, 1)
                e_hi.wait(dve, m)
                dve.tensor_tensor(xs[:, u, 1, :], xn[:, u, :], xs[:, u, 0, :], ALU.subtract).then_inc(e_xs.sem, 1)

            def store(m, u, j):
                e_xt.wait(dve, m)
                dve.tensor_copy(x2t[:, :, :, bass.ds(j * P, P)].rearrange("p a c n -> p (a c) n"),
                                ps[:, u, :].bitcast(F16).rearrange("p (k n) -> p k n", n=P)).then_inc(e_x2.sem, 1)

            for u in range(2):
                norm(u + 1, u, u)
                apply(u + 1, u, u, None)
                store(u + 1, u, u)
            with dve.Fori(1, NT // 2) as i:
                for u in range(2):
                    m = dve.snap(i * 2 + u + 1)
                    norm(m, u, i * 2 + u)
                    apply(m, u, i * 2 + u, i * 16)
                    store(m, u, i * 2 + u)

            TT = dve.tensor_tensor
            fl = lambda t: t.rearrange("p j e -> p (j e)")
            scores, sc, masked, mask, tmp, wv = rt
            e_ez.wait(dve, 1)
            chain(dve.tensor_scalar(fl(tmp), fl(scores), 1.0, None, ALU.add))
            chain(dve.reciprocal(fl(scores), fl(tmp)))
            chain(TT(sc[:, :, :], scores[:, :, :], ebias[:, :].unsqueeze(1).to_broadcast([P, NT, E]), ALU.add))
            q4 = sc[:, :, :].rearrange("p j (g k) -> p (j g) k", k=4)
            G = [t[:, :, :].rearrange("p j g -> p (j g)") for t in gt]
            chain(TT(G[0], q4[:, :, 0], q4[:, :, 1], ALU.max))
            chain(TT(G[1], q4[:, :, 0], q4[:, :, 1], ALU.min))
            chain(TT(G[2], q4[:, :, 2], q4[:, :, 3], ALU.max))
            chain(TT(G[3], q4[:, :, 2], q4[:, :, 3], ALU.min))
            chain(TT(G[4], G[0], G[2], ALU.max))
            chain(TT(G[5], G[0], G[2], ALU.min))
            chain(TT(G[0], G[1], G[3], ALU.max))
            chain(TT(G[1], G[5], G[0], ALU.max))
            chain(TT(G[2], G[4], G[1], ALU.add))

            def top(values):
                for j in range(NT):
                    ins = dve.max(top8[:, j, :], values[:, j, :])
                chain(ins)
                for j in range(NT):
                    ins = dve.max_index(gidx[:, j, :], top8[:, j, :], values[:, j, :])
                chain(ins)
                chain(dve.tensor_copy(gt[5][:, :, :], gidx[:, :, :]))

            def chosen(outm, t, k, iota, n):
                for r in range(k):
                    dst = outm if r == 0 else t
                    chain(TT(dst[:, :, :], gt[5][:, :, r:r + 1].to_broadcast([P, NT, n]),
                             iota[:, :].unsqueeze(1).to_broadcast([P, NT, n]), ALU.is_equal))
                    if r:
                        chain(TT(outm[:, :, :], outm[:, :, :], t[:, :, :], ALU.add))

            top(gt[2])
            chosen(gt[0], gt[1], TOPG, io8, GRP)
            chain(TT(masked[:, :, :].rearrange("p j (g k) -> p (j g) k", k=4), q4,
                     G[0].unsqueeze(2).to_broadcast([P, NT * GRP, 4]), ALU.mult))
            chain(dve.tensor_scalar(fl(masked), fl(masked), 0.0, None, ALU.add))
            top(masked)
            chosen(mask, tmp, TOPK, io32, E)
            chain(TT(fl(tmp), fl(scores), fl(mask), ALU.mult))
            chain(dve.tensor_reduce(wsum[:, :], tmp[:, :, :], mybir.AxisListType.X, ALU.add))
            chain(dve.tensor_scalar(wsum[:, :], wsum[:, :], 1e-20, None, ALU.add))
            chain(dve.reciprocal(wsum[:, :], wsum[:, :]))
            chain(dve.scalar_tensor_tensor(wv[:, :, :], tmp[:, :, :], RSCALE, wsum[:, :].unsqueeze(2).to_broadcast([P, NT, E]),
                                           ALU.mult, ALU.mult))
            chain(dve.tensor_copy(fl(m16), fl(mask)))
            for j in range(1, NT):
                chain(TT(c16[:, j, :], c16[:, j - 1, :], m16[:, j - 1, :], ALU.add))
            dve.sem_inc(e_m16.sem, 1)
            e_pos.wait(dve, 1)
            chain(dve.scalar_tensor_tensor(fl(tmp), ps[:, 3, :], float(CAP), fl(mask), ALU.is_lt, ALU.mult))
            chain(TT(fl(wv), fl(wv), fl(tmp), ALU.mult))
            dve.sem_inc(e_wv.sem, 1)
            chain(dve.scalar_tensor_tensor(fl(masked), ps[:, 3, :], -BIG, fl(tmp), ALU.add, ALU.mult))
            chain(dve.tensor_scalar(fl(pv16), fl(masked), BIG, None, ALU.add))
            for j in range(NT):
                if j >= 2:
                    e_a2.wait(dve, j - 1)
                TT(oneh[:, j % 2, :, :], ioS[:, :, :], pv16[:, j, :].unsqueeze(1).to_broadcast([P, CAP, E]),
                   ALU.is_equal).then_inc(e_oh.sem, 1)
            dve.wait_ge(s_ia, 16)
            chain(dve.tensor_scalar(ib[:, :], ia[:, :], 0.0, None, ALU.is_equal))
            chain(dve.tensor_scalar(ib[:, :], ib[:, :], sio[0:CAP, 0:1], None, ALU.mult))
            chain(dve.scalar_tensor_tensor(ib[:, :], ia[:, :], float(T), ib[:, :], ALU.add, ALU.add))
            dve.tensor_copy(idx[:, :], ib[:, :]).then_inc(e_idx.sem, 1)

            with dve.Fori(0, NT // 4) as bk:
                for it in range(NI):
                    n = dve.snap(bk * NI + it + 1)
                    f_e.wait(dve, n)
                    f_lo.wait(dve, n - 1)
                    dve.tensor_scalar(rc[:, :], ex[:, :], 1.0, None, ALU.add).then_inc(f_1.sem, 1)
                    f_1.wait(dve, n)
                    dve.reciprocal(rc[:, :], rc[:, :]).then_inc(f_r.sem, 1)
                    f_r.wait(dve, n)
                    dve.scalar_tensor_tensor(rc[:, :], ps[:, it % 2, :], 1.0 / WS / WS, rc[:, :], ALU.mult,
                                             ALU.mult).then_inc(f_t.sem, 1)
                    f_t.wait(dve, n)
                    TT(rc[:, :], rc[:, :], ps[:, 2 + it % 2, :], ALU.mult).then_inc(f_h.sem, 1)
                    f_hi.wait(dve, n)
                    TT(hs[:, 1, it, :], rc[:, :], hs[:, 0, it, :], ALU.subtract).then_inc(f_lo.sem, 1)
                for q in range(4):
                    n = bk * 4 + q + 1
                    f_dn.wait(dve, n)
                    xq = x1s[:, bass.ds(bk * 4 + q, 1), :].rearrange("p a n -> p (a n)")
                    dve.scalar_tensor_tensor(xq, ps[:, 4 + q % 2, :], 1.0 / WS, xq, ALU.mult, ALU.add).then_inc(f_ac.sem, 1)

            def take(n, u, e, count):
                m_xt.wait(dve, n)
                dve.tensor_copy(xgt[u][:, :, :].rearrange("p c s -> p (c s)"), ps[:, 6, 0:NC * CAP]).then_inc(m_xc.sem, 1)
                dve.wait_ge(s_g[u], count)
                m_yf.wait(dve, n - 2)
                dve.tensor_copy(wc[u][:, :], xg[u][:, bass.ds(e + D, 1)]).then_inc(m_w.sem, 1)

            def hidden(n, u):
                gu = ps[0:CAP, 7 if u == 0 else 0, :]
                m_e.wait(dve, n)
                dve.tensor_scalar(hh, eg, 1.0, None, ALU.add).then_inc(m_1.sem, 1)
                m_1.wait(dve, n)
                dve.reciprocal(hh, hh).then_inc(m_r.sem, 1)
                m_r.wait(dve, n)
                TT(hh, hh, gu[:, 0:I], ALU.mult).then_inc(m_t.sem, 1)
                m_t.wait(dve, n)
                TT(hh, hh, gu[:, I:2 * I], ALU.mult).then_inc(m_h.sem, 1)
                m_ht.wait(dve, n)
                dve.tensor_copy(ht[u][:, :, :].rearrange("p c s -> p (c s)"), ps[:, 1, 0:2 * CAP]).then_inc(m_hc.sem, 1)

            def step(n, u, e, look, cnt):
                if look:
                    take(n + 1, 1 - u, e + 1, cnt)
                hidden(n, u)

            take(1, 0, 0, 16)
            with dve.Fori(0, E // 2 - 1) as i:
                step(i * 2 + 1, 0, i * 2, True, i * 16 + 16)
                step(i * 2 + 2, 1, i * 2 + 1, True, i * 16 + 32)
            step(E - 1, 0, E - 2, True, 8 * E)
            step(E, 1, E - 1, False, 0)

        @block.tensor
        def _(pe):
            s_const.wait(pe, N_CONST)
            PARTS = ((0, 0), (0, 1), (1, 0))

            def product(out_, lhs, rhs, chunks):
                steps = [(c, a, z) for c in range(chunks) for a, z in PARTS]
                for k, (c, a, z) in enumerate(steps):
                    mm = pe.matmul(out_, lhs(a, c), rhs(z, c), start=(k == 0), stop=(k == len(steps) - 1))
                return mm

            link.wait(pe, 1)
            with pe.Fori(0, NT // 2) as i:
                for u in range(2):
                    m = pe.snap(i * 2 + u + 1)
                    e_xs.wait(pe, m)
                    e_x2.wait(pe, m - 2)
                    xt = ps[:, u, :].bitcast(F16)
                    for a in range(2):
                        for c in range(NC):
                            tr = pe.transpose(xt[:, (a * NC + c) * P:(a * NC + c + 1) * P],
                                              xs[:, u, a, c * P:(c + 1) * P], ident[:, :])
                    tr.then_inc(e_xt.sem, 1)
            with pe.Fori(0, NT) as j:
                e_x2.wait(pe, j + 1)
                product(ps[:, 2, bass.ds(j * E, E)], lambda a, c: x2t[:, a, c, bass.ds(j * P, P)],
                        lambda z, c: rwt[:, z, c * E:(c + 1) * E], NC)
            pe.drain().then_inc(e_r.sem, 1)
            e_m16.wait(pe, 1)
            pe.matmul(ps[:, 3, :], before[:, :], m16[:, :, :].rearrange("p j e -> p (j e)"), start=True, stop=False)
            pe.matmul(ps[:, 3, :], ones16[:, :], c16[:, :, :].rearrange("p j e -> p (j e)"), start=False,
                      stop=True).then_inc(e_pos.sem, 1)
            NA = CAP * E // 512
            for j in range(NT):
                e_oh.wait(pe, j + 1)
                flat = oneh[:, j % 2, :, :].rearrange("p s e -> p (s e)")
                for k in range(NA):
                    mm = pe.matmul(ps[0:1, 3 + k, :], tok[:, j:j + 1], flat[:, k * 512:(k + 1) * 512],
                                   start=(j == 0), stop=(j == NT - 1))
                mm.then_inc(e_a2.sem, 1)
                if j == NT - 1:
                    e_a2.wait(pe, NT)
                    pe.sem_inc(e_a.sem, 1)
            wlo.wait(pe, 3)
            with pe.Fori(0, NT // 4) as bk:
                for it in range(NI):
                    n = pe.snap(bk * NI + it + 1)
                    f_lo.wait(pe, n - 2)
                    if it == 0:
                        e_ar.wait(pe, 1)
                    for w, bank in ((SG, it % 2), (SU, 2 + it % 2)):
                        mm = product(ps[:, bank, :], lambda a, c: swt[:, w, a, c * D + it * P:c * D + (it + 1) * P],
                                     lambda z, c: x2t[:, z, c, bass.ds(bk * 512, 512)], NC)
                    mm.then_inc(f_gu.sem, 1)
                f_lo.wait(pe, bk * NI + NI)
                for q in range(4):
                    n = bk * 4 + q + 1
                    f_ac.wait(pe, n - 2)
                    product(ps[:, 4 + q % 2, :], lambda a, c: hs[:, a, c, q * P:(q + 1) * P],
                            lambda z, c: swt[:, SD, z, c * D:(c + 1) * D], NI).then_inc(f_dn.sem, 1)

            def turn_rows(n, u, cnt):
                pe.wait_ge(s_g[u], cnt)
                m_xc.wait(pe, n - 1)
                for c in range(NC):
                    tr = pe.transpose(ps[:, 6, c * CAP:(c + 1) * CAP], xg[u][:, c * P:(c + 1) * P], identf[0:CAP, 0:CAP])
                tr.then_inc(m_xt.sem, 1)

            def gate_up(n, u, slot, cnt):
                pe.wait_ge(s_ring[slot], cnt)
                m_xc.wait(pe, n)
                m_h.wait(pe, n - 2)
                for c in range(NC):
                    mm = pe.matmul(ps[0:CAP, 7 if u == 0 else 0, :], xgt[u][:, c, :], wring[:, slot, c * 512:(c + 1) * 512],
                                   start=(c == 0), stop=(c == NC - 1))
                mm.then_inc(m_gu.sem, 1)

            def down(n, u, slot):
                m_h.wait(pe, n)
                m_hc.wait(pe, n - 1)
                for c in range(2):
                    tr = pe.transpose(ps[:, 1, c * CAP:(c + 1) * CAP], hh[:, c * P:(c + 1) * P], identf[0:CAP, 0:CAP])
                tr.then_inc(m_ht.sem, 1)
                m_hc.wait(pe, n)
                m_yf.wait(pe, n - 2)
                for c in range(2):
                    mm = pe.matmul(ps[0:CAP, 2 + u, :], ht[u][:, c, :], wring[:, slot, 2048 + c * D:2048 + (c + 1) * D],
                                   start=(c == 0), stop=(c == 1))
                mm.then_inc(m_y.sem, 1)

            f_ac.wait(pe, NT)
            turn_rows(1, 0, 16)
            gate_up(1, 0, 0, 16)

            def four(o, last):
                for k in range(RING):
                    n, u = o * RING + k + 1, k % 2
                    if not (last and k == RING - 1):
                        turn_rows(n + 1, 1 - u, o * 32 + 16 * ((k + 1) // 2 + 1))
                        gate_up(n + 1, 1 - u, (k + 1) % RING, o * 16 + 16 + (16 if k == RING - 1 else 0))
                    down(n, u, k)

            with pe.Fori(0, E // RING - 1) as o:
                four(o, False)
            four(E // RING - 1, True)


def lay_ffn(inputs):
    f = {k[len("L0_ffn_"):]: np.asarray(v) for k, v in inputs.items() if k.startswith("L0_ffn_")}

    def chunks(w):
        k, n = w.shape
        return w.reshape(k // P, P, n).transpose(1, 0, 2).reshape(P, -1)
    w3 = np.stack([chunks(f["shared_gate"].T), chunks(f["shared_up"].T), chunks(f["shared_down"].T)])
    gu = np.concatenate([f["W_gate"], f["W_up"]], axis=2).reshape(E, NC, P, 2 * I).transpose(0, 2, 1, 3).reshape(E, P, -1)
    dn = f["W_down"].reshape(E, 2, P, D).transpose(0, 2, 1, 3).reshape(E, P, -1)
    return {"rw": chunks(f["router_w"].T), "ebias": f["e_bias"], "w3": w3, "wx": np.concatenate([gu, dn], axis=2)}


def build(nc, d, out):
    x1_dram = nc.dram_tensor("x1", (T, D), F32).ap()
    table = nc.dram_tensor("table", (T + DUMMY, TROW), F32).ap()
    arow = nc.dram_tensor("arow", (1, CAP * E), F32).ap()
    attention_program(nc, d, x1_dram)
    ffn_program(nc, d, x1_dram, table, arow, out)


def kernel(**inputs):
    import concourse.bacc as bacc
    from concourse.bass_utils import run_bass_kernel_spmd

    arrays = {**lay_attention(inputs), **lay_ffn(inputs)}
    arrays = {f"in_{n}": np.ascontiguousarray(a) for n, a in arrays.items()}
    nc = bacc.Bacc("TRN2", target_bir_lowering=False, num_devices=1)
    d = {n[3:]: nc.dram_tensor(n, a.shape, mybir.dt.from_np(a.dtype), kind="ExternalInput").ap()
         for n, a in arrays.items()}
    out = nc.dram_tensor("out", (T + DUMMY, D), F32, kind="ExternalOutput").ap()
    build(nc, d, out)
    result = run_bass_kernel_spmd(nc, [arrays], core_ids=[0]).results[0]["out"]
    return result[:T].reshape(B, L, D)
```

```python
from contextlib import ExitStack

import numpy as np

import concourse.bass as bass
from concourse import mybir

ALU = mybir.AluOpType
ACT = mybir.ActivationFunctionType
F32 = mybir.dt.float32
F16 = mybir.dt.float16
U32 = mybir.dt.uint32

P = 128
B, L, D = 4, 512, 512
T = B * L
NC = D // P
HEADS, HD = 16, 32
NG = HEADS // 4
TXT, IMG = 1344, 257
KT = 13
KPAD = KT * P
MIX = TXT // P
SPLIT = TXT - MIX * P
LAST = TXT + IMG - (KT - 1) * P
QT = L // P
POS = KT + QT
WS = 256.0
STK = 3 * HD
SHIFT = 16.0
SCALE = 1.0 / float(np.sqrt(HD))
ORDER = [KT - 2, KT - 1, MIX] + list(range(MIX))
ADDED = range(3, KT - 1)
NA = len(ADDED)
SAFE = 1e20
ODD = 1e30


class Event:

    def __init__(self, ctx, nc, name, ahead=0):
        self.sem = ctx.enter_context(nc.semaphore(name))
        self.ahead = ahead

    def wait(self, eng, n):
        if not (isinstance(n, int) and n + self.ahead <= 0):
            eng.wait_ge(self.sem, n + self.ahead)


def attention_program(nc, d, x1_dram):
    with ExitStack() as ctx:
        def sb(name, shape, dt):
            return ctx.enter_context(nc.sbuf_tensor(name, shape, dt))

        def event(name, ahead=0):
            e = Event(ctx, nc, name, ahead)
            events.append(e)
            return e

        s_apart = ctx.enter_context(nc.semaphore("s_apart"))

        def apart(eng):
            eng.sem_inc(s_apart, 1)

        events = []
        wts = sb("wts", [P, 6, 2, NC * D], F16)
        WQ, WK, WV, WKI, WVI, WO = range(6)
        vec = sb("vec", [P, 9, D], F32)
        KB, KW, VB = 0, 2, 4
        QB, QW, OB = 6, 7, 8
        keys = sb("keys", [P, HEADS, KPAD], F16)
        vals = sb("vals", [P, KT, D], F32)
        quer = sb("quer", [P, HEADS, L], F16)
        vgrp = sb("vgrp", [P, KT, P], F32)
        attn = sb("attn", [P, NG, 2, L], F16)
        work = sb("work", [P, 16 * D], F32)
        ident = sb("ident", [P, P], F16)
        ones = sb("ones", [P, HD], F32)
        small = sb("small", [P, 24], F32)
        flag = sb("flag", [1, 1], mybir.dt.int32)
        ps = ctx.enter_context(nc.psum_tensor("ps", [P, 8, 512], F32))

        raw = [work[:, i * D:(i + 1) * D] for i in range(2)]
        hl = [work[:, (2 + i) * D:(3 + i) * D].bitcast(F16).rearrange("p (s n) -> p s n", s=2) for i in range(2)]
        kraw = work[:, 4 * D:5 * D]
        knorm = work[:, 5 * D:6 * D]
        xnorm = work[:, 6 * D:7 * D]
        xs = work[:, 7 * D:8 * D].bitcast(F16).rearrange("p (s n) -> p s n", s=2)
        stw = HEADS * STK // 2
        stack = [work[:, 8 * D + i * stw:8 * D + (i + 1) * stw].bitcast(F16).rearrange("p (h r) -> p h r", h=HEADS)
                 for i in range(2)]
        prob = work[:, 0:8 * D].rearrange("p (s h q) -> p s h q", s=2, h=4)
        rden_t, rden_i = work[:, 8 * D:9 * D], work[:, 9 * D:10 * D]
        added = work[:, 10 * D:14 * D].rearrange("p (h q) -> p h q", h=4)
        odds = work[:, 14 * D:15 * D]
        attn32 = attn[:, :, :, :].rearrange("p g s q -> p (g s q)").bitcast(F32).rearrange("p (g q) -> p g q", g=NG)
        mx = work[:, 0:P].rearrange("p (h t s) -> p h t s", h=HEADS, t=QT)
        mh = work[:, D:D + (STK + P) // 2].bitcast(F16)
        xres = [work[:, j * D:(j + 1) * D] for j in range(QT)]
        proj = work[:, 15 * D:16 * D]
        wstage = [work[:, i * 4 * D:(i + 1) * 4 * D] for i in range(2)]
        ssq, rin, rtmp, st6, mv, rs, rs2 = (small[:, 0:1], small[:, 1:2], small[:, 2:3], small[:, 4:10],
                                            small[:, 10:12], small[:, 12:13], small[:, 13:14])
        mhalf = small[:, 14:15]
        total = small[:, 15:16]

        turned = ps[:, 4:6, :].rearrange("p a n -> p (a n)").bitcast(F16).rearrange("p (h k) -> p h k", h=HEADS)
        xturned = ps[:, 6, :].bitcast(F16)
        NUM_T, DEN_T, NUM_I, DEN_I = 4, 5, 6, 7

        s_w = [ctx.enter_context(nc.semaphore(f"s_w{i}")) for i in range(2)]
        s_c = ctx.enter_context(nc.semaphore("s_c"))
        s_in = [ctx.enter_context(nc.semaphore(f"s_in{i}")) for i in range(2)]
        s_x = [ctx.enter_context(nc.semaphore(f"s_x{i}")) for i in range(QT)]
        s_st = ctx.enter_context(nc.semaphore("s_st"))
        s_i0 = event("s_i0")
        s_const = event("s_const")
        whi, wlo = event("whi"), event("wlo")
        e_hi = event("e_hi")
        e_hl = event("e_hl")
        e_pv = event("e_pv", 2)
        e_pk = event("e_pk", 2)
        e_kr = event("e_kr")
        e_ssq = event("e_ssq")
        e_rt = event("e_rt")
        e_rin = event("e_rin")
        e_kn = event("e_kn")
        e_c0 = event("e_c0")
        e_c1 = event("e_c1", 1)
        e_lo = event("e_lo")
        e_t = event("e_t", 2)
        e_td = event("e_td", 1)
        e_ta = event("e_ta", 1)
        e_v = event("e_v", 2)
        e_st = event("e_st")
        e_mv = event("e_mv")
        e_rv = event("e_rv")
        e_rs = event("e_rs")
        e_xn = event("e_xn")
        e_xs = event("e_xs")
        e_xt = event("e_xt")
        e_ms = event("e_ms")
        e_mt, e_mi = event("e_mt"), event("e_mi", 2)
        e_mh = event("e_mh")
        e_mr = event("e_mr")
        e_mc = event("e_mc")
        e_qz = event("e_qz")
        e_vg = event("e_vg", 1)
        e_s = event("e_s")
        e_e = event("e_e", 2)
        e_ad = event("e_ad", 1)
        e_av = event("e_av", KT)
        e_ri = event("e_ri")
        e_oi = event("e_oi", 1)
        e_rt2 = event("e_rt2")
        e_ot = event("e_ot", 1)
        e_os = event("e_os")
        e_oh = event("e_oh")
        e_at = event("e_at", 1)
        e_ck = event("e_ck", 4)
        e_fz = event("e_fz")
        e_fm = event("e_fm")
        e_fs = event("e_fs")
        e_fl = event("e_fl")
        e_po = event("e_po")
        e_ob = event("e_ob")
        e_x1 = event("e_x1", 2)
        e_b = event("e_b", 1)

        block = ctx.enter_context(nc.Block())

        def kind(pos):
            return 0 if pos < MIX else 1 if pos == MIX else 2

        def is_q(pos):
            return pos >= KT

        def parts(n):
            t = ORDER[n]
            rows = {KT - 1: [(0, LAST, 1)], MIX: [(SPLIT, P, 1), (0, SPLIT, 0)]}.get(t, [(0, P, 1 if t > MIX else 0)])
            return [(a, z, img, n == 0 if img else t == MIX, t == MIX if img else n == KT - 1) for a, z, img in rows]

        def again(eng, b):
            e_fl.wait(eng, b + 1)
            apart(eng)
            return eng.If(eng.value_load(flag[0:1, 0:1], min_val=0, max_val=1) > 0)

        def otherwise(eng, counts):
            with eng.Else():
                for e, n in counts:
                    eng.sem_inc(e.sem, n)
            eng.end_ifs()

        def slots(b, pos):
            return (b * ((POS + 1) // 2) if pos % 2 == 0 else b * (POS // 2)) + pos // 2 + 1

        PAIRS = 4

        @block.sync
        def _(sp):
            for e in events:
                if e.ahead:
                    sp.sem_inc(e.sem, e.ahead)
            for i in range(6):
                if i >= 2:
                    wlo.wait(sp, i - 1)
                sp.dma_start(wstage[i % 2], d["w6"][i]).then_inc(s_w[i % 2], 16)
            srcs = [(k, d[n]) for k, n in ((KB, "kb"), (KW, "kw"), (VB, "vb"))]
            irng = {KB: "kib", KW: "kiw", VB: "vib"}
            for k, txt in srcs:
                sp.dma_start(vec[:, k, :], txt.partition_broadcast(P)).then_inc(s_c, 16)
                sp.dma_start(vec[:, k + 1, :], d[irng[k]].partition_broadcast(P)).then_inc(s_c, 16)
            for k, n in ((QB, "qb"), (QW, "qw"), (OB, "ob")):
                sp.dma_start(vec[:, k, :], d[n].partition_broadcast(P)).then_inc(s_c, 16)
            for h in range(HEADS):
                sp.dma_start(keys[STK:P, h, :], d["mark"]).then_inc(s_c, 16)
            wlo.wait(sp, 6)

            with sp.Fori(0, B) as b:
                e_b.wait(sp, b)

                def load(b, pos, q_tile=None, key_tile=None):
                    if q_tile is not None:
                        src = d["x"][bass.ds(b * L + q_tile * P, P), :]
                    else:
                        src = d["ctx"][bass.ds(b * KT + key_tile, 1)].rearrange("a p n -> (a p) n")
                    sp.dma_start(raw[pos % 2], src).then_inc(s_in[pos % 2], 16)

                load(b, 0, key_tile=0)
                load(b, 1, key_tile=1)
                with sp.Fori(0, PAIRS) as i:
                    for u in range(2):
                        e_hl.wait(sp, b * POS + i * 2 + u + 1)
                        load(b, u, key_tile=i * 2 + u + 2)
                for pos in range(2 * PAIRS, POS - 2):
                    if is_q(pos):
                        e_xn.wait(sp, b * QT + pos - KT + 1)
                    else:
                        e_hl.wait(sp, b * POS + pos + 1)
                    nxt = pos + 2
                    load(b, nxt, **({"q_tile": nxt - KT} if is_q(nxt) else {"key_tile": nxt}))
                e_at.wait(sp, (2 * b + 2) * NG)
                for j in range(QT):
                    sp.dma_start(xres[j], d["x"][bass.ds(b * L + j * P, P), :]).then_inc(s_x[j], 16)
                for j in range(QT):
                    e_x1.wait(sp, b * QT + j + 1)
                    sp.dma_start(x1_dram[bass.ds(b * L + j * P, P), :], xres[j]).then_inc(s_st, 16)
                sp.wait_ge(s_st, (b + 1) * 16 * QT)
                sp.sem_inc(e_b.sem, 1)

        @block.gpsimd
        def _(pool):
            pool.memset(ident[:, :], 0.0).then_inc(s_i0.sem, 1)
            s_i0.wait(pool, 1)
            pool.affine_select(out=ident[:, :], in_=ident[:, :], pattern=[[-1, P]], compare_op=ALU.not_equal, fill=1.0,
                               base=0, channel_multiplier=1).then_inc(s_const.sem, 1)
            pool.memset(mhalf, -0.5).then_inc(s_const.sem, 1)
            s_const.wait(pool, 4)

            def rinv(n):
                e_ssq.wait(pool, n)
                apart(pool)
                pool.tensor_scalar(rtmp, ssq, 1.0 / D, 1e-6, ALU.mult, ALU.add).then_inc(e_rt.sem, 1)
                e_rt.wait(pool, n)
                pool.tensor_tensor(rin, rtmp, mhalf, ALU.pow).then_inc(e_rin.sem, 1)

            def rstd(m):
                e_mv.wait(pool, m)
                apart(pool)
                pool.tensor_scalar(rs2, mv[:, 1:2], 1.0, 1e-5, ALU.mult, ALU.add).then_inc(e_rv.sem, 1)
                e_rv.wait(pool, m)
                pool.tensor_tensor(rs, rs2, mhalf, ALU.pow).then_inc(e_rs.sem, 1)

            with pool.Fori(0, B) as b:
                with pool.Fori(0, 2 * PAIRS) as i:
                    rinv(b * POS + i + 1)
                for pos in range(2 * PAIRS, POS):
                    if pos + 1 < POS and is_q(pos + 1):
                        rstd(b * QT + pos + 1 - KT + 1)
                    rinv(b * POS + pos + 1)
                pool.memset(odds, 0.0).then_inc(e_fz.sem, 1)
                e_fz.wait(pool, b + 1)
                e_v.wait(pool, b * KT + KT)
                apart(pool)

                def values(p, g):
                    for n, t in enumerate(ORDER):
                        e_av.wait(pool, ((2 * b + p) * NG + g) * KT + n + 1 - KT)
                        if isinstance(g, int):
                            apart(pool)
                        pool.tensor_copy(vgrp[:, t, :], vals[:, t, bass.ds(g * P, P)]).then_inc(e_vg.sem, 1)

                def bounds(g, text):
                    k = (b * NG + g) * 6 + 3 * text
                    rden, read = (rden_t, e_ot) if text else (rden_i, e_oi)
                    read.wait(pool, 2 * b * NG + g + 1)
                    apart(pool)
                    pool.tensor_tensor(odds, odds, rden, ALU.add).then_inc(e_ck.sem, 1)
                    e_ck.wait(pool, k + 1)
                    apart(pool)
                    pool.tensor_scalar(rden, rden, 1.0 / SAFE, ODD, ALU.is_lt, ALU.mult).then_inc(e_ck.sem, 1)
                    e_ck.wait(pool, k + 2)
                    apart(pool)
                    pool.tensor_tensor(odds, odds, rden, ALU.add).then_inc(e_ck.sem, 1)
                    e_ck.wait(pool, k + 3)

                values(0, 0)
                with pool.Fori(1, NG) as g:
                    values(0, g)
                    bounds(g - 1, 0)
                    bounds(g - 1, 1)
                bounds(NG - 1, 0)
                bounds(NG - 1, 1)
                with again(pool, b):
                    with pool.Fori(0, NG) as g:
                        values(1, g)
                otherwise(pool, ((e_vg, NG * KT),))

        @block.scalar
        def _(act):
            for i in range(6):
                act.wait_ge(s_w[i % 2], 16 * (i // 2 + 1))
                act.activation(wts[:, i, 0, :], wstage[i % 2], ACT.Copy, scale=WS).then_inc(whi.sem, 1)

            def high(n, pos, b):
                if is_q(pos):
                    e_xn.wait(act, b * QT + pos - KT + 1)
                    act.copy(xs[:, 0, :], xnorm).then_inc(e_hi.sem, 1)
                else:
                    act.wait_ge(s_in[pos % 2], 16 * slots_of(pos, n, b))
                    e_pk.wait(act, n - 2)
                    act.copy(hl[pos % 2][:, 0, :], raw[pos % 2]).then_inc(e_hi.sem, 1)

            def store_turned(n, tile, q):
                e_t.wait(act, n)
                dst = quer if q else keys
                act.copy(dst[0:STK, 0:8, bass.ds(tile * P, P)], turned[0:STK, 0:8, :]).then_inc(e_ta.sem, 1)

            def turn(n, pos, b, tile, prev):
                if pos + 1 < POS:
                    high(n + 1, pos + 1, b)
                e_kr.wait(act, n)
                act.activation(ps[:, 7, :], kraw, ACT.Square, accum_out=ssq).then_inc(e_ssq.sem, 1)
                if prev is not None:
                    store_turned(n - 1, *prev)
                e_kn.wait(act, n)
                e_t.wait(act, n - 2)
                st = stack[pos % 2]
                kn = knorm.rearrange("p (h d) -> p h d", h=HEADS)
                second = 2 if is_q(pos) else 1
                act.copy(st[:, :, 0:HD], kn).then_inc(e_c0.sem, 1)
                act.copy(st[:, :, second * HD:(second + 1) * HD], kn).then_inc(e_c1.sem, 1)

            def slots_of(pos, n, b):
                return slots(b, pos) if not isinstance(pos, tuple) else None

            with act.Fori(0, B) as b:
                act.wait_ge(s_in[0], 16 * slots(b, 0))
                e_pk.wait(act, b * POS - 1)
                act.copy(hl[0][:, 0, :], raw[0]).then_inc(e_hi.sem, 1)
                turn(b * POS + 1, 0, b, 0, None)
                with act.Fori(0, PAIRS) as i:
                    for u in range(2):
                        n = act.snap(b * POS + i * 2 + u + 2)
                        s = (u + 2) % 2
                        act.wait_ge(s_in[s], 16 * (slots(b, s) + i + (1 if u == 0 else 1)))
                        e_pk.wait(act, n - 1)
                        act.copy(hl[s][:, 0, :], raw[s]).then_inc(e_hi.sem, 1)
                        e_kr.wait(act, n)
                        act.activation(ps[:, 7, :], kraw, ACT.Square, accum_out=ssq).then_inc(e_ssq.sem, 1)
                        store_turned(n - 1, i * 2 + u, False)
                        e_kn.wait(act, n)
                        e_t.wait(act, n - 2)
                        kn = knorm.rearrange("p (h d) -> p h d", h=HEADS)
                        act.copy(stack[1 - u][:, :, 0:HD], kn).then_inc(e_c0.sem, 1)
                        act.copy(stack[1 - u][:, :, HD:2 * HD], kn).then_inc(e_c1.sem, 1)
                for pos in range(2 * PAIRS + 1, POS):
                    q = pos - 1 >= KT
                    turn(b * POS + pos + 1, pos, b, None, (pos - 1 - KT if q else pos - 1, q))
                store_turned(b * POS + POS, QT - 1, True)

                def exponentials(p):
                    with act.Fori(0, NG) as g:
                        gg = act.snap((2 * b + p) * NG + g)
                        for n, t in enumerate(ORDER):
                            rows = LAST if t == KT - 1 else P
                            for half in range(2):
                                e_s.wait(act, gg * 2 * KT + 2 * n + half + 1)
                                if half == 0:
                                    e_av.wait(act, gg * KT + n - 1)
                                    if n == 0:
                                        e_ad.wait(act, gg * NA)
                                    elif n - 2 in ADDED:
                                        e_ad.wait(act, gg * NA + n - 1 - ADDED[0])
                                act.activation(prob[0:rows, n % 2, 2 * half:2 * half + 2, :],
                                               ps[0:rows, 2 * half:2 * half + 2, :], ACT.Exp,
                                               scale=SCALE).then_inc(e_e.sem, 1)

                exponentials(0)
                with again(act, b):
                    exponentials(1)
                otherwise(act, ((e_e, 2 * KT * NG),))

        @block.vector
        def _(dve):
            dve.memset(ones[:, :], 1.0).then_inc(s_const.sem, 1)
            dve.memset(quer[STK:P, :, :], 0.0).then_inc(s_const.sem, 1)
            for i in range(6):
                whi.wait(dve, i + 1)
                dve.scalar_tensor_tensor(wts[:, i, 1, :], wstage[i % 2], WS, wts[:, i, 0, :], ALU.mult,
                                         ALU.subtract).then_inc(wlo.sem, 1)
            dve.wait_ge(s_c, 16 * (6 + 3 + HEADS))

            def low(s, n, count):
                e_hi.wait(dve, n)
                dve.tensor_tensor(hl[s][:, 1, :], raw[s], hl[s][:, 0, :], ALU.subtract).then_inc(e_hl.sem, 1)

            def norm_x(pos, n, b):
                m = dve.snap(b * QT + pos - KT + 1)
                dve.wait_ge(s_in[pos % 2], 16 * slots(b, pos))
                dve.bn_stats(st6, raw[pos % 2]).then_inc(e_st.sem, 1)
                e_st.wait(dve, m)
                apart(dve)
                dve.bn_aggr(mv, st6).then_inc(e_mv.sem, 1)
                e_rs.wait(dve, m)
                dve.tensor_scalar(xnorm, raw[pos % 2], mv[:, 0:1], rs, ALU.subtract, ALU.mult).then_inc(e_xn.sem, 1)
                e_hi.wait(dve, n)
                dve.tensor_tensor(xs[:, 1, :], xnorm, xs[:, 0, :], ALU.subtract).then_inc(e_xs.sem, 1)

            def tile(n, s, ranges, value, prep, prev, after):
                prep()
                e_pk.wait(dve, n)
                for a, z, bias, _, _ in ranges:
                    ins = dve.scalar_tensor_tensor(kraw[a:z, :], ps[a:z, s, :], 1.0 / WS, vec[a:z, bias, :], ALU.mult,
                                                   ALU.add)
                ins.then_inc(e_kr.sem, 1)
                if value is not None:
                    for a, z, _, _, vb in ranges:
                        ins = dve.scalar_tensor_tensor(
                            vals[a:z, bass.ds(value, 1), :].rearrange("p a n -> p (a n)"), ps[a:z, 2 + s, :],
                            1.0 / WS, vec[a:z, vb, :], ALU.mult, ALU.add)
                    ins.then_inc(e_v.sem, 1)
                after()
                if prev is not None:
                    store_turned(n - 1, *prev)
                e_rin.wait(dve, n)
                e_c1.wait(dve, n - 1)
                for a, z, _, weight, _ in ranges:
                    ins = dve.scalar_tensor_tensor(knorm[a:z, :], kraw[a:z, :], rin[a:z, :], vec[a:z, weight, :],
                                                   ALU.mult, ALU.mult)
                ins.then_inc(e_kn.sem, 1)
                e_c0.wait(dve, n)
                st = stack[s]
                kn = knorm.rearrange("p (h d) -> p h d", h=HEADS)
                third = 1 if value is None else 2
                dve.tensor_tensor(st[:, :, third * HD:(third + 1) * HD], kn, st[:, :, 0:HD],
                                  ALU.subtract).then_inc(e_lo.sem, 1)

            def store_turned(n, tile, q):
                e_t.wait(dve, n)
                dst = quer if q else keys
                dve.tensor_copy(dst[0:STK, 8:16, bass.ds(tile * P, P)], turned[0:STK, 8:16, :]).then_inc(e_td.sem, 1)

            def nothing():
                pass

            TEXT = [(0, P, KB, KW, VB)]
            IMAGE = [(0, P, KB + 1, KW + 1, VB + 1)]
            MIXED = [(0, SPLIT, KB, KW, VB), (SPLIT, P, KB + 1, KW + 1, VB + 1)]
            QUERY = [(0, P, QB, QW, None)]

            with dve.Fori(0, B) as b:
                e_vg.wait(dve, 2 * b * NG * KT)
                low(0, b * POS + 1, None)
                tile(b * POS + 1, 0, TEXT, 0, lambda: low(1, b * POS + 2, None), None, nothing)
                with dve.Fori(0, PAIRS) as i:
                    for u in range(2):
                        n = dve.snap(b * POS + i * 2 + u + 2)
                        tile(n, 1 - u, TEXT, i * 2 + u + 1, lambda: low(u, n + 1, None),
                             (i * 2 + u, False), nothing)
                for pos in range(2 * PAIRS + 1, POS):
                    n = dve.snap(b * POS + pos + 1)
                    nxt = pos + 1
                    prep, after = nothing, nothing
                    if nxt < POS and is_q(nxt):
                        prep = lambda: norm_x(nxt, n + 1, b)

                        def after():
                            e_xt.wait(dve, b * QT + nxt - KT + 1)
                            e_pk.wait(dve, n - 1)
                            dve.tensor_copy(hl[nxt % 2].rearrange("p s n -> p (s n)"), xturned).then_inc(e_hl.sem, 1)
                    elif nxt < POS:
                        prep = lambda: low(nxt % 2, n + 1, None)
                    q = pos - 1 >= KT
                    prev = (pos - 1 - KT if q else pos - 1, q)
                    ranges = QUERY if is_q(pos) else (TEXT, MIXED, IMAGE)[kind(pos)]
                    tile(n, pos % 2, ranges, None if is_q(pos) else pos, prep, prev, after)
                store_turned(b * POS + POS, QT - 1, True)

                def results(p):
                    with dve.Fori(0, NG) as g:
                        gg = dve.snap((2 * b + p) * NG + g + 1)
                        pr = lambda n: prob[:, n % 2, :, :].rearrange("p h q -> p (h q)")
                        sm = added.rearrange("p h q -> p (h q)")
                        e_av.wait(dve, gg * KT - KT)
                        for k, n in enumerate(ADDED):
                            e_e.wait(dve, (gg - 1) * 2 * KT + 2 * n + 2)
                            if k == 0:
                                ins = dve.tensor_copy(sm, pr(n))
                            else:
                                e_ad.wait(dve, (gg - 1) * NA + k)
                                ins = dve.tensor_tensor(sm, sm, pr(n), ALU.add)
                            ins.then_inc(e_ad.sem, 1)
                        oimg = attn32[:, bass.ds(g, 1), :].rearrange("p a n -> p (a n)")
                        part = lambda k: attn[:, bass.ds(g, 1), k, :].rearrange("p a n -> p (a n)")
                        if p == 0:
                            e_ck.wait(dve, (b * NG + g) * 6 - 3)
                        dve.reciprocal(rden_i, ps[:, DEN_I, :]).then_inc(e_ri.sem, 1)
                        e_ri.wait(dve, gg)
                        dve.tensor_tensor(oimg, ps[:, NUM_I, :], rden_i, ALU.mult).then_inc(e_oi.sem, 1)
                        e_av.wait(dve, gg * KT)
                        e_oi.wait(dve, gg)
                        if p == 0:
                            e_ck.wait(dve, (b * NG + g) * 6)
                        dve.reciprocal(rden_t, ps[:, DEN_T, :]).then_inc(e_rt2.sem, 1)
                        e_rt2.wait(dve, gg)
                        e_at.wait(dve, gg - 1)
                        dve.tensor_tensor(proj, ps[:, NUM_T, :], rden_t, ALU.mult).then_inc(e_ot.sem, 1)
                        e_ot.wait(dve, gg)
                        dve.tensor_tensor(proj, proj, oimg, ALU.add).then_inc(e_os.sem, 1)
                        e_os.wait(dve, gg)
                        dve.tensor_copy(part(0), proj).then_inc(e_oh.sem, 1)
                        e_oh.wait(dve, gg)
                        dve.tensor_tensor(part(1), proj, part(0), ALU.subtract).then_inc(e_at.sem, 1)

                def maxima():
                    with dve.Fori(0, HEADS) as h:
                        for t in range(QT):
                            k = dve.snap(b * HEADS * QT + h * QT + t + 1)
                            bank = 4 * (t % 2)
                            e_ms.wait(dve, k)
                            for kd, (a, z, e) in enumerate(((0, TXT, e_mt), (1536, 1536 + IMG, e_mi))):
                                dve.tensor_reduce(mx[:, bass.ds(h, 1), t, kd],
                                                  ps[:, bank:bank + 4, :].rearrange("p a n -> p (a n)")[:, a:z],
                                                  mybir.AxisListType.X, ALU.max).then_inc(e.sem, 1)
                    e_mt.wait(dve, b * HEADS * QT + HEADS * QT)
                    e_mi.wait(dve, b * HEADS * QT + HEADS * QT)
                    dve.memset(mh[:, 0:STK], 0.0).then_inc(e_mh.sem, 1)
                    dve.tensor_scalar(mh[:, STK:], mx.rearrange("p h t s -> p (h t s)"), -1.0 / SHIFT, None,
                                      ALU.mult).then_inc(e_mh.sem, 1)
                    e_mr.wait(dve, b + 1)
                    dve.tensor_copy(quer[STK:STK + 2, :, :].rearrange("p h q -> p (h q)"),
                                    ps[STK:STK + 2, :, :].rearrange("p a n -> p (a n)").bitcast(F16)).then_inc(e_mc.sem, 1)

                results(0)
                e_ck.wait(dve, (b * NG + NG) * 6)
                dve.tensor_reduce(total, odds, mybir.AxisListType.X, ALU.add).then_inc(e_fm.sem, 1)
                e_fs.wait(dve, b + 1)
                dve.tensor_scalar(flag[:, :], ps[0:1, 0, 0:1], SAFE, 0.0, ALU.is_le, ALU.is_equal).then_inc(e_fl.sem, 1)
                with again(dve, b):
                    maxima()
                    results(1)
                    dve.memset(quer[STK:STK + 2, :, :], 0.0).then_inc(e_qz.sem, 1)
                otherwise(dve, ((e_mt, HEADS * QT), (e_mi, HEADS * QT), (e_mh, 2), (e_mc, 1), (e_ad, NA * NG),
                                (e_ri, NG), (e_oi, NG), (e_rt2, NG), (e_ot, NG), (e_os, NG), (e_oh, NG), (e_at, NG),
                                (e_qz, 1)))
                for j in range(QT):
                    m = b * QT + j + 1
                    e_po.wait(dve, m)
                    e_x1.wait(dve, m - 1)
                    dve.scalar_tensor_tensor(proj, ps[:, j % 2, :], 1.0 / WS, vec[:, OB, :], ALU.mult,
                                             ALU.add).then_inc(e_ob.sem, 1)
                    e_ob.wait(dve, m)
                    dve.wait_ge(s_x[j], 16 * (b + 1))
                    dve.tensor_tensor(xres[j], xres[j], proj, ALU.add).then_inc(e_x1.sem, 1)

        @block.tensor
        def _(pe):
            s_const.wait(pe, 4)
            wlo.wait(pe, 6)

            def product(out, lhs, w, cols=slice(0, P)):
                steps = [(c, a, z) for c in range(NC) for a, z in ((0, 0), (0, 1), (1, 0))]
                for k, (c, a, z) in enumerate(steps):
                    mm = pe.matmul(out, lhs(a, c)[:, cols], wts[:, w, z, c * D:(c + 1) * D],
                                   start=(k == 0), stop=(k == len(steps) - 1))
                return mm

            def project(n, s, pos):
                e_hl.wait(pe, n)
                lhs = lambda a, c: hl[s][:, a, c * P:(c + 1) * P]
                if is_q(pos):
                    product(ps[:, s, :], lhs, WQ).then_inc(e_pk.sem, 1)
                elif kind(pos) == 1:
                    lo, hi = slice(0, SPLIT), slice(SPLIT, P)
                    product(ps[0:SPLIT, 2 + s, :], lhs, WV, lo)
                    product(ps[SPLIT:P, 2 + s, :], lhs, WVI, hi).then_inc(e_pv.sem, 1)
                    product(ps[0:SPLIT, s, :], lhs, WK, lo)
                    product(ps[SPLIT:P, s, :], lhs, WKI, hi).then_inc(e_pk.sem, 1)
                else:
                    txt = kind(pos) == 0
                    product(ps[:, 2 + s, :], lhs, WV if txt else WVI).then_inc(e_pv.sem, 1)
                    product(ps[:, s, :], lhs, WK if txt else WKI).then_inc(e_pk.sem, 1)

            def turn_stacks(n, s):
                e_lo.wait(pe, n)
                e_c1.wait(pe, n)
                e_td.wait(pe, n - 1)
                e_ta.wait(pe, n - 1)
                for h in range(HEADS):
                    tr = pe.transpose(turned[0:STK, h, :], stack[s][:, h, :], ident[:, :])
                tr.then_inc(e_t.sem, 1)

            def turn_x(m):
                e_xs.wait(pe, m)
                for a in range(2):
                    for c in range(NC):
                        tr = pe.transpose(xturned[:, (a * NC + c) * P:(a * NC + c + 1) * P],
                                          xs[:, a, c * P:(c + 1) * P], ident[:, :])
                tr.then_inc(e_xt.sem, 1)

            with pe.Fori(0, B) as b:
                e_ot.wait(pe, 2 * b * NG)
                e_x1.wait(pe, b * QT)
                project(b * POS + 1, 0, 0)
                with pe.Fori(0, PAIRS) as i:
                    for u in range(2):
                        n = pe.snap(b * POS + i * 2 + u + 2)
                        project(n, 1 - u, 0)
                        turn_stacks(n - 1, u)
                for pos in range(2 * PAIRS + 1, POS):
                    n = pe.snap(b * POS + pos + 1)
                    project(n, pos % 2, pos)
                    if pos + 1 < POS and is_q(pos + 1):
                        turn_x(b * QT + pos + 1 - KT + 1)
                    turn_stacks(n - 1, (pos - 1) % 2)
                turn_stacks(b * POS + POS, (POS - 1) % 2)
                e_td.wait(pe, b * POS + POS)
                e_ta.wait(pe, b * POS + POS)
                apart(pe)

                def score_maxima():
                    with pe.Fori(0, HEADS) as h:
                        for t in range(QT):
                            k = pe.snap(b * HEADS * QT + h * QT + t + 1)
                            bank = 4 * (t % 2)
                            e_mi.wait(pe, k - 2)
                            for c, (a, z) in enumerate(((0, 512), (512, 1024), (1024, TXT), (TXT, TXT + IMG))):
                                mm = pe.matmul(ps[:, bank + c, 0:z - a],
                                               quer[0:STK, bass.ds(h, 1), t * P:(t + 1) * P].rearrange("p a n -> p (a n)"),
                                               keys[0:STK, bass.ds(h, 1), a:z].rearrange("p a n -> p (a n)"),
                                               start=True, stop=True)
                            mm.then_inc(e_ms.sem, 1)
                    e_mh.wait(pe, 2 * b + 2)
                    turned_mx = ps[:, :, :].rearrange("p a n -> p (a n)").bitcast(F16)
                    for k in range(HEADS * QT):
                        tr = pe.transpose(turned_mx[0:STK + 2, k * P:(k + 1) * P], mh[:, 2 * k:2 * k + STK + 2], ident[:, :])
                    tr.then_inc(e_mr.sem, 1)
                    e_mc.wait(pe, b + 1)
                    apart(pe)

                def attention(p):
                    with pe.Fori(0, NG) as g:
                        gg = pe.snap((2 * b + p) * NG + g)

                        def scores(n, half):
                            t = ORDER[n]
                            rows = LAST if t == KT - 1 else P
                            e_e.wait(pe, gg * 2 * KT + 2 * n + half - 1)
                            for h in range(2 * half, 2 * half + 2):
                                mm = pe.matmul(ps[0:rows, h, :],
                                               keys[:, bass.ds(g * 4 + h, 1), t * P:t * P + rows].rearrange("p a n -> p (a n)"),
                                               quer[:, bass.ds(g * 4 + h, 1), :].rearrange("p a n -> p (a n)"),
                                               start=True, stop=True)
                            mm.then_inc(e_s.sem, 1)

                        def numerators(n):
                            t = ORDER[n]
                            for a, z, img, first, last in parts(n):
                                for h in range(4):
                                    mm = pe.matmul(ps[h * HD:(h + 1) * HD, NUM_I if img else NUM_T, :],
                                                   vgrp[a:z, t, h * HD:(h + 1) * HD], prob[a:z, n % 2, h, :],
                                                   start=first, stop=last)
                            return mm

                        def denominators(n, src):
                            for a, z, img, first, last in parts(n):
                                for h in range(4):
                                    mm = pe.matmul(ps[h * HD:(h + 1) * HD, DEN_I if img else DEN_T, :], ones[a:z, :],
                                                   src[a:z, h, :], start=first, stop=last and img == 1)
                            return mm

                        scores(0, 0)
                        scores(0, 1)
                        for n in range(KT):
                            if n + 1 < KT:
                                scores(n + 1, 0)
                                scores(n + 1, 1)
                            e_vg.wait(pe, gg * KT + n + 1)
                            e_e.wait(pe, gg * 2 * KT + 2 * n + 2)
                            if n == 0:
                                e_oi.wait(pe, gg)
                            if ORDER[n] == MIX:
                                e_ot.wait(pe, gg)
                                apart(pe)
                            mm = numerators(n)
                            if n not in ADDED:
                                mm = denominators(n, prob[:, n % 2, :, :])
                            if n == KT - 1:
                                e_ad.wait(pe, gg * NA + NA)
                                for h in range(4):
                                    mm = pe.matmul(ps[h * HD:(h + 1) * HD, DEN_T, :], ones[:, :], added[:, h, :],
                                                   start=False, stop=True)
                            mm.then_inc(e_av.sem, 1)

                attention(0)
                e_fm.wait(pe, b + 1)
                pe.matmul(ps[0:1, 0, 0:1], total, ones[:, 0:1], start=True, stop=True).then_inc(e_fs.sem, 1)
                with again(pe, b):
                    score_maxima()
                    attention(1)
                otherwise(pe, ((e_ms, HEADS * QT), (e_mr, 1), (e_s, 2 * KT * NG), (e_av, KT * NG)))
                e_at.wait(pe, (2 * b + 2) * NG)
                e_qz.wait(pe, b + 1)
                for j in range(QT):
                    if j >= 2:
                        e_ob.wait(pe, b * QT + j - 1)
                    product(ps[:, j % 2, :], lambda a, c: attn[:, c, a, j * P:(j + 1) * P], WO).then_inc(e_po.sem, 1)


_ORDER_OF_W = ("q_w", "k_w", "v_w", "k_img_w", "v_img_w", "o_w")


def lay_attention(inputs):
    a = {k[len("L0_xattn_"):]: np.asarray(v) for k, v in inputs.items() if k.startswith("L0_xattn_")}
    w6 = np.stack([a[n].T.reshape(NC, P, D).transpose(1, 0, 2).reshape(P, NC * D) for n in _ORDER_OF_W])
    c = np.asarray(inputs["ctx_2048"])
    c = np.concatenate([c[:, IMG:], c[:, :IMG], np.zeros((B, KPAD - TXT - IMG, D), c.dtype)], axis=1)
    c = c.reshape(B, KT, P, NC, P).transpose(0, 1, 4, 3, 2).reshape(B * KT, P, D)
    mark = np.zeros((P - STK, KPAD), np.float16)
    mark[0, :TXT] = SHIFT
    mark[1, TXT:TXT + IMG] = SHIFT
    return {
        "x": np.asarray(inputs["x"]).reshape(T, D), "ctx": c, "w6": w6, "mark": mark,
        "kb": a["k_b"], "kw": a["norm_k_w"], "vb": a["v_b"], "kib": a["k_img_b"], "kiw": a["norm_k_img_w"],
        "vib": a["v_img_b"], "qb": a["q_b"], "qw": a["norm_q_w"], "ob": a["o_b"],
    }


E, TOPK, CAP, I = 32, 4, 80, 256
GRP, TOPG = 8, 3
NT = T // P
I2 = 512
NI = I2 // P
TROW = D + E
DUMMY = P
BIG = 1000.0
RING = 4
RSCALE = 2.5
N_CONST = 14


def ffn_program(nc, d, x1_dram, table, arow, out):
    with ExitStack() as ctx:
        def sb(name, shape, dt):
            return ctx.enter_context(nc.sbuf_tensor("f_" + name, shape, dt))

        s_apart = ctx.enter_context(nc.semaphore("f_s_apart"))

        def apart(eng):
            eng.sem_inc(s_apart, 1)

        events = []

        def event(name, ahead=0):
            e = Event(ctx, nc, "f_" + name, ahead)
            events.append(e)
            return e

        def dma_sem(name):
            return ctx.enter_context(nc.semaphore("f_" + name))

        x1s = sb("x1s", [P, NT, D], F32)
        x2t = sb("x2t", [P, 2, NC, T], F16)
        swt = sb("swt", [P, 3, 2, NC * D], F16)
        SG, SU, SD = range(3)
        rwt = sb("rwt", [P, 2, NC * E], F16)
        rraw = sb("rraw", [P, NC * E], F32)
        xn = sb("xn", [P, 2, D], F32)
        xs = sb("xs", [P, 2, 2, D], F16)
        stat = sb("stat", [P, 2, 16], F32)
        mhalf = sb("mhalf", [P, 1], F32)
        ident = sb("ident", [P, P], F16)
        identf = sb("identf", [P, P], F32)
        zero = sb("zero", [P, TROW], F32)
        wring = sb("wring", [P, RING, 3 * 2 * D], F32)
        ex = sb("ex", [P, D], F32)
        rc = sb("rc", [P, D], F32)
        hs = sb("hs", [P, 2, NI, D], F16)
        ebias = sb("ebias", [P, E], F32)
        rt = [sb(f"rt{i}", [P, NT, E], F32) for i in range(6)]
        gt = [sb(f"gt{i}", [P, NT, GRP], F32) for i in range(6)]
        gidx = sb("gidx", [P, NT, 8], U32)
        top8 = sb("top8", [P, NT, 8], F32)
        io8 = sb("io8", [P, GRP], F32)
        io32 = sb("io32", [P, E], F32)
        m16 = sb("m16", [P, NT, E], F16)
        c16 = sb("c16", [P, NT, E], F16)
        pv16 = sb("pv16", [P, NT, E], F16)
        wsum = sb("wsum", [P, NT], F32)
        before = sb("before", [P, P], F16)
        ones16 = sb("ones16", [P, P], F16)
        ioS = sb("ioS", [P, CAP, E], F16)
        oneh = sb("oneh", [P, 2, CAP, E], F16)
        tok = sb("tok", [P, NT], F16)
        arow_sb = oneh[0:1, :, :, :].rearrange("p a s e -> p (a s e)").bitcast(F32)
        ia = sb("ia", [CAP, E], F32)
        ib = sb("ib", [CAP, E], F32)
        sio = sb("sio", [P, 1], F32)
        idx = sb("idx", [CAP, E], U32)
        idc = [sb(f"idc{i}", [CAP, 1], U32) for i in range(RING)]
        wc = [sb(f"wc{i}", [CAP, 1], F32) for i in range(RING)]
        free = x2t[:, :, :, :].rearrange("p a c n -> p (a c n)").bitcast(F32)
        at = 0

        def take(rows, width):
            nonlocal at
            at += width
            return free[0:rows, at - width:at]

        xg = [take(CAP, TROW) for i in range(RING)]
        xgt = [take(P, NC * CAP).rearrange("p (c s) -> p c s", c=NC) for i in range(2)]
        ht = [take(P, 2 * CAP).rearrange("p (c s) -> p c s", c=2) for i in range(2)]
        yf = [take(CAP, D) for i in range(2)]
        eg, hh = take(CAP, I), take(CAP, I)
        ps = ctx.enter_context(nc.psum_tensor("f_ps", [P, 8, 512], F32))
        wst = [wring[:, i, 0:NC * D] for i in range(2)]

        s_w = [dma_sem(f"s_w{i}") for i in range(2)]
        s_r, s_z, s_tab, s_o, s_a, s_ia, s_wt = (dma_sem(n) for n in ("s_r", "s_z", "s_tab", "s_o", "s_a", "s_ia", "s_wt"))
        s_xl = [dma_sem(f"s_xl{i}") for i in range(4)]
        s_xt = [dma_sem(f"s_xt{i}") for i in range(2)]
        s_ring = [dma_sem(f"s_ring{i}") for i in range(RING)]
        s_g = [dma_sem(f"s_g{i}") for i in range(RING)]
        s_sc = dma_sem("s_sc")
        s_i0, s_const = event("s_i0"), event("s_const")
        whi, wlo = event("whi"), event("wlo")
        e_st, e_mv, e_rv, e_rs = event("e_st"), event("e_mv"), event("e_rv"), event("e_rs")
        e_xn, e_hi, e_xs, e_xt, e_x2 = event("e_xn"), event("e_hi"), event("e_xs", 2), event("e_xt", 2), event("e_x2", 2)
        e_r = event("e_r")
        e_ez = event("e_ez")
        link = event("link")
        e_m16, e_pos, e_pv, e_oh, e_a, e_ar, e_wv, e_idx = (event(n) for n in (
            "e_m16", "e_pos", "e_pv", "e_oh", "e_a", "e_ar", "e_wv", "e_idx"))
        e_a2 = event("e_a2")
        f_gu, f_e, f_t, f_h, f_hi, f_lo = (event(n, a) for n, a in (
            ("f_gu", 0), ("f_e", 0), ("f_t", 1), ("f_h", 1), ("f_hi", 0), ("f_lo", 2)))
        f_dn, f_ac = event("f_dn"), event("f_ac", 2)
        m_ix = event("m_ix")
        m_xt = event("m_xt")
        m_xc = event("m_xc", 1)
        m_w = event("m_w", 1)
        m_gu = event("m_gu")
        m_e = event("m_e")
        m_t = event("m_t", 1)
        m_h = event("m_h", 2)
        m_ht = event("m_ht", 1)
        m_hc = event("m_hc", 1)
        m_y = event("m_y", 2)
        m_yf = event("m_yf", 2)

        block = ctx.enter_context(nc.Block())

        def x1_rows(j, k=1):
            return x1_dram[j * P:(j + k) * P, :].rearrange("(k p) n -> p k n", p=P)

        @block.sync
        def _(sp):
            for e in events:
                if e.ahead:
                    sp.sem_inc(e.sem, e.ahead)
            sp.dma_start(rraw[:, :], d["rw"]).then_inc(s_r, 16)
            for k in range(4):
                sp.dma_start(x1s[:, 4 * k:4 * k + 4, :], x1_rows(4 * k, 4)).then_inc(s_xl[k], 16)
            sp.dma_start(ebias[:, :], d["ebias"].partition_broadcast(P)).then_inc(s_r, 16)
            for i in range(3):
                if i >= 2:
                    wlo.wait(sp, i - 1)
                sp.dma_start(wst[i % 2], d["w3"][i]).then_inc(s_w[i % 2], 16)
            s_const.wait(sp, N_CONST)
            sp.dma_start(table[T:T + DUMMY, :], zero[:, :]).then_inc(s_tab, 16)
            sp.dma_start(out[T:T + DUMMY, :], zero[:, 0:D]).then_inc(s_o, 16)
            with sp.Fori(0, NT // 2) as i:
                for u in range(2):
                    e_xn.wait(sp, i * 2 + u + 1)
                    sp.dma_start(table[bass.ds((i * 2 + u) * P, P), 0:D], xn[:, u, :]).then_inc(s_xt[u], 16)
            wlo.wait(sp, 3)
            for e in range(RING):
                sp.dma_start(wring[:, e, :], d["wx"][e]).then_inc(s_ring[e], 16)
            e_wv.wait(sp, 1)
            sp.dma_start(table[0:T, D:TROW].rearrange("(j p) n -> p j n", p=P), rt[5][:, :, :]).then_inc(s_wt, 16)
            e_ar.wait(sp, 1)
            sp.dma_start(arow, arow_sb).then_inc(s_a, 16)
            sp.wait_ge(s_a, 16)
            sp.dma_start(ia[:, :], arow.rearrange("a (s e) -> (a s) e", e=E)).then_inc(s_ia, 16)
            with sp.Fori(0, NT // 4) as bk:
                for q in range(4):
                    j = bk * 4 + q
                    f_ac.wait(sp, j + 1)
                    sp.dma_start(out[bass.ds(j * P, P), :], x1s[:, bass.ds(j, 1), :].rearrange("p a n -> p (a n)")).then_inc(s_o, 16)
            with sp.Fori(0, E // RING - 1) as o:
                for k in range(RING):
                    m_y.wait(sp, o * RING + k + 1)
                    sp.dma_start(wring[:, k, :], d["wx"][bass.ds((o + 1) * RING + k, 1)].rearrange("a p n -> (a p) n")).then_inc(s_ring[k], 16)
            sp.wait_ge(s_o, 16 * (NT + 1))
            sp.wait_ge(s_sc, 16 * E)


        @block.gpsimd
        def _(pool):
            c = s_const.sem
            pool.memset(ident[:, :], 0.0).then_inc(s_i0.sem, 1)
            pool.memset(identf[:, :], 0.0).then_inc(s_i0.sem, 1)
            pool.memset(before[:, :], 1.0).then_inc(s_i0.sem, 1)
            s_i0.wait(pool, 3)
            for t in (ident, identf):
                pool.affine_select(out=t[:, :], in_=t[:, :], pattern=[[-1, P]], compare_op=ALU.not_equal, fill=1.0,
                                   base=0, channel_multiplier=1).then_inc(c, 1)
            pool.affine_select(out=before[:, :], in_=before[:, :], pattern=[[1, P]], compare_op=ALU.is_gt, fill=0.0,
                               base=0, channel_multiplier=-1).then_inc(c, 1)
            pool.memset(mhalf[:, :], -0.5).then_inc(c, 1)
            pool.memset(zero[:, :], 0.0).then_inc(c, 1)
            pool.memset(ones16[:, :], 1.0).then_inc(c, 1)
            pool.iota(io8[:, :], [[1, GRP]], base=0, channel_multiplier=0, allow_small_or_imprecise_dtypes=True).then_inc(c, 1)
            pool.iota(io32[:, :], [[1, E]], base=0, channel_multiplier=0, allow_small_or_imprecise_dtypes=True).then_inc(c, 1)
            pool.iota(ioS[:, :, :], [[1, CAP], [0, E]], base=0, channel_multiplier=0, allow_small_or_imprecise_dtypes=True).then_inc(c, 1)
            pool.iota(tok[:, :], [[P, NT]], base=-T, channel_multiplier=1, allow_small_or_imprecise_dtypes=True).then_inc(c, 1)
            pool.iota(sio[:, :], [[1, 1]], base=0, channel_multiplier=1, allow_small_or_imprecise_dtypes=True).then_inc(c, 1)
            pool.memset(c16[:, 0, :], 0.0).then_inc(c, 1)
            s_const.wait(pool, N_CONST)
            with pool.Fori(0, NT // 2) as i:
                for u in range(2):
                    m = i * 2 + u + 1
                    e_mv.wait(pool, m)
                    apart(pool)
                    pool.tensor_scalar(stat[:, u, 9:10], stat[:, u, 7:8], 1.0, 1e-5, ALU.mult, ALU.add).then_inc(e_rv.sem, 1)
                    e_rv.wait(pool, m)
                    pool.tensor_tensor(stat[:, u, 8:9], stat[:, u, 9:10], mhalf[:, :], ALU.pow).then_inc(e_rs.sem, 1)
            e_idx.wait(pool, 1)
            pool.wait_ge(s_tab, 16)
            pool.wait_ge(s_wt, 16)
            for s in s_xt:
                pool.wait_ge(s, 16 * (NT // 2))

            f_ac.wait(pool, NT)

            def gather(n, u):
                pool.tensor_copy(idc[u][:, :], idx[:, bass.ds(n - 1, 1)]).then_inc(m_ix.sem, 1)
                m_ix.wait(pool, n)
                apart(pool)
                pool.indirect_dma_start(out=xg[u], out_offset=None, in_=table[:, :],
                                        in_offset=bass.IndirectOffsetOnAxis(ap=idc[u][:, 0:1], axis=0)).then_inc(s_g[u], 16)

            def scatter(n, u):
                m_yf.wait(pool, n)
                apart(pool)
                pool.indirect_dma_start(out=out[:, :], out_offset=bass.IndirectOffsetOnAxis(ap=idc[u][:, 0:1], axis=0),
                                        in_=yf[u % 2], in_offset=None, compute_op=ALU.add).then_inc(s_sc, 16)

            for u in range(RING):
                gather(u + 1, u)
            pool.wait_ge(s_o, 16 * (NT + 1))

            def experts(o, last):
                for k in range(RING):
                    n = o * RING + k + 1
                    scatter(n, k)
                    pool.wait_ge(s_sc, n * 16)
                    if not last:
                        gather(n + RING, k)

            with pool.Fori(0, E // RING - 1) as o:
                experts(o, False)
            experts(E // RING - 1, True)

        @block.scalar
        def _(act):
            act.wait_ge(s_r, 32)
            act.activation(rwt[:, 0, :], rraw[:, :], ACT.Copy, scale=WS).then_inc(whi.sem, 1)
            for i in range(3):
                act.wait_ge(s_w[i % 2], 16 * (i // 2 + 1))
                act.activation(swt[:, i, 0, :], wst[i % 2], ACT.Copy, scale=WS).then_inc(whi.sem, 1)
            with act.Fori(0, NT // 2) as i:
                for u in range(2):
                    m = act.snap(i * 2 + u + 1)
                    e_xn.wait(act, m)
                    e_xt.wait(act, m - 2)
                    act.copy(xs[:, u, 0, :], xn[:, u, :]).then_inc(e_hi.sem, 1)
            e_r.wait(act, 1)
            act.activation(rt[0].rearrange("p j e -> p (j e)"), ps[:, 2, :], ACT.Exp, scale=-1.0 / WS).then_inc(e_ez.sem, 1)
            e_a.wait(act, 1)
            for k in range(CAP * E // 512):
                cp = act.copy(arow_sb[:, k * 512:(k + 1) * 512], ps[0:1, 3 + k, :])
            cp.then_inc(e_ar.sem, 1)
            with act.Fori(0, NT // 4) as bk:
                for it in range(NI):
                    n = act.snap(bk * NI + it + 1)
                    f_gu.wait(act, n)
                    f_t.wait(act, n - 1)
                    act.activation(ex[:, :], ps[:, it % 2, :], ACT.Tanh, scale=0.5 / WS).then_inc(f_e.sem, 1)
                    f_h.wait(act, n)
                    act.copy(hs[:, 0, it, :], rc[:, :]).then_inc(f_hi.sem, 1)

            def expert(n, u):
                m_gu.wait(act, n)
                m_t.wait(act, n - 1)
                act.activation(eg, ps[0:CAP, 7 if u % 2 == 0 else 0, 0:I], ACT.Tanh, scale=0.5).then_inc(m_e.sem, 1)
                m_y.wait(act, n)
                m_w.wait(act, n)
                if not isinstance(n, int):
                    act.wait_ge(s_sc, (n - 2) * 16)
                act.activation(yf[u % 2], ps[0:CAP, 2 + u % 2, :], ACT.Copy, scale=wc[u][:, 0:1]).then_inc(m_yf.sem, 1)

            for u in range(RING):
                if u >= 2:
                    act.wait_ge(s_sc, (u - 1) * 16)
                expert(u + 1, u)
            with act.Fori(1, E // RING) as o:
                for u in range(RING):
                    expert(act.snap(o * RING + u + 1), u)

        @block.vector
        def _(dve):
            count = [0]

            def chain(ins):
                count[0] += 1
                ins.then_inc(link.sem, 1)
                link.wait(dve, count[0])

            dve.memset(stat[:, :, :], 0.0).then_inc(s_const.sem, 1)
            dve.memset(ia[:, :], 0.0).then_inc(s_const.sem, 1)
            s_const.wait(dve, N_CONST)
            whi.wait(dve, 1)
            chain(dve.scalar_tensor_tensor(rwt[:, 1, :], rraw[:, :], WS, rwt[:, 0, :], ALU.mult, ALU.subtract))
            for i in range(3):
                whi.wait(dve, i + 2)
                dve.scalar_tensor_tensor(swt[:, i, 1, :], wst[i % 2], WS, swt[:, i, 0, :], ALU.mult,
                                         ALU.subtract).then_inc(wlo.sem, 1)

            for k in range(4):
                dve.wait_ge(s_xl[k], 16)

            def norm(m, u, j):
                xj = x1s[:, bass.ds(j, 1), :].rearrange("p a n -> p (a n)")
                e_xs.wait(dve, m - 2)
                dve.bn_stats(stat[:, u, 0:6], xj).then_inc(e_st.sem, 1)
                e_st.wait(dve, m)
                apart(dve)
                dve.bn_aggr(stat[:, u, 6:8], stat[:, u, 0:6]).then_inc(e_mv.sem, 1)

            def apply(m, u, j, stored):
                xj = x1s[:, bass.ds(j, 1), :].rearrange("p a n -> p (a n)")
                e_rs.wait(dve, m)
                if stored is not None:
                    dve.wait_ge(s_xt[u], stored)
                dve.tensor_scalar(xn[:, u, :], xj, stat[:, u, 6:7], stat[:, u, 8:9], ALU.subtract, ALU.mult).then_inc(e_xn.sem, 1)
                e_hi.wait(dve, m)
                dve.tensor_tensor(xs[:, u, 1, :], xn[:, u, :], xs[:, u, 0, :], ALU.subtract).then_inc(e_xs.sem, 1)

            def store(m, u, j):
                e_xt.wait(dve, m)
                dve.tensor_copy(x2t[:, :, :, bass.ds(j * P, P)].rearrange("p a c n -> p (a c) n"),
                                ps[:, u, :].bitcast(F16).rearrange("p (k n) -> p k n", n=P)).then_inc(e_x2.sem, 1)

            for u in range(2):
                norm(u + 1, u, u)
                apply(u + 1, u, u, None)
                store(u + 1, u, u)
            with dve.Fori(1, NT // 2) as i:
                for u in range(2):
                    m = dve.snap(i * 2 + u + 1)
                    norm(m, u, i * 2 + u)
                    apply(m, u, i * 2 + u, i * 16)
                    store(m, u, i * 2 + u)

            TT = dve.tensor_tensor
            fl = lambda t: t.rearrange("p j e -> p (j e)")
            scores, sc, masked, mask, tmp, wv = rt
            e_ez.wait(dve, 1)
            chain(dve.tensor_scalar(fl(tmp), fl(scores), 1.0, None, ALU.add))
            chain(dve.reciprocal(fl(scores), fl(tmp)))
            chain(TT(sc[:, :, :], scores[:, :, :], ebias[:, :].unsqueeze(1).to_broadcast([P, NT, E]), ALU.add))
            q4 = sc[:, :, :].rearrange("p j (g k) -> p (j g) k", k=4)
            G = [t[:, :, :].rearrange("p j g -> p (j g)") for t in gt]
            chain(TT(G[0], q4[:, :, 0], q4[:, :, 1], ALU.max))
            chain(TT(G[1], q4[:, :, 0], q4[:, :, 1], ALU.min))
            chain(TT(G[2], q4[:, :, 2], q4[:, :, 3], ALU.max))
            chain(TT(G[3], q4[:, :, 2], q4[:, :, 3], ALU.min))
            chain(TT(G[4], G[0], G[2], ALU.max))
            chain(TT(G[5], G[0], G[2], ALU.min))
            chain(TT(G[0], G[1], G[3], ALU.max))
            chain(TT(G[1], G[5], G[0], ALU.max))
            chain(TT(G[2], G[4], G[1], ALU.add))

            def top(values):
                for j in range(NT):
                    ins = dve.max(top8[:, j, :], values[:, j, :])
                chain(ins)
                for j in range(NT):
                    ins = dve.max_index(gidx[:, j, :], top8[:, j, :], values[:, j, :])
                chain(ins)
                chain(dve.tensor_copy(gt[5][:, :, :], gidx[:, :, :]))

            def chosen(outm, t, k, iota, n):
                for r in range(k):
                    dst = outm if r == 0 else t
                    chain(TT(dst[:, :, :], gt[5][:, :, r:r + 1].to_broadcast([P, NT, n]),
                             iota[:, :].unsqueeze(1).to_broadcast([P, NT, n]), ALU.is_equal))
                    if r:
                        chain(TT(outm[:, :, :], outm[:, :, :], t[:, :, :], ALU.add))

            top(gt[2])
            chosen(gt[0], gt[1], TOPG, io8, GRP)
            chain(TT(masked[:, :, :].rearrange("p j (g k) -> p (j g) k", k=4), q4,
                     G[0].unsqueeze(2).to_broadcast([P, NT * GRP, 4]), ALU.mult))
            chain(dve.tensor_scalar(fl(masked), fl(masked), 0.0, None, ALU.add))
            top(masked)
            chosen(mask, tmp, TOPK, io32, E)
            chain(TT(fl(tmp), fl(scores), fl(mask), ALU.mult))
            chain(dve.tensor_reduce(wsum[:, :], tmp[:, :, :], mybir.AxisListType.X, ALU.add))
            chain(dve.tensor_scalar(wsum[:, :], wsum[:, :], 1e-20, None, ALU.add))
            chain(dve.reciprocal(wsum[:, :], wsum[:, :]))
            chain(dve.scalar_tensor_tensor(wv[:, :, :], tmp[:, :, :], RSCALE, wsum[:, :].unsqueeze(2).to_broadcast([P, NT, E]),
                                           ALU.mult, ALU.mult))
            chain(dve.tensor_copy(fl(m16), fl(mask)))
            for j in range(1, NT):
                chain(TT(c16[:, j, :], c16[:, j - 1, :], m16[:, j - 1, :], ALU.add))
            dve.sem_inc(e_m16.sem, 1)
            e_pos.wait(dve, 1)
            chain(dve.scalar_tensor_tensor(fl(tmp), ps[:, 3, :], float(CAP), fl(mask), ALU.is_lt, ALU.mult))
            chain(TT(fl(wv), fl(wv), fl(tmp), ALU.mult))
            dve.sem_inc(e_wv.sem, 1)
            chain(dve.scalar_tensor_tensor(fl(masked), ps[:, 3, :], -BIG, fl(tmp), ALU.add, ALU.mult))
            chain(dve.tensor_scalar(fl(pv16), fl(masked), BIG, None, ALU.add))
            for j in range(NT):
                if j >= 2:
                    e_a2.wait(dve, j - 1)
                TT(oneh[:, j % 2, :, :], ioS[:, :, :], pv16[:, j, :].unsqueeze(1).to_broadcast([P, CAP, E]),
                   ALU.is_equal).then_inc(e_oh.sem, 1)
            dve.wait_ge(s_ia, 16)
            chain(dve.tensor_scalar(ib[:, :], ia[:, :], 0.0, None, ALU.is_equal))
            chain(dve.tensor_scalar(ib[:, :], ib[:, :], sio[0:CAP, 0:1], None, ALU.mult))
            chain(dve.scalar_tensor_tensor(ib[:, :], ia[:, :], float(T), ib[:, :], ALU.add, ALU.add))
            dve.tensor_copy(idx[:, :], ib[:, :]).then_inc(e_idx.sem, 1)

            with dve.Fori(0, NT // 4) as bk:
                for it in range(NI):
                    n = dve.snap(bk * NI + it + 1)
                    f_e.wait(dve, n)
                    f_lo.wait(dve, n - 1)
                    dve.scalar_tensor_tensor(rc[:, :], ex[:, :], 1.0, ps[:, it % 2, :], ALU.add, ALU.mult).then_inc(f_t.sem, 1)
                    f_t.wait(dve, n)
                    dve.scalar_tensor_tensor(rc[:, :], rc[:, :], 0.5 / WS / WS, ps[:, 2 + it % 2, :], ALU.mult,
                                             ALU.mult).then_inc(f_h.sem, 1)
                    f_hi.wait(dve, n)
                    TT(hs[:, 1, it, :], rc[:, :], hs[:, 0, it, :], ALU.subtract).then_inc(f_lo.sem, 1)
                for q in range(4):
                    n = bk * 4 + q + 1
                    f_dn.wait(dve, n)
                    xq = x1s[:, bass.ds(bk * 4 + q, 1), :].rearrange("p a n -> p (a n)")
                    dve.scalar_tensor_tensor(xq, ps[:, 4 + q % 2, :], 1.0 / WS, xq, ALU.mult, ALU.add).then_inc(f_ac.sem, 1)

            def rows(n, u, count):
                m_xt.wait(dve, n)
                dve.tensor_copy(xgt[u % 2].rearrange("p c s -> p (c s)"), ps[:, 6, 0:NC * CAP]).then_inc(m_xc.sem, 1)
                dve.wait_ge(s_g[u], count)
                m_yf.wait(dve, n - RING)
                dve.tensor_copy(wc[u][:, :], xg[u][:, bass.ds(n - 1 + D, 1)]).then_inc(m_w.sem, 1)

            def hidden(n, u):
                gu = ps[0:CAP, 7 if u % 2 == 0 else 0, :]
                m_e.wait(dve, n)
                m_ht.wait(dve, n - 1)
                dve.scalar_tensor_tensor(hh, eg, 1.0, gu[:, 0:I], ALU.add, ALU.mult).then_inc(m_t.sem, 1)
                m_t.wait(dve, n)
                dve.scalar_tensor_tensor(hh, hh, 0.5, gu[:, I:2 * I], ALU.mult, ALU.mult).then_inc(m_h.sem, 1)
                m_ht.wait(dve, n)
                dve.tensor_copy(ht[u % 2].rearrange("p c s -> p (c s)"), ps[:, 1, 0:2 * CAP]).then_inc(m_hc.sem, 1)

            rows(1, 0, 16)
            rows(2, 1, 16)

            def experts(o, last):
                for k in range(RING):
                    n = o * RING + k + 1
                    hidden(n, k)
                    if not (last and k >= RING - 2):
                        rows(n + 2, (k + 2) % RING, o * 16 + (16 if k < 2 else 32))

            with dve.Fori(0, E // RING - 1) as o:
                experts(o, False)
            experts(E // RING - 1, True)

        @block.tensor
        def _(pe):
            s_const.wait(pe, N_CONST)
            PARTS = ((0, 0), (0, 1), (1, 0))

            def product(out_, lhs, rhs, chunks):
                steps = [(c, a, z) for c in range(chunks) for a, z in PARTS]
                for k, (c, a, z) in enumerate(steps):
                    mm = pe.matmul(out_, lhs(a, c), rhs(z, c), start=(k == 0), stop=(k == len(steps) - 1))
                return mm

            link.wait(pe, 1)
            with pe.Fori(0, NT // 2) as i:
                for u in range(2):
                    m = pe.snap(i * 2 + u + 1)
                    e_xs.wait(pe, m)
                    e_x2.wait(pe, m - 2)
                    xt = ps[:, u, :].bitcast(F16)
                    for a in range(2):
                        for c in range(NC):
                            tr = pe.transpose(xt[:, (a * NC + c) * P:(a * NC + c + 1) * P],
                                              xs[:, u, a, c * P:(c + 1) * P], ident[:, :])
                    tr.then_inc(e_xt.sem, 1)
            with pe.Fori(0, NT) as j:
                e_x2.wait(pe, j + 1)
                product(ps[:, 2, bass.ds(j * E, E)], lambda a, c: x2t[:, a, c, bass.ds(j * P, P)],
                        lambda z, c: rwt[:, z, c * E:(c + 1) * E], NC)
            pe.drain().then_inc(e_r.sem, 1)
            e_m16.wait(pe, 1)
            pe.matmul(ps[:, 3, :], before[:, :], m16[:, :, :].rearrange("p j e -> p (j e)"), start=True, stop=False)
            pe.matmul(ps[:, 3, :], ones16[:, :], c16[:, :, :].rearrange("p j e -> p (j e)"), start=False,
                      stop=True).then_inc(e_pos.sem, 1)
            NA = CAP * E // 512
            for j in range(NT):
                e_oh.wait(pe, j + 1)
                flat = oneh[:, j % 2, :, :].rearrange("p s e -> p (s e)")
                for k in range(NA):
                    mm = pe.matmul(ps[0:1, 3 + k, :], tok[:, j:j + 1], flat[:, k * 512:(k + 1) * 512],
                                   start=(j == 0), stop=(j == NT - 1))
                mm.then_inc(e_a2.sem, 1)
                if j == NT - 1:
                    e_a2.wait(pe, NT)
                    pe.sem_inc(e_a.sem, 1)
            wlo.wait(pe, 3)
            with pe.Fori(0, NT // 4) as bk:
                for it in range(NI):
                    n = pe.snap(bk * NI + it + 1)
                    f_lo.wait(pe, n - 2)
                    if it == 0:
                        e_ar.wait(pe, 1)
                    for w, bank in ((SG, it % 2), (SU, 2 + it % 2)):
                        mm = product(ps[:, bank, :], lambda a, c: swt[:, w, a, c * D + it * P:c * D + (it + 1) * P],
                                     lambda z, c: x2t[:, z, c, bass.ds(bk * 512, 512)], NC)
                    mm.then_inc(f_gu.sem, 1)
                f_lo.wait(pe, bk * NI + NI)
                for q in range(4):
                    n = bk * 4 + q + 1
                    f_ac.wait(pe, n - 2)
                    product(ps[:, 4 + q % 2, :], lambda a, c: hs[:, a, c, q * P:(q + 1) * P],
                            lambda z, c: swt[:, SD, z, c * D:(c + 1) * D], NI).then_inc(f_dn.sem, 1)

            def turn_rows(n, u, count):
                pe.wait_ge(s_g[u], count)
                m_xc.wait(pe, n - 1)
                for c in range(NC):
                    tr = pe.transpose(ps[:, 6, c * CAP:(c + 1) * CAP], xg[u][:, c * P:(c + 1) * P], identf[0:CAP, 0:CAP])
                tr.then_inc(m_xt.sem, 1)

            def gate_up(n, u, count):
                pe.wait_ge(s_ring[u], count)
                m_xc.wait(pe, n)
                m_h.wait(pe, n - 2)
                for c in range(NC):
                    mm = pe.matmul(ps[0:CAP, 7 if u % 2 == 0 else 0, :], xgt[u % 2][:, c, :], wring[:, u, c * 512:(c + 1) * 512],
                                   start=(c == 0), stop=(c == NC - 1))
                mm.then_inc(m_gu.sem, 1)

            def turn_hidden(n):
                m_h.wait(pe, n)
                m_hc.wait(pe, n - 1)
                for c in range(2):
                    tr = pe.transpose(ps[:, 1, c * CAP:(c + 1) * CAP], hh[:, c * P:(c + 1) * P], identf[0:CAP, 0:CAP])
                tr.then_inc(m_ht.sem, 1)

            def down(n, u):
                m_hc.wait(pe, n)
                m_yf.wait(pe, n - 2)
                for c in range(2):
                    mm = pe.matmul(ps[0:CAP, 2 + u % 2, :], ht[u % 2][:, c, :], wring[:, u, 2048 + c * D:2048 + (c + 1) * D],
                                   start=(c == 0), stop=(c == 1))
                mm.then_inc(m_y.sem, 1)

            f_ac.wait(pe, NT)
            turn_rows(1, 0, 16)
            turn_rows(2, 1, 16)
            gate_up(1, 0, 16)

            def experts(o, last):
                for k in range(RING):
                    n = o * RING + k + 1
                    if not (last and k == RING - 1):
                        gate_up(n + 1, (k + 1) % RING, o * 16 + (16 if k < RING - 1 else 32))
                    turn_hidden(n)
                    if not (last and k >= RING - 2):
                        turn_rows(n + 2, (k + 2) % RING, o * 16 + (16 if k < 2 else 32))
                    down(n, k)

            with pe.Fori(0, E // RING - 1) as o:
                experts(o, False)
            experts(E // RING - 1, True)


def lay_ffn(inputs):
    f = {k[len("L0_ffn_"):]: np.asarray(v) for k, v in inputs.items() if k.startswith("L0_ffn_")}

    def chunks(w):
        k, n = w.shape
        return w.reshape(k // P, P, n).transpose(1, 0, 2).reshape(P, -1)
    w3 = np.stack([chunks(f["shared_gate"].T), chunks(f["shared_up"].T), chunks(f["shared_down"].T)])
    gu = np.concatenate([f["W_gate"], f["W_up"]], axis=2).reshape(E, NC, P, 2 * I).transpose(0, 2, 1, 3).reshape(E, P, -1)
    dn = f["W_down"].reshape(E, 2, P, D).transpose(0, 2, 1, 3).reshape(E, P, -1)
    return {"rw": chunks(f["router_w"].T), "ebias": f["e_bias"], "w3": w3, "wx": np.concatenate([gu, dn], axis=2)}


def build(nc, d, out):
    x1_dram = nc.dram_tensor("x1", (T, D), F32).ap()
    table = nc.dram_tensor("table", (T + DUMMY, TROW), F32).ap()
    arow = nc.dram_tensor("arow", (1, CAP * E), F32).ap()
    attention_program(nc, d, x1_dram)
    ffn_program(nc, d, x1_dram, table, arow, out)


def kernel(**inputs):
    import concourse.bacc as bacc
    from concourse.bass_utils import run_bass_kernel_spmd

    arrays = {**lay_attention(inputs), **lay_ffn(inputs)}
    arrays = {f"in_{n}": np.ascontiguousarray(a) for n, a in arrays.items()}
    nc = bacc.Bacc("TRN2", target_bir_lowering=False, num_devices=1)
    d = {n[3:]: nc.dram_tensor(n, a.shape, mybir.dt.from_np(a.dtype), kind="ExternalInput").ap()
         for n, a in arrays.items()}
    out = nc.dram_tensor("out", (T + DUMMY, D), F32, kind="ExternalOutput").ap()
    build(nc, d, out)
    result = run_bass_kernel_spmd(nc, [arrays], core_ids=[0]).results[0]["out"]
    return result[:T].reshape(B, L, D)
```

```python
from contextlib import ExitStack

import numpy as np

import concourse.bass as bass
from concourse import mybir

ALU = mybir.AluOpType
ACT = mybir.ActivationFunctionType
F32 = mybir.dt.float32
F16 = mybir.dt.float16
U32 = mybir.dt.uint32

P = 128
B, L, D = 4, 512, 512
T = B * L
NC = D // P
HEADS, HD = 16, 32
NG = HEADS // 4
TXT, IMG = 1344, 257
KT = 13
KPAD = KT * P
MIX = TXT // P
SPLIT = TXT - MIX * P
LAST = TXT + IMG - (KT - 1) * P
QT = L // P
POS = KT + QT
WS = 256.0
STK = 3 * HD
SHIFT = 16.0
SCALE = 1.0 / float(np.sqrt(HD))
ORDER = [KT - 2, KT - 1, MIX] + list(range(MIX))
ADDED = range(3, KT - 1)
NA = len(ADDED)
VHEADS = 3
VDMAS = (3, 1, 1, 1)
VCUTS = [(0, MIX, KT), (3, 0, 2), (5, 2, 7), (10, 7, MIX)]
SAFE = 1e20
ODD = 1e30


class Event:

    def __init__(self, ctx, nc, name, ahead=0):
        self.sem = ctx.enter_context(nc.semaphore(name))
        self.ahead = ahead

    def wait(self, eng, n):
        if not (isinstance(n, int) and n + self.ahead <= 0):
            eng.wait_ge(self.sem, n + self.ahead)


def attention_program(nc, d, x1_dram):
    with ExitStack() as ctx:
        def sb(name, shape, dt):
            return ctx.enter_context(nc.sbuf_tensor(name, shape, dt))

        def event(name, ahead=0):
            e = Event(ctx, nc, name, ahead)
            events.append(e)
            return e

        s_apart = ctx.enter_context(nc.semaphore("s_apart"))

        def apart(eng):
            eng.sem_inc(s_apart, 1)

        events = []
        wts = sb("wts", [P, 6, 2, NC * D], F16)
        WQ, WK, WV, WKI, WVI, WO = range(6)
        vec = sb("vec", [P, 9, D], F32)
        KB, KW, VB = 0, 2, 4
        QB, QW, OB = 6, 7, 8
        keys = sb("keys", [P, HEADS, KPAD], F16)
        vals = sb("vals", [P, KT, D], F32)
        quer = sb("quer", [P, HEADS, L], F16)
        vgrp = sb("vgrp", [P, KT + 1, P], F32)
        attn = sb("attn", [P, NG, 2, L], F16)
        work = sb("work", [P, 16 * D], F32)
        ident = sb("ident", [P, P], F16)
        ones = sb("ones", [P, 3, HD], F32)
        small = sb("small", [P, 24], F32)
        flag = sb("flag", [1, 1], mybir.dt.int32)
        ps = ctx.enter_context(nc.psum_tensor("ps", [P, 8, 512], F32))

        raw = [work[:, i * D:(i + 1) * D] for i in range(2)]
        hl = [work[:, (2 + i) * D:(3 + i) * D].bitcast(F16).rearrange("p (s n) -> p s n", s=2) for i in range(2)]
        kraw = work[:, 4 * D:5 * D]
        knorm = work[:, 5 * D:6 * D]
        xraw = work[:, 11 * D:15 * D].rearrange("p (j n) -> p j n", j=QT)
        xnorm = work[:, 6 * D:7 * D]
        xs = work[:, 7 * D:8 * D].bitcast(F16).rearrange("p (s n) -> p s n", s=2)
        stw = HEADS * STK // 2
        stack = [work[:, 8 * D + i * stw:8 * D + (i + 1) * stw].bitcast(F16).rearrange("p (h r) -> p h r", h=HEADS)
                 for i in range(2)]
        prob = work[:, 0:8 * D].rearrange("p (s h q) -> p s h q", s=2, h=4)
        rden_t, rden_i = work[:, 8 * D:9 * D], work[:, 9 * D:10 * D]
        added = work[:, 10 * D:14 * D].rearrange("p (h q) -> p h q", h=4)
        odds = work[:, 14 * D:15 * D]
        xt = attn[:, :, :, :].rearrange("p j s q -> p j (s q)")
        attn32 = attn[:, :, :, :].rearrange("p g s q -> p (g s q)").bitcast(F32).rearrange("p (g q) -> p g q", g=NG)
        mx = work[:, 0:P].rearrange("p (h t s) -> p h t s", h=HEADS, t=QT)
        mh = work[:, D:D + (STK + P) // 2].bitcast(F16)
        xres = [work[:, (4 + j) * D:(5 + j) * D] for j in range(QT)]
        proj = work[:, 15 * D:16 * D]
        quer32 = quer[:, :, :].rearrange("p h q -> p (h q)").bitcast(F32)
        wstage = [work[:, i * 4 * D:(i + 1) * 4 * D] for i in range(4)] + [quer32[:, i * 4 * D:(i + 1) * 4 * D] for i in range(2)]
        ssq, rin, rtmp, st6, mv, rs, rs2 = (small[:, 0:1], small[:, 1:2], small[:, 2:3], small[:, 4:10],
                                            small[:, 10:12], small[:, 12:13], small[:, 13:14])
        mhalf = small[:, 14:15]
        total = small[:, 15:16]

        turned = ps[:, 4:6, :].rearrange("p a n -> p (a n)").bitcast(F16).rearrange("p (h k) -> p h k", h=HEADS)
        xturned = ps[:, 6, :].bitcast(F16)
        NUM_T, DEN_T, NUM_I, DEN_I = 4, 5, 6, 7
        CHECKS = 6 * NG

        s_w = [ctx.enter_context(nc.semaphore(f"s_w{i}")) for i in range(6)]
        s_ct = ctx.enter_context(nc.semaphore("s_ct"))
        s_c = ctx.enter_context(nc.semaphore("s_c"))
        s_in = [ctx.enter_context(nc.semaphore(f"s_in{i}")) for i in range(2)]
        s_x = [ctx.enter_context(nc.semaphore(f"s_x{i}")) for i in range(QT)]
        s_vg = [ctx.enter_context(nc.semaphore(f"s_vg{i}")) for i in range(len(VCUTS))]
        s_xr = ctx.enter_context(nc.semaphore("s_xr"))
        s_st = ctx.enter_context(nc.semaphore("s_st"))
        s_i0 = event("s_i0")
        s_const = event("s_const")
        whi, wlo = event("whi"), event("wlo")
        e_hi = event("e_hi")
        e_hl = event("e_hl")
        e_pv = event("e_pv", 2)
        e_pk = event("e_pk", 2)
        e_kr = event("e_kr")
        e_ssq = event("e_ssq")
        e_rt = event("e_rt")
        e_rin = event("e_rin")
        e_kn = event("e_kn")
        e_c0 = event("e_c0")
        e_c1 = event("e_c1", 1)
        e_lo = event("e_lo")
        e_t = event("e_t", 2)
        e_td = event("e_td", 1)
        e_ta = event("e_ta", 1)
        e_v = event("e_v", 2)
        e_st = event("e_st")
        e_mv = event("e_mv")
        e_rv = event("e_rv")
        e_rs = event("e_rs")
        e_xn = event("e_xn")
        e_xh = event("e_xh")
        e_xs = event("e_xs", 1)
        e_xt = event("e_xt", 1)
        e_xc = event("e_xc", 1)
        e_ms = event("e_ms")
        e_mt, e_mi = event("e_mt"), event("e_mi", 2)
        e_mh = event("e_mh")
        e_mr = event("e_mr")
        e_mc = event("e_mc")
        e_qz = event("e_qz")
        e_s = event("e_s")
        e_e = event("e_e", 2)
        e_ad = event("e_ad", 1)
        e_ap = event("e_ap", 1)
        e_av = event("e_av", KT)
        e_ds = event("e_ds", 1)
        e_ri = event("e_ri")
        e_oi = event("e_oi", 1)
        e_rt2 = event("e_rt2")
        e_ot = event("e_ot", 1)
        e_os = event("e_os")
        e_oh = event("e_oh")
        e_at = event("e_at", 1)
        e_ck = event("e_ck", 4)
        e_fz = event("e_fz")
        e_fm = event("e_fm")
        e_fs = event("e_fs")
        e_fl = event("e_fl")
        e_po = event("e_po", 1)
        e_ob = event("e_ob", 1)
        e_x1 = event("e_x1", 2)
        e_b = event("e_b", 1)

        block = ctx.enter_context(nc.Block())

        def kind(pos):
            return 0 if pos < MIX else 1 if pos == MIX else 2

        def is_q(pos):
            return pos >= KT

        def parts(n):
            t = ORDER[n]
            uses = {KT - 1: [(LAST, t, 0, True)], MIX: [(P, KT, 2, True), (P, t, 1, False)]}.get(t, [(P, t, 0, t > MIX)])
            return [(rows, vt, o, img, n == 0 if img else t == MIX, t == MIX if img else n == KT - 1)
                    for rows, vt, o, img in uses]

        def again(eng, b):
            e_fl.wait(eng, b + 1)
            apart(eng)
            return eng.If(eng.value_load(flag[0:1, 0:1], min_val=0, max_val=1) > 0)

        def otherwise(eng, counts):
            with eng.Else():
                for e, n in counts:
                    eng.sem_inc(e.sem if isinstance(e, Event) else e, n)
            eng.end_ifs()

        def slots(b, pos):
            return (b * ((KT + 1) // 2) if pos % 2 == 0 else b * (KT // 2)) + pos // 2 + 1

        PAIRS = 4

        @block.sync
        def _(sp):
            for e in events:
                if e.ahead:
                    sp.sem_inc(e.sem, e.ahead)
            for i in range(6):
                sp.dma_start(wstage[i], d["w6"][i]).then_inc(s_w[i], 16)
            def load(b, pos):
                src = d["ctx"][bass.ds(b * KT + pos, 1)].rearrange("a p n -> (a p) n")
                sp.dma_start(raw[pos % 2], src).then_inc(s_in[pos % 2], 16)

            def first_loads(b):
                load(b, 0)
                load(b, 1)
                sp.dma_start(xraw, d["x"][bass.ds(b * L, L), :].rearrange("(j p) n -> p j n", p=P)).then_inc(s_xr, 16)

            for k, n in ((KB, "kb"), (KW, "kw"), (VB, "vb")):
                sp.dma_start(vec[:, k, :], d[n].partition_broadcast(P)).then_inc(s_ct, 16)
            wlo.wait(sp, 4)
            first_loads(0)
            for k, n in ((KB, "kib"), (KW, "kiw"), (VB, "vib")):
                sp.dma_start(vec[:, k + 1, :], d[n].partition_broadcast(P)).then_inc(s_c, 16)
            for k, n in ((QB, "qb"), (QW, "qw"), (OB, "ob")):
                sp.dma_start(vec[:, k, :], d[n].partition_broadcast(P)).then_inc(s_c, 16)
            for h in range(HEADS):
                sp.dma_start(keys[STK:P, h, :], d["mark"]).then_inc(s_c, 16)
            with sp.Fori(0, B) as b:
                with sp.Fori(0, PAIRS) as i:
                    for u in range(2):
                        e_hl.wait(sp, b * KT + i * 2 + u + 1)
                        src = d["ctx"][bass.ds(b * KT + i * 2 + u + 2, 1)].rearrange("a p n -> (a p) n")
                        sp.dma_start(raw[u], src).then_inc(s_in[u], 16)
                for pos in range(2 * PAIRS, KT - 2):
                    e_hl.wait(sp, b * KT + pos + 1)
                    load(b, pos + 2)

                def values(p):
                    with sp.Fori(0, NG) as g:
                        for (n, a, z), s in zip(VCUTS, s_vg):
                            e_av.wait(sp, ((2 * b + p) * NG + g) * KT + n + z - a - KT)
                            if z == KT:
                                sp.dma_start(vgrp[0:SPLIT, MIX, :], vals[0:SPLIT, MIX, bass.ds(g * P, P)]).then_inc(s, 16)
                                sp.dma_start(vgrp[SPLIT:P, KT, :], vals[SPLIT:P, MIX, bass.ds(g * P, P)]).then_inc(s, 16)
                                a = MIX + 1
                            sp.dma_start(vgrp[:, a:z, :], vals[:, a:z, bass.ds(g * P, P)]).then_inc(s, 16)

                e_v.wait(sp, b * KT + KT)
                apart(sp)
                values(0)
                with again(sp, b):
                    values(1)
                otherwise(sp, [(s, 16 * NG * k) for s, k in zip(s_vg, VDMAS)])
                e_at.wait(sp, (2 * b + 2) * NG)
                for j in range(QT):
                    sp.dma_start(xres[j], d["x"][bass.ds(b * L + j * P, P), :]).then_inc(s_x[j], 16)
                with sp.If(b < B - 1):
                    first_loads((b + 1).with_bounds(min_val=1, max_val=B - 1))
                sp.end_ifs()
                for j in range(QT):
                    e_x1.wait(sp, b * QT + j + 1)
                    sp.dma_start(x1_dram[bass.ds(b * L + j * P, P), :], xres[j]).then_inc(s_st, 16)
                sp.wait_ge(s_st, (b + 1) * 16 * QT)
                sp.sem_inc(e_b.sem, 1)

        @block.gpsimd
        def _(pool):
            pool.memset(ident[:, :], 0.0).then_inc(s_i0.sem, 1)
            s_i0.wait(pool, 2)
            pool.affine_select(out=ident[:, :], in_=ident[:, :], pattern=[[-1, P]], compare_op=ALU.not_equal, fill=1.0,
                               base=0, channel_multiplier=1).then_inc(s_const.sem, 1)
            pool.memset(mhalf, -0.5).then_inc(s_const.sem, 1)
            s_const.wait(pool, 8)

            def rinv(n):
                e_ssq.wait(pool, n)
                apart(pool)
                pool.tensor_scalar(rtmp, ssq, 1.0 / D, 1e-6, ALU.mult, ALU.add).then_inc(e_rt.sem, 1)
                e_rt.wait(pool, n)
                pool.tensor_tensor(rin, rtmp, mhalf, ALU.pow).then_inc(e_rin.sem, 1)

            def rstd(m):
                e_mv.wait(pool, m)
                apart(pool)
                pool.tensor_scalar(rs2, mv[:, 1:2], 1.0, 1e-5, ALU.mult, ALU.add).then_inc(e_rv.sem, 1)
                e_rv.wait(pool, m)
                pool.tensor_tensor(rs, rs2, mhalf, ALU.pow).then_inc(e_rs.sem, 1)

            with pool.Fori(0, B) as b:
                rinv(b * POS + 1)
                with pool.Fori(0, PAIRS) as i:
                    rstd(b * QT + i + 1)
                    rinv(b * POS + i * 2 + 2)
                    rinv(b * POS + i * 2 + 3)
                with pool.Fori(2 * PAIRS + 1, POS) as i:
                    rinv(b * POS + i + 1)
                pool.memset(odds, 0.0).then_inc(e_fz.sem, 1)
                e_fz.wait(pool, b + 1)
                def bounds(g, text):
                    k = b * CHECKS + g * 6 + 3 * text
                    rden, read = (rden_t, e_ot) if text else (rden_i, e_oi)
                    read.wait(pool, 2 * b * NG + g + 1)
                    apart(pool)
                    pool.tensor_tensor(odds, odds, rden, ALU.add).then_inc(e_ck.sem, 1)
                    yield
                    e_ck.wait(pool, k + 1)
                    apart(pool)
                    pool.tensor_scalar(rden, rden, 1.0 / SAFE, ODD, ALU.is_lt, ALU.mult).then_inc(e_ck.sem, 1)
                    yield
                    e_ck.wait(pool, k + 2)
                    apart(pool)
                    pool.tensor_tensor(odds, odds, rden, ALU.add).then_inc(e_ck.sem, 1)
                    e_ck.wait(pool, k + 3)
                    yield

                def adding(p, g, check):
                    gg = pool.snap((2 * b + p) * NG + g)
                    sm = added[:, VHEADS:, :].rearrange("p h q -> p (h q)")
                    if check:
                        for _ in bounds(g - 1, 0):
                            pass
                        text = bounds(g - 1, 1)
                    e_ds.wait(pool, gg)
                    for k, n in enumerate(ADDED):
                        e_e.wait(pool, gg * 2 * KT + 2 * n + 2)
                        pr = prob[:, n % 2, VHEADS:, :].rearrange("p h q -> p (h q)")
                        if k == 0:
                            apart(pool)
                            ins = pool.tensor_copy(sm, pr)
                        else:
                            e_ap.wait(pool, gg * NA + k)
                            ins = pool.tensor_tensor(sm, sm, pr, ALU.add)
                        ins.then_inc(e_ap.sem, 1)
                        if check and k % 2 == 0 and k < 6:
                            next(text)

                adding(0, 0, False)
                with pool.Fori(1, NG) as g:
                    adding(0, g, True)
                for _ in bounds(NG - 1, 0):
                    pass
                with again(pool, b):
                    with pool.Fori(0, NG) as g:
                        adding(1, g, False)
                otherwise(pool, ((e_ap, NG * NA),))

        @block.scalar
        def _(act):
            for i in range(6):
                act.wait_ge(s_w[i], 16)
                act.activation(wts[:, i, 0, :], wstage[i], ACT.Copy, scale=WS).then_inc(whi.sem, 1)

            def high(n, pos, b):
                act.wait_ge(s_in[pos % 2], 16 * slots(b, pos))
                e_pk.wait(act, n - 2)
                act.copy(hl[pos % 2][:, 0, :], raw[pos % 2]).then_inc(e_hi.sem, 1)

            def store_turned(n, tile, q):
                e_t.wait(act, n)
                dst = quer if q else keys
                act.copy(dst[0:STK, 0:8, bass.ds(tile * P, P)], turned[0:STK, 0:8, :]).then_inc(e_ta.sem, 1)

            def turn(n, pos, b, tile, prev):
                if pos + 1 < KT:
                    high(n + 1, pos + 1, b)
                e_kr.wait(act, n)
                act.activation(ps[:, 7, :], kraw, ACT.Square, accum_out=ssq).then_inc(e_ssq.sem, 1)
                if prev is not None:
                    store_turned(n - 1, *prev)
                e_kn.wait(act, n)
                e_t.wait(act, n - 2)
                st = stack[pos % 2]
                kn = knorm.rearrange("p (h d) -> p h d", h=HEADS)
                second = 2 if is_q(pos) else 1
                act.copy(st[:, :, 0:HD], kn).then_inc(e_c0.sem, 1)
                act.copy(st[:, :, second * HD:(second + 1) * HD], kn).then_inc(e_c1.sem, 1)

            with act.Fori(0, B) as b:
                act.wait_ge(s_in[0], 16 * slots(b, 0))
                e_pk.wait(act, b * POS - 1)
                act.copy(hl[0][:, 0, :], raw[0]).then_inc(e_hi.sem, 1)
                turn(b * POS + 1, 0, b, 0, None)
                with act.Fori(0, PAIRS) as i:
                    for u in range(2):
                        n = act.snap(b * POS + i * 2 + u + 2)
                        s = (u + 2) % 2
                        act.wait_ge(s_in[s], 16 * (slots(b, s) + i + (1 if u == 0 else 1)))
                        e_pk.wait(act, n - 1)
                        act.copy(hl[s][:, 0, :], raw[s]).then_inc(e_hi.sem, 1)
                        e_kr.wait(act, n)
                        act.activation(ps[:, 7, :], kraw, ACT.Square, accum_out=ssq).then_inc(e_ssq.sem, 1)
                        if u == 0:
                            e_xn.wait(act, b * QT + i + 1)
                            e_xt.wait(act, b * QT + i)
                            act.copy(xs[:, 0, :], xnorm).then_inc(e_xh.sem, 1)
                        store_turned(n - 1, i * 2 + u, False)
                        e_kn.wait(act, n)
                        e_t.wait(act, n - 2)
                        kn = knorm.rearrange("p (h d) -> p h d", h=HEADS)
                        act.copy(stack[1 - u][:, :, 0:HD], kn).then_inc(e_c0.sem, 1)
                        act.copy(stack[1 - u][:, :, HD:2 * HD], kn).then_inc(e_c1.sem, 1)
                for pos in range(2 * PAIRS + 1, POS):
                    q = pos - 1 >= KT
                    turn(b * POS + pos + 1, pos, b, None, (pos - 1 - KT if q else pos - 1, q))
                store_turned(b * POS + POS, QT - 1, True)

                def exponentials(p):
                    with act.Fori(0, NG) as g:
                        gg = act.snap((2 * b + p) * NG + g)
                        for n, t in enumerate(ORDER):
                            rows = LAST if t == KT - 1 else P
                            for half in range(2):
                                e_s.wait(act, gg * 2 * KT + 2 * n + half + 1)
                                if half == 0:
                                    e_av.wait(act, gg * KT + n - (1 if n else 0))
                                    for e in (e_ad, e_ap):
                                        if n == 0:
                                            e.wait(act, gg * NA)
                                        elif n - 2 in ADDED:
                                            e.wait(act, gg * NA + n - 1 - ADDED[0])
                                act.activation(prob[0:rows, n % 2, 2 * half:2 * half + 2, :],
                                               ps[0:rows, 2 * half:2 * half + 2, :], ACT.Exp,
                                               scale=SCALE).then_inc(e_e.sem, 1)

                exponentials(0)
                with again(act, b):
                    exponentials(1)
                otherwise(act, ((e_e, 2 * KT * NG),))

        @block.vector
        def _(dve):
            dve.memset(ones[:, :, :], 0.0).then_inc(s_i0.sem, 1)
            s_i0.wait(dve, 2)
            dve.memset(ones[:, 0, :], 1.0).then_inc(s_const.sem, 1)
            dve.memset(ones[0:SPLIT, 1, :], 1.0).then_inc(s_const.sem, 1)
            dve.memset(ones[SPLIT:P, 2, :], 1.0).then_inc(s_const.sem, 1)
            dve.memset(vgrp[SPLIT:P, MIX, :], 0.0).then_inc(s_const.sem, 1)
            dve.memset(vgrp[0:SPLIT, KT, :], 0.0).then_inc(s_const.sem, 1)
            for i in range(6):
                whi.wait(dve, i + 1)
                dve.scalar_tensor_tensor(wts[:, i, 1, :], wstage[i], WS, wts[:, i, 0, :], ALU.mult,
                                         ALU.subtract).then_inc(wlo.sem, 1)
            wlo.wait(dve, 6)
            dve.memset(quer[STK:P, :, :], 0.0).then_inc(s_const.sem, 1)
            def low(s, n):
                e_hi.wait(dve, n)
                dve.tensor_tensor(hl[s][:, 1, :], raw[s], hl[s][:, 0, :], ALU.subtract).then_inc(e_hl.sem, 1)

            def stats(m, i):
                dve.bn_stats(st6, xraw[:, bass.ds(i, 1), :].rearrange("p a n -> p (a n)")).then_inc(e_st.sem, 1)
                e_st.wait(dve, m)
                apart(dve)
                dve.bn_aggr(mv, st6).then_inc(e_mv.sem, 1)

            def norm_x(m, i):
                e_rs.wait(dve, m)
                e_xs.wait(dve, m - 1)
                dve.tensor_scalar(xnorm, xraw[:, bass.ds(i, 1), :].rearrange("p a n -> p (a n)"), mv[:, 0:1], rs,
                                  ALU.subtract, ALU.mult).then_inc(e_xn.sem, 1)

            def low_x(m):
                e_xh.wait(dve, m)
                dve.tensor_tensor(xs[:, 1, :], xnorm, xs[:, 0, :], ALU.subtract).then_inc(e_xs.sem, 1)

            def tile(n, s, ranges, value, prep, prev, after):
                prep()
                e_pk.wait(dve, n)
                for a, z, bias, _, _ in ranges:
                    ins = dve.scalar_tensor_tensor(kraw[a:z, :], ps[a:z, s, :], 1.0 / WS, vec[a:z, bias, :], ALU.mult,
                                                   ALU.add)
                ins.then_inc(e_kr.sem, 1)
                if value is not None:
                    for a, z, _, _, vb in ranges:
                        ins = dve.scalar_tensor_tensor(
                            vals[a:z, bass.ds(value, 1), :].rearrange("p a n -> p (a n)"), ps[a:z, 2 + s, :],
                            1.0 / WS, vec[a:z, vb, :], ALU.mult, ALU.add)
                    ins.then_inc(e_v.sem, 1)
                after()
                if prev is not None:
                    store_turned(n - 1, *prev)
                e_rin.wait(dve, n)
                e_c1.wait(dve, n - 1)
                for a, z, _, weight, _ in ranges:
                    ins = dve.scalar_tensor_tensor(knorm[a:z, :], kraw[a:z, :], rin[a:z, :], vec[a:z, weight, :],
                                                   ALU.mult, ALU.mult)
                ins.then_inc(e_kn.sem, 1)
                e_c0.wait(dve, n)
                st = stack[s]
                kn = knorm.rearrange("p (h d) -> p h d", h=HEADS)
                third = 1 if value is None else 2
                dve.tensor_tensor(st[:, :, third * HD:(third + 1) * HD], kn, st[:, :, 0:HD],
                                  ALU.subtract).then_inc(e_lo.sem, 1)

            def store_turned(n, tile, q):
                e_t.wait(dve, n)
                dst = quer if q else keys
                dve.tensor_copy(dst[0:STK, 8:16, bass.ds(tile * P, P)], turned[0:STK, 8:16, :]).then_inc(e_td.sem, 1)

            def nothing():
                pass

            TEXT = [(0, P, KB, KW, VB)]
            IMAGE = [(0, P, KB + 1, KW + 1, VB + 1)]
            MIXED = [(0, SPLIT, KB, KW, VB), (SPLIT, P, KB + 1, KW + 1, VB + 1)]
            QUERY = [(0, P, QB, QW, None)]

            with dve.Fori(0, B) as b:
                e_ds.wait(dve, 2 * b * NG)
                low(0, b * KT + 1)
                dve.wait_ge(s_ct, 16 * 3)
                e_b.wait(dve, b)
                tile(b * POS + 1, 0, TEXT, 0, lambda: low(1, b * KT + 2), None, nothing)
                dve.wait_ge(s_xr, 16 * b + 16)
                e_po.wait(dve, b * QT)
                apart(dve)
                with dve.Fori(0, PAIRS) as i:
                    for u in range(2):
                        n = dve.snap(b * POS + i * 2 + u + 2)
                        m = dve.snap(b * QT + i + 1)

                        def prep():
                            low(u, b * KT + i * 2 + u + 3)
                            if u == 0:
                                stats(m, i)
                            else:
                                low_x(m)
                        tile(n, 1 - u, TEXT, i * 2 + u + 1, prep, (i * 2 + u, False),
                             (lambda: norm_x(m, i)) if u == 0 else nothing)
                    e_xt.wait(dve, m)
                    dve.tensor_copy(xt[:, bass.ds(i, 1), :].rearrange("p a n -> p (a n)"), xturned).then_inc(e_xc.sem, 1)
                for pos in range(2 * PAIRS + 1, POS):
                    n = dve.snap(b * POS + pos + 1)
                    prep = nothing
                    if pos + 1 < KT:
                        prep = lambda: low((pos + 1) % 2, b * KT + pos + 2)
                    q = pos - 1 >= KT
                    prev = (pos - 1 - KT if q else pos - 1, q)
                    if pos == MIX:
                        dve.wait_ge(s_c, 16 * (3 + 3 + HEADS))
                    ranges = QUERY if is_q(pos) else (TEXT, MIXED, IMAGE)[kind(pos)]
                    tile(n, pos % 2, ranges, None if is_q(pos) else pos, prep, prev, nothing)
                store_turned(b * POS + POS, QT - 1, True)

                def group(p, g, last):
                    gg = dve.snap((2 * b + p) * NG + g + 1)
                    pr = lambda n: prob[:, n % 2, 0:VHEADS, :].rearrange("p h q -> p (h q)")
                    sm = added[:, 0:VHEADS, :].rearrange("p h q -> p (h q)")
                    e_ds.wait(dve, gg - 1)
                    for k, n in enumerate(ADDED):
                        e_e.wait(dve, (gg - 1) * 2 * KT + 2 * n + 2)
                        if k == 0:
                            ins = dve.tensor_copy(sm, pr(n))
                        else:
                            e_ad.wait(dve, (gg - 1) * NA + k)
                            ins = dve.tensor_tensor(sm, sm, pr(n), ALU.add)
                        ins.then_inc(e_ad.sem, 1)
                    oimg = attn32[:, bass.ds(g, 1), :].rearrange("p a n -> p (a n)")
                    part = lambda k: attn[:, bass.ds(g, 1), k, :].rearrange("p a n -> p (a n)")
                    if p == 0:
                        e_ck.wait(dve, b * CHECKS + g * 6 - 3)
                    dve.reciprocal(rden_i, ps[:, DEN_I, :]).then_inc(e_ri.sem, 1)
                    e_ri.wait(dve, gg)
                    dve.tensor_tensor(oimg, ps[:, NUM_I, :], rden_i, ALU.mult).then_inc(e_oi.sem, 1)
                    e_ds.wait(dve, gg)
                    e_oi.wait(dve, gg)
                    if p == 0:
                        e_ck.wait(dve, b * CHECKS + g * 6)
                    dve.reciprocal(rden_t, ps[:, DEN_T, :]).then_inc(e_rt2.sem, 1)
                    e_rt2.wait(dve, gg)
                    e_at.wait(dve, gg - 1)
                    dve.tensor_tensor(proj, ps[:, NUM_T, :], rden_t, ALU.mult).then_inc(e_ot.sem, 1)
                    e_ot.wait(dve, gg)
                    if last and p == 0:
                        k = b * CHECKS + CHECKS - 3
                        e_ck.wait(dve, k)
                        dve.tensor_tensor(odds, odds, rden_t, ALU.add).then_inc(e_ck.sem, 1)
                        e_ck.wait(dve, k + 1)
                        dve.tensor_scalar(rden_t, rden_t, 1.0 / SAFE, ODD, ALU.is_lt, ALU.mult).then_inc(e_ck.sem, 1)
                        e_ck.wait(dve, k + 2)
                        dve.tensor_tensor(odds, odds, rden_t, ALU.add).then_inc(e_ck.sem, 1)
                        e_ck.wait(dve, k + 3)
                        dve.tensor_reduce(total, odds, mybir.AxisListType.X, ALU.add).then_inc(e_fm.sem, 1)
                    dve.tensor_tensor(proj, proj, oimg, ALU.add).then_inc(e_os.sem, 1)
                    e_os.wait(dve, gg)
                    dve.tensor_copy(part(0), proj).then_inc(e_oh.sem, 1)
                    e_oh.wait(dve, gg)
                    dve.tensor_tensor(part(1), proj, part(0), ALU.subtract).then_inc(e_at.sem, 1)

                def results(p):
                    with dve.Fori(0, NG - 1) as g:
                        group(p, g, False)
                    group(p, NG - 1, True)

                def maxima():
                    with dve.Fori(0, HEADS) as h:
                        for t in range(QT):
                            k = dve.snap(b * HEADS * QT + h * QT + t + 1)
                            bank = 4 * (t % 2)
                            e_ms.wait(dve, k)
                            for kd, (a, z, e) in enumerate(((0, TXT, e_mt), (1536, 1536 + IMG, e_mi))):
                                dve.tensor_reduce(mx[:, bass.ds(h, 1), t, kd],
                                                  ps[:, bank:bank + 4, :].rearrange("p a n -> p (a n)")[:, a:z],
                                                  mybir.AxisListType.X, ALU.max).then_inc(e.sem, 1)
                    e_mt.wait(dve, b * HEADS * QT + HEADS * QT)
                    e_mi.wait(dve, b * HEADS * QT + HEADS * QT)
                    dve.memset(mh[:, 0:STK], 0.0).then_inc(e_mh.sem, 1)
                    dve.tensor_scalar(mh[:, STK:], mx.rearrange("p h t s -> p (h t s)"), -1.0 / SHIFT, None,
                                      ALU.mult).then_inc(e_mh.sem, 1)
                    e_mr.wait(dve, b + 1)
                    dve.tensor_copy(quer[STK:STK + 2, :, :].rearrange("p h q -> p (h q)"),
                                    ps[STK:STK + 2, :, :].rearrange("p a n -> p (a n)").bitcast(F16)).then_inc(e_mc.sem, 1)

                results(0)
                e_fs.wait(dve, b + 1)
                dve.tensor_scalar(flag[:, :], ps[0:1, NUM_I, 0:1], SAFE, 0.0, ALU.is_le, ALU.is_equal).then_inc(e_fl.sem, 1)
                with again(dve, b):
                    maxima()
                    results(1)
                    dve.memset(quer[STK:STK + 2, :, :], 0.0).then_inc(e_qz.sem, 1)
                otherwise(dve, ((e_mt, HEADS * QT), (e_mi, HEADS * QT), (e_mh, 2), (e_mc, 1), (e_ad, NA * NG),
                                (e_ri, NG), (e_oi, NG), (e_rt2, NG), (e_ot, NG), (e_os, NG), (e_oh, NG), (e_at, NG),
                                (e_qz, 1)))
                for j in range(QT):
                    m = b * QT + j + 1
                    e_po.wait(dve, m)
                    e_x1.wait(dve, m - 1)
                    dve.scalar_tensor_tensor(proj, ps[:, j, :], 1.0 / WS, vec[:, OB, :], ALU.mult,
                                             ALU.add).then_inc(e_ob.sem, 1)
                    e_ob.wait(dve, m)
                    dve.wait_ge(s_x[j], 16 * (b + 1))
                    dve.tensor_tensor(xres[j], xres[j], proj, ALU.add).then_inc(e_x1.sem, 1)

        @block.tensor
        def _(pe):
            s_const.wait(pe, 8)
            wlo.wait(pe, 6)

            def product(out, lhs, w, cols=slice(0, P)):
                steps = [(c, a, z) for c in range(NC) for a, z in ((0, 0), (0, 1), (1, 0))]
                for k, (c, a, z) in enumerate(steps):
                    mm = pe.matmul(out, lhs(a, c)[:, cols], wts[:, w, z, c * D:(c + 1) * D],
                                   start=(k == 0), stop=(k == len(steps) - 1))
                return mm

            def project(n, s, pos, hn=None):
                if is_q(pos):
                    lhs = lambda a, c: attn[:, pos - KT, a, c * P:(c + 1) * P]
                    product(ps[:, s, :], lhs, WQ).then_inc(e_pk.sem, 1)
                    return
                e_hl.wait(pe, hn)
                lhs = lambda a, c: hl[s][:, a, c * P:(c + 1) * P]
                if kind(pos) == 1:
                    lo, hi = slice(0, SPLIT), slice(SPLIT, P)
                    product(ps[0:SPLIT, 2 + s, :], lhs, WV, lo)
                    product(ps[SPLIT:P, 2 + s, :], lhs, WVI, hi).then_inc(e_pv.sem, 1)
                    product(ps[0:SPLIT, s, :], lhs, WK, lo)
                    product(ps[SPLIT:P, s, :], lhs, WKI, hi).then_inc(e_pk.sem, 1)
                else:
                    txt = kind(pos) == 0
                    product(ps[:, 2 + s, :], lhs, WV if txt else WVI).then_inc(e_pv.sem, 1)
                    product(ps[:, s, :], lhs, WK if txt else WKI).then_inc(e_pk.sem, 1)

            def turn_stacks(n, s):
                e_lo.wait(pe, n)
                e_c1.wait(pe, n)
                e_td.wait(pe, n - 1)
                e_ta.wait(pe, n - 1)
                for h in range(HEADS):
                    tr = pe.transpose(turned[0:STK, h, :], stack[s][:, h, :], ident[:, :])
                tr.then_inc(e_t.sem, 1)

            def turn_x(m):
                e_xs.wait(pe, m)
                e_xc.wait(pe, m - 1)
                for a in range(2):
                    for c in range(NC):
                        tr = pe.transpose(xturned[:, (a * NC + c) * P:(a * NC + c + 1) * P],
                                          xs[:, a, c * P:(c + 1) * P], ident[:, :])
                tr.then_inc(e_xt.sem, 1)

            with pe.Fori(0, B) as b:
                e_ot.wait(pe, 2 * b * NG)
                e_ob.wait(pe, b * QT)
                project(b * POS + 1, 0, 0, b * KT + 1)
                with pe.Fori(0, PAIRS) as i:
                    for u in range(2):
                        n = pe.snap(b * POS + i * 2 + u + 2)
                        project(n, 1 - u, 0, b * KT + i * 2 + u + 2)
                        if u == 1:
                            turn_x(b * QT + i + 1)
                        turn_stacks(n - 1, u)
                for pos in range(2 * PAIRS + 1, POS):
                    n = pe.snap(b * POS + pos + 1)
                    if pos == KT:
                        e_xc.wait(pe, b * QT + QT)
                    project(n, pos % 2, pos, b * KT + pos + 1)
                    turn_stacks(n - 1, (pos - 1) % 2)
                turn_stacks(b * POS + POS, (POS - 1) % 2)
                e_td.wait(pe, b * POS + POS)
                e_ta.wait(pe, b * POS + POS)
                apart(pe)

                def score_maxima():
                    with pe.Fori(0, HEADS) as h:
                        for t in range(QT):
                            k = pe.snap(b * HEADS * QT + h * QT + t + 1)
                            bank = 4 * (t % 2)
                            e_mi.wait(pe, k - 2)
                            for c, (a, z) in enumerate(((0, 512), (512, 1024), (1024, TXT), (TXT, TXT + IMG))):
                                mm = pe.matmul(ps[:, bank + c, 0:z - a],
                                               quer[0:STK, bass.ds(h, 1), t * P:(t + 1) * P].rearrange("p a n -> p (a n)"),
                                               keys[0:STK, bass.ds(h, 1), a:z].rearrange("p a n -> p (a n)"),
                                               start=True, stop=True)
                            mm.then_inc(e_ms.sem, 1)
                    e_mh.wait(pe, 2 * b + 2)
                    turned_mx = ps[:, :, :].rearrange("p a n -> p (a n)").bitcast(F16)
                    for k in range(HEADS * QT):
                        tr = pe.transpose(turned_mx[0:STK + 2, k * P:(k + 1) * P], mh[:, 2 * k:2 * k + STK + 2], ident[:, :])
                    tr.then_inc(e_mr.sem, 1)
                    e_mc.wait(pe, b + 1)
                    apart(pe)

                def attention(p):
                    def scores(g, n, half):
                        t = ORDER[n]
                        rows = LAST if t == KT - 1 else P
                        e_e.wait(pe, ((2 * b + p) * NG + g) * 2 * KT + 2 * n + half - 1)
                        for h in range(2 * half, 2 * half + 2):
                            mm = pe.matmul(ps[0:rows, h, :],
                                           keys[:, bass.ds(g * 4 + h, 1), t * P:t * P + rows].rearrange("p a n -> p (a n)"),
                                           quer[:, bass.ds(g * 4 + h, 1), :].rearrange("p a n -> p (a n)"),
                                           start=True, stop=True)
                        mm.then_inc(e_s.sem, 1)

                    def group(g, last):
                        gg = pe.snap((2 * b + p) * NG + g)
                        for n in range(KT):
                            if n + 1 < KT:
                                scores(g, n + 1, 0)
                                scores(g, n + 1, 1)
                            elif not last:
                                scores(g + 1, 0, 0)
                                scores(g + 1, 0, 1)
                            for (first, _, _), s, k in zip(VCUTS, s_vg, VDMAS):
                                if n == first:
                                    pe.wait_ge(s, (gg * 16 + 16) * k)
                            e_e.wait(pe, gg * 2 * KT + 2 * n + 2)
                            if n == 0:
                                e_oi.wait(pe, gg)
                            if ORDER[n] == MIX:
                                e_ot.wait(pe, gg)
                            for rows, vt, o, img, first, stop in parts(n):
                                for h in range(4):
                                    mm = pe.matmul(ps[h * HD:(h + 1) * HD, NUM_I if img else NUM_T, :],
                                                   vgrp[0:rows, vt, h * HD:(h + 1) * HD], prob[0:rows, n % 2, h, :],
                                                   start=first, stop=stop)
                                if n not in ADDED:
                                    for h in range(4):
                                        mm = pe.matmul(ps[h * HD:(h + 1) * HD, DEN_I if img else DEN_T, :],
                                                       ones[0:rows, o, :], prob[0:rows, n % 2, h, :], start=first, stop=stop and img)
                            mm.then_inc(e_av.sem, 1)
                            if n == KT - 1:
                                e_ad.wait(pe, gg * NA + NA)
                                e_ap.wait(pe, gg * NA + NA)
                                for h in range(4):
                                    mm = pe.matmul(ps[h * HD:(h + 1) * HD, DEN_T, :], ones[:, 0, :], added[:, h, :],
                                                   start=False, stop=True)
                                mm.then_inc(e_ds.sem, 1)

                    scores(0, 0, 0)
                    scores(0, 0, 1)
                    with pe.Fori(0, NG - 1) as g:
                        group(g, False)
                    group(NG - 1, True)

                def output(chunks):
                    for j in range(QT):
                        steps = [(c, a, z) for c in chunks for a, z in ((0, 0), (0, 1), (1, 0))]
                        for k, (c, a, z) in enumerate(steps):
                            mm = pe.matmul(ps[:, j, :], attn[:, c, a, j * P:(j + 1) * P], wts[:, WO, z, c * D:(c + 1) * D],
                                           start=(c == 0 and k == 0), stop=(c == NC - 1 and k == len(steps) - 1))
                        if NC - 1 in chunks:
                            mm.then_inc(e_po.sem, 1)

                def early_output(p):
                    e_e.wait(pe, (2 * b + p + 1) * NG * 2 * KT)
                    e_at.wait(pe, (2 * b + p + 1) * NG - 1)
                    output(range(NC - 1))

                attention(0)
                early_output(0)
                e_fm.wait(pe, b + 1)
                pe.matmul(ps[0:1, NUM_I, 0:1], total, ones[:, 0, 0:1], start=True, stop=True).then_inc(e_fs.sem, 1)
                with again(pe, b):
                    for j in range(QT):
                        pe.matmul(ps[:, j, :], attn[:, 0, 0, j * P:(j + 1) * P], wts[:, WO, 0, 0:D], start=False, stop=True)
                    score_maxima()
                    attention(1)
                    early_output(1)
                otherwise(pe, ((e_ms, HEADS * QT), (e_mr, 1), (e_s, 2 * KT * NG), (e_av, KT * NG), (e_ds, NG)))
                e_at.wait(pe, (2 * b + 2) * NG)
                e_qz.wait(pe, b + 1)
                output((NC - 1,))


_ORDER_OF_W = ("q_w", "k_w", "v_w", "k_img_w", "v_img_w", "o_w")


def lay_attention(inputs):
    a = {k[len("L0_xattn_"):]: np.asarray(v) for k, v in inputs.items() if k.startswith("L0_xattn_")}
    w6 = np.stack([a[n].T.reshape(NC, P, D).transpose(1, 0, 2).reshape(P, NC * D) for n in _ORDER_OF_W])
    c = np.asarray(inputs["ctx_2048"])
    c = np.concatenate([c[:, IMG:], c[:, :IMG], np.zeros((B, KPAD - TXT - IMG, D), c.dtype)], axis=1)
    c = c.reshape(B, KT, P, NC, P).transpose(0, 1, 4, 3, 2).reshape(B * KT, P, D)
    mark = np.zeros((P - STK, KPAD), np.float16)
    mark[0, :TXT] = SHIFT
    mark[1, TXT:TXT + IMG] = SHIFT
    return {
        "x": np.asarray(inputs["x"]).reshape(T, D), "ctx": c, "w6": w6, "mark": mark,
        "kb": a["k_b"], "kw": a["norm_k_w"], "vb": a["v_b"], "kib": a["k_img_b"], "kiw": a["norm_k_img_w"],
        "vib": a["v_img_b"], "qb": a["q_b"], "qw": a["norm_q_w"], "ob": a["o_b"],
    }


E, TOPK, CAP, I = 32, 4, 80, 256
GRP, TOPG = 8, 3
NT = T // P
I2 = 512
NI = I2 // P
TROW = D + E
DUMMY = P
BIG = 1000.0
RING = 4
IRING = 2 * RING
RSCALE = 2.5
LATE = 3
EVERY = 2
N_FIRST = 4
N_CONST = 10


def ffn_program(nc, d, x1_dram, table, out):
    with ExitStack() as ctx:
        def sb(name, shape, dt):
            return ctx.enter_context(nc.sbuf_tensor("f_" + name, shape, dt))

        s_apart = ctx.enter_context(nc.semaphore("f_s_apart"))

        def apart(eng):
            eng.sem_inc(s_apart, 1)

        events = []

        def event(name, ahead=0):
            e = Event(ctx, nc, "f_" + name, ahead)
            events.append(e)
            return e

        def dma_sem(name):
            return ctx.enter_context(nc.semaphore("f_" + name))

        x1s = sb("x1s", [P, NT, D], F32)
        x2t = sb("x2t", [P, 2, NC, T], F16)
        swt = sb("swt", [P, 3, 2, NC * D], F16)
        SG, SU, SD = range(3)
        rwt = sb("rwt", [P, 2, NC * E], F16)
        rraw = sb("rraw", [P, NC * E], F32)
        xn = sb("xn", [P, 4, D], F32)
        xs = sb("xs", [P, 4, 2, D], F16)
        stat = sb("stat", [P, 4, 16], F32)
        mhalf = sb("mhalf", [P, 1], F32)
        ident = sb("ident", [P, P], F16)
        identf = sb("identf", [P, P], F32)
        zero = sb("zero", [P, TROW], F32)
        wring = sb("wring", [P, RING, 3 * 2 * D], F32)
        ex = sb("ex", [P, D], F32)
        rc = sb("rc", [P, D], F32)
        hs = sb("hs", [P, 2, NI, D], F16)
        ebias = sb("ebias", [P, E], F32)
        rt = [sb(f"rt{i}", [P, NT, E], F32) for i in range(6)]
        gt = [sb(f"gt{i}", [P, NT, GRP], F32) for i in range(6)]
        gidx = sb("gidx", [P, NT, 8], U32)
        top8 = sb("top8", [P, NT, 8], F32)
        io8 = sb("io8", [P, GRP], F32)
        io32 = sb("io32", [P, E], F32)
        m16 = sb("m16", [P, NT, E], F16)
        c16 = sb("c16", [P, NT, E], F16)
        pv16 = sb("pv16", [P, NT, E], F16)
        wsum = sb("wsum", [P, NT], F32)
        before = sb("before", [P, P], F16)
        ones16 = sb("ones16", [P, P], F16)
        ioS = sb("ioS", [P, CAP, E], F16)
        oneh = sb("oneh", [P, 2, CAP, E], F16)
        tok = sb("tok", [P, NT], F16)
        arow_sb = oneh[0:1, :, :, :].rearrange("p a s e -> p (a s e)").bitcast(F32)
        ia = sb("ia", [CAP, E], F32)
        ib = sb("ib", [CAP, E], F32)
        sio = sb("sio", [P, 1], F32)
        idx = sb("idx", [CAP, E], U32)
        idc = [sb(f"idc{i}", [CAP, 1], U32) for i in range(IRING)]
        wc = [sb(f"wc{i}", [CAP, 1], F32) for i in range(RING)]
        free = x2t[:, :, :, :].rearrange("p a c n -> p (a c n)").bitcast(F32)
        at = 0

        def take(rows, width):
            nonlocal at
            at += width
            return free[0:rows, at - width:at]

        xg = [take(CAP, TROW) for i in range(RING)]
        xgt = [take(P, NC * CAP).rearrange("p (c s) -> p c s", c=NC) for i in range(2)]
        ht = [take(P, 2 * CAP).rearrange("p (c s) -> p c s", c=2) for i in range(2)]
        yf = [take(CAP, D) for i in range(2)]
        eg, hh = take(CAP, I), take(CAP, I)
        ps = ctx.enter_context(nc.psum_tensor("f_ps", [P, 8, 512], F32))
        wst = [wring[:, i, 0:NC * D] for i in range(3)]

        s_w = [dma_sem(f"s_w{i}") for i in range(3)]
        s_r, s_tab, s_o, s_ia, s_wt = (dma_sem(n) for n in ("s_r", "s_tab", "s_o", "s_ia", "s_wt"))
        s_xl = [dma_sem(f"s_xl{i}") for i in range(4)]
        s_xt = dma_sem("s_xt")
        s_ring = [dma_sem(f"s_ring{i}") for i in range(RING)]
        s_g = [dma_sem(f"s_g{i}") for i in range(RING)]
        s_sc = dma_sem("s_sc")
        s_i0, s_const = event("s_i0"), event("s_const")
        whi, wlo = event("whi"), event("wlo")
        e_st, e_mv, e_rv, e_rs = event("e_st"), event("e_mv"), event("e_rv"), event("e_rs")
        s_first = event("s_first")
        e_xl = event("e_xl")
        e_xd = event("e_xd", 1)
        e_xn, e_hi, e_xs, e_xt = event("e_xn", 1), event("e_hi"), event("e_xs"), event("e_xt", 4)
        e_xsp = event("e_xsp", 1)
        e_x2, e_x2a = event("e_x2", 2), event("e_x2a", 2)
        e_r = event("e_r")
        e_ez = event("e_ez")
        link = event("link")
        e_m16, e_pos, e_oh, e_a, e_ar, e_wv, e_idx = (event(n) for n in (
            "e_m16", "e_pos", "e_oh", "e_a", "e_ar", "e_wv", "e_idx"))
        e_a2 = event("e_a2")
        f_gu, f_e, f_t, f_h, f_hi, f_lo = (event(n, a) for n, a in (
            ("f_gu", 0), ("f_e", 0), ("f_t", 1), ("f_h", 1), ("f_hi", 0), ("f_lo", 2)))
        f_dn, f_ac = event("f_dn"), event("f_ac", 2)
        m_ix = event("m_ix")
        m_xt = event("m_xt")
        m_xc = event("m_xc", 1)
        m_w = event("m_w", 1)
        m_gu = event("m_gu")
        m_e = event("m_e")
        m_t = event("m_t", 1)
        m_h = event("m_h", 2)
        m_ht = event("m_ht", 1)
        m_hc = event("m_hc", 1)
        m_y = event("m_y", 2)
        m_yf = event("m_yf", 2)

        block = ctx.enter_context(nc.Block())

        ROUTER, POSITION = 6, 7

        def slot_row(k):
            return (32 * k, 6) if k < 4 else (0, 7)

        def turned_parts(u):
            return ps[:, u, :].bitcast(F16).rearrange("p (k n) -> p k n", n=P)

        def x2t_tile(j):
            return x2t[:, :, :, bass.ds(j * P, P)].rearrange("p a c n -> p (a c) n")

        def copied(eng, bk, u):
            (e_x2 if u % 2 == 0 else e_x2a).wait(eng, bk * 2 + u // 2 + 1)

        def x1_rows(j, k=1):
            return x1_dram[j * P:(j + k) * P, :].rearrange("(k p) n -> p k n", p=P)

        @block.sync
        def _(sp):
            for e in events:
                if e.ahead:
                    sp.sem_inc(e.sem, e.ahead)
            sp.dma_start(rraw[:, :], d["rw"]).then_inc(s_r, 16)
            sp.dma_start(ebias[:, :], d["ebias"].partition_broadcast(P)).then_inc(s_r, 16)
            for k in range(4):
                sp.dma_start(x1s[:, 4 * k:4 * k + 4, :], x1_rows(4 * k, 4)).then_inc(s_xl[k], 16)
            for i in range(3):
                sp.dma_start(wst[i], d["w3"][i]).then_inc(s_w[i], 16)
            for s in s_xl:
                sp.wait_ge(s, 16)
                sp.sem_inc(e_xl.sem, 1)
            s_first.wait(sp, N_FIRST)
            sp.dma_start(table[T:T + DUMMY, :], zero[:, :]).then_inc(s_tab, 16)
            sp.dma_start(out[T:T + DUMMY, :], zero[:, 0:D]).then_inc(s_o, 16)
            with sp.Fori(0, NT // 4) as bk:
                e_xn.wait(sp, bk * 4 + 4)
                sp.dma_start(table[bass.ds(bk * 4 * P, 4 * P), 0:D].rearrange("(u p) n -> p u n", p=P),
                             xn[:, :, :]).then_inc(s_xt, 16)
                sp.wait_ge(s_xt, bk * 16 + 16)
                sp.sem_inc(e_xd.sem, 1)
            wlo.wait(sp, 3)
            for e in range(RING):
                sp.dma_start(wring[:, e, :], d["wx"][e]).then_inc(s_ring[e], 16)
            e_wv.wait(sp, 1)
            sp.dma_start(table[0:T, D:TROW].rearrange("(j p) n -> p j n", p=P), rt[5][:, :, :]).then_inc(s_wt, 16)
            with sp.Fori(0, NT // 4) as bk:
                for q in range(4):
                    j = bk * 4 + q
                    f_ac.wait(sp, j + 1)
                    sp.dma_start(out[bass.ds(j * P, P), :], x1s[:, bass.ds(j, 1), :].rearrange("p a n -> p (a n)")).then_inc(s_o, 16)
            e_ar.wait(sp, 1)
            sp.dma_start(ia[:, :], arow_sb.rearrange("a (s e) -> a s e", e=E)).then_inc(s_ia, 16)
            with sp.Fori(0, E // RING - 1) as o:
                for k in range(RING):
                    m_y.wait(sp, o * RING + k + 1)
                    sp.dma_start(wring[:, k, :], d["wx"][bass.ds((o + 1) * RING + k, 1)].rearrange("a p n -> (a p) n")).then_inc(s_ring[k], 16)
            sp.wait_ge(s_o, 16 * (NT + 1))
            sp.wait_ge(s_sc, 16 * E)


        @block.gpsimd
        def _(pool):
            c, first = s_const.sem, s_first.sem
            pool.memset(ident[:, :], 0.0).then_inc(s_i0.sem, 1)
            pool.memset(identf[:, :], 0.0).then_inc(s_i0.sem, 1)
            pool.memset(before[:, :], 1.0).then_inc(s_i0.sem, 1)
            s_i0.wait(pool, 3)
            pool.affine_select(out=ident[:, :], in_=ident[:, :], pattern=[[-1, P]], compare_op=ALU.not_equal, fill=1.0,
                               base=0, channel_multiplier=1).then_inc(first, 1)
            pool.memset(mhalf[:, :], -0.5).then_inc(first, 1)
            pool.memset(zero[:, :], 0.0).then_inc(first, 1)
            s_first.wait(pool, N_FIRST)
            def deviations(bk):
                e_mv.wait(pool, bk * 4 + 4)
                apart(pool)
                pool.tensor_scalar(stat[:, :, 9], stat[:, :, 7], 1.0, 1e-5, ALU.mult, ALU.add).then_inc(e_rv.sem, 1)
                e_rv.wait(pool, bk + 1)
                pool.tensor_tensor(stat[:, :, 8], stat[:, :, 9], mhalf[:, 0:1].to_broadcast([P, 4]), ALU.pow).then_inc(e_rs.sem, 1)

            def low(bk):
                for k, u in enumerate((1, 3)):
                    e_hi.wait(pool, bk * 4 + u + 1)
                    e_xt.wait(pool, bk * 4 + u - 3)
                    pool.tensor_tensor(xs[:, u, 1, :], xn[:, u, :], xs[:, u, 0, :], ALU.subtract).then_inc(e_xsp.sem, 1)

            deviations(0)
            with pool.Fori(0, NT // 4 - 1) as bk:
                deviations(bk + 1)
                low(bk)
            low(NT // 4 - 1)
            pool.affine_select(out=identf[:, :], in_=identf[:, :], pattern=[[-1, P]], compare_op=ALU.not_equal, fill=1.0,
                               base=0, channel_multiplier=1).then_inc(c, 1)
            pool.affine_select(out=before[:, :], in_=before[:, :], pattern=[[1, P]], compare_op=ALU.is_gt, fill=0.0,
                               base=0, channel_multiplier=-1).then_inc(c, 1)
            pool.memset(ones16[:, :], 1.0).then_inc(c, 1)
            pool.iota(io8[:, :], [[1, GRP]], base=0, channel_multiplier=0, allow_small_or_imprecise_dtypes=True).then_inc(c, 1)
            pool.iota(io32[:, :], [[1, E]], base=0, channel_multiplier=0, allow_small_or_imprecise_dtypes=True).then_inc(c, 1)
            pool.iota(ioS[:, :, :], [[1, CAP], [0, E]], base=0, channel_multiplier=0, allow_small_or_imprecise_dtypes=True).then_inc(c, 1)
            pool.iota(tok[:, :], [[P, NT]], base=-T, channel_multiplier=1, allow_small_or_imprecise_dtypes=True).then_inc(c, 1)
            pool.iota(sio[:, :], [[1, 1]], base=0, channel_multiplier=1, allow_small_or_imprecise_dtypes=True).then_inc(c, 1)
            pool.memset(c16[:, 0, :], 0.0).then_inc(c, 1)
            s_const.wait(pool, N_CONST)
            e_idx.wait(pool, 1)
            pool.wait_ge(s_tab, 16)
            pool.wait_ge(s_wt, 16)
            pool.wait_ge(s_xt, 16 * (NT // 4))

            f_ac.wait(pool, NT)

            def gather(n, i):
                pool.tensor_copy(idc[i][:, :], idx[:, bass.ds(n - 1, 1)]).then_inc(m_ix.sem, 1)
                m_ix.wait(pool, n)
                apart(pool)
                pool.indirect_dma_start(out=xg[i % RING], out_offset=None, in_=table[:, :],
                                        in_offset=bass.IndirectOffsetOnAxis(ap=idc[i][:, 0:1], axis=0)).then_inc(
                    s_g[i % RING], 16)

            def scatter(n, i):
                m_yf.wait(pool, n)
                apart(pool)
                pool.indirect_dma_start(out=out[:, :], out_offset=bass.IndirectOffsetOnAxis(ap=idc[i][:, 0:1], axis=0),
                                        in_=yf[i % 2], in_offset=None, compute_op=ALU.add).then_inc(s_sc, 16)

            for i in range(RING):
                gather(i + 1, i)
            pool.wait_ge(s_o, 16 * (NT + 1))

            def experts(o, last):
                for k in range(IRING):
                    n = o * IRING + k + 1
                    if not (last and k >= RING):
                        m_xt.wait(pool, n)
                        m_w.wait(pool, n)
                        gather(n + RING, (k + RING) % IRING)
                    scatter(n, k)
                    pool.wait_ge(s_sc, n * 16)

            with pool.Fori(0, E // IRING - 1) as o:
                experts(o, False)
            experts(E // IRING - 1, True)

        @block.scalar
        def _(act):
            act.wait_ge(s_r, 32)
            act.activation(rwt[:, 0, :], rraw[:, :], ACT.Copy, scale=WS).then_inc(whi.sem, 1)
            with act.Fori(0, NT // 4) as bk:
                for u in range(4):
                    e_xn.wait(act, bk * 4 + u + 1)
                    e_xt.wait(act, bk * 4 + u - 3)
                    act.copy(xs[:, u, 0, :], xn[:, u, :]).then_inc(e_hi.sem, 1)
                for u in (1, 3):
                    e_xt.wait(act, bk * 4 + u + 1)
                    act.copy(x2t_tile(bk * 4 + u), turned_parts(u)).then_inc(e_x2a.sem, 1)
            for i in range(3):
                act.wait_ge(s_w[i], 16)
                act.activation(swt[:, i, 0, :], wst[i], ACT.Copy, scale=WS).then_inc(whi.sem, 1)
            e_r.wait(act, 1)
            act.activation(rt[0].rearrange("p j e -> p (j e)"), ps[:, ROUTER, :], ACT.Exp, scale=-1.0 / WS).then_inc(e_ez.sem, 1)
            with act.Fori(0, NT // 4) as bk:
                for it in range(NI):
                    n = act.snap(bk * NI + it + 1)
                    f_gu.wait(act, n)
                    f_t.wait(act, n - 1)
                    act.activation(ex[:, :], ps[:, it % 2, :], ACT.Tanh, scale=0.5 / WS).then_inc(f_e.sem, 1)
                    f_h.wait(act, n)
                    act.copy(hs[:, 0, it, :], rc[:, :]).then_inc(f_hi.sem, 1)
            e_a.wait(act, 1)
            for k in range(CAP * E // 512):
                row, bank = slot_row(k)
                cp = act.copy(arow_sb[:, k * 512:(k + 1) * 512], ps[row:row + 1, bank, :])
            cp.then_inc(e_ar.sem, 1)

            def expert(n, u):
                m_gu.wait(act, n)
                m_t.wait(act, n - 1)
                act.activation(eg, ps[0:CAP, 7 if u % 2 == 0 else 0, 0:I], ACT.Tanh, scale=0.5).then_inc(m_e.sem, 1)
                m_y.wait(act, n)
                m_w.wait(act, n)
                if not isinstance(n, int):
                    act.wait_ge(s_sc, (n - 2) * 16)
                act.activation(yf[u % 2], ps[0:CAP, 2 + u % 2, :], ACT.Copy, scale=wc[u][:, 0:1]).then_inc(m_yf.sem, 1)

            for u in range(RING):
                if u >= 2:
                    act.wait_ge(s_sc, (u - 1) * 16)
                expert(u + 1, u)
            with act.Fori(1, E // RING) as o:
                for u in range(RING):
                    expert(act.snap(o * RING + u + 1), u)

        @block.vector
        def _(dve):
            count = [0]

            def chain(ins):
                count[0] += 1
                ins.then_inc(link.sem, 1)
                link.wait(dve, count[0])

            dve.memset(stat[:, :, :], 0.0).then_inc(s_first.sem, 1)
            dve.memset(ia[:, :], 0.0).then_inc(s_const.sem, 1)
            s_first.wait(dve, N_FIRST)
            whi.wait(dve, 1)
            chain(dve.scalar_tensor_tensor(rwt[:, 1, :], rraw[:, :], WS, rwt[:, 0, :], ALU.mult, ALU.subtract))
            xj = lambda bk, u: x1s[:, bass.ds(bk * 4 + u, 1), :].rearrange("p a n -> p (a n)")

            def stats(bk):
                e_xl.wait(dve, bk + 1)
                for u in range(4):
                    dve.bn_stats(stat[:, u, 0:6], xj(bk, u)).then_inc(e_st.sem, 1)
                e_xn.wait(dve, bk * 4)
                for u in range(4):
                    e_st.wait(dve, bk * 4 + u + 1)
                    apart(dve)
                    dve.bn_aggr(stat[:, u, 6:8], stat[:, u, 0:6]).then_inc(e_mv.sem, 1)

            def norms(bk, last):
                e_rs.wait(dve, bk + 1)
                e_xd.wait(dve, bk)
                e_xsp.wait(dve, bk * 2)
                for u in range(4):
                    dve.tensor_scalar(xn[:, u, :], xj(bk, u), stat[:, u, 6:7], stat[:, u, 8:9], ALU.subtract,
                                      ALU.mult).then_inc(e_xn.sem, 1)
                if not last:
                    stats(bk + 1)
                for u in (0, 2):
                    e_hi.wait(dve, bk * 4 + u + 1)
                    e_xt.wait(dve, bk * 4 + u - 3)
                    dve.tensor_tensor(xs[:, u, 1, :], xn[:, u, :], xs[:, u, 0, :], ALU.subtract).then_inc(e_xs.sem, 1)
                for u in (0, 2):
                    e_xt.wait(dve, bk * 4 + u + 1)
                    dve.tensor_copy(x2t_tile(bk * 4 + u), turned_parts(u)).then_inc(e_x2.sem, 1)

            stats(0)
            with dve.Fori(0, NT // 4 - 1) as bk:
                norms(bk, False)
            norms(NT // 4 - 1, True)
            for i in range(3):
                whi.wait(dve, i + 2)
                dve.scalar_tensor_tensor(swt[:, i, 1, :], wst[i], WS, swt[:, i, 0, :], ALU.mult,
                                         ALU.subtract).then_inc(wlo.sem, 1)

            def shared(first, end):
                for bk in range(first, end):
                    for it in range(NI):
                        n = bk * NI + it + 1
                        f_e.wait(dve, n)
                        f_lo.wait(dve, n - 1)
                        dve.scalar_tensor_tensor(rc[:, :], ex[:, :], 1.0, ps[:, it % 2, :], ALU.add,
                                                 ALU.mult).then_inc(f_t.sem, 1)
                        f_t.wait(dve, n)
                        dve.scalar_tensor_tensor(rc[:, :], rc[:, :], 0.5 / WS / WS, ps[:, 2 + it % 2, :], ALU.mult,
                                                 ALU.mult).then_inc(f_h.sem, 1)
                        yield
                        f_hi.wait(dve, n)
                        TT(hs[:, 1, it, :], rc[:, :], hs[:, 0, it, :], ALU.subtract).then_inc(f_lo.sem, 1)
                        yield
                    for _ in range(LATE):
                        yield
                    for q in range(4):
                        n = bk * 4 + q + 1
                        f_dn.wait(dve, n)
                        xq = x1s[:, bk * 4 + q, :]
                        dve.scalar_tensor_tensor(xq, ps[:, 4 + q % 2, :], 1.0 / WS, xq, ALU.mult, ALU.add).then_inc(f_ac.sem, 1)
                    yield

            ops = [0]

            def step(ins):
                chain(ins)
                ops[0] += 1
                if ops[0] % EVERY == 0:
                    next(rest[0], None)

            TT = dve.tensor_tensor
            fl = lambda t: t.rearrange("p j e -> p (j e)")
            scores, sc, masked, mask, tmp, wv = rt
            s_const.wait(dve, N_CONST)
            e_ez.wait(dve, 1)
            rest = [shared(0, 2)]
            step(dve.tensor_scalar(fl(tmp), fl(scores), 1.0, None, ALU.add))
            step(dve.reciprocal(fl(scores), fl(tmp)))
            step(TT(sc[:, :, :], scores[:, :, :], ebias[:, :].unsqueeze(1).to_broadcast([P, NT, E]), ALU.add))
            q4 = sc[:, :, :].rearrange("p j (g k) -> p (j g) k", k=4)
            G = [t[:, :, :].rearrange("p j g -> p (j g)") for t in gt]
            step(TT(G[0], q4[:, :, 0], q4[:, :, 1], ALU.max))
            step(TT(G[1], q4[:, :, 0], q4[:, :, 1], ALU.min))
            step(TT(G[2], q4[:, :, 2], q4[:, :, 3], ALU.max))
            step(TT(G[3], q4[:, :, 2], q4[:, :, 3], ALU.min))
            step(TT(G[4], G[0], G[2], ALU.max))
            step(TT(G[5], G[0], G[2], ALU.min))
            step(TT(G[0], G[1], G[3], ALU.max))
            step(TT(G[1], G[5], G[0], ALU.max))
            step(TT(G[2], G[4], G[1], ALU.add))

            def top(values):
                for j in range(NT):
                    ins = dve.max(top8[:, j, :], values[:, j, :])
                step(ins)
                for j in range(NT):
                    ins = dve.max_index(gidx[:, j, :], top8[:, j, :], values[:, j, :])
                step(ins)
                step(dve.tensor_copy(gt[5][:, :, :], gidx[:, :, :]))

            def chosen(outm, t, k, iota, n):
                for r in range(k):
                    dst = outm if r == 0 else t
                    step(TT(dst[:, :, :], gt[5][:, :, r:r + 1].to_broadcast([P, NT, n]),
                             iota[:, :].unsqueeze(1).to_broadcast([P, NT, n]), ALU.is_equal))
                    if r:
                        step(TT(outm[:, :, :], outm[:, :, :], t[:, :, :], ALU.add))

            top(gt[2])
            chosen(gt[0], gt[1], TOPG, io8, GRP)
            step(TT(masked[:, :, :].rearrange("p j (g k) -> p (j g) k", k=4), q4,
                     G[0].unsqueeze(2).to_broadcast([P, NT * GRP, 4]), ALU.mult))
            step(dve.tensor_scalar(fl(masked), fl(masked), 0.0, None, ALU.add))
            top(masked)
            chosen(mask, tmp, TOPK, io32, E)
            step(TT(fl(tmp), fl(scores), fl(mask), ALU.mult))
            step(dve.tensor_reduce(wsum[:, :], tmp[:, :, :], mybir.AxisListType.X, ALU.add))
            step(dve.tensor_scalar(wsum[:, :], wsum[:, :], 1e-20, None, ALU.add))
            step(dve.reciprocal(wsum[:, :], wsum[:, :]))
            step(dve.scalar_tensor_tensor(wv[:, :, :], tmp[:, :, :], RSCALE, wsum[:, :].unsqueeze(2).to_broadcast([P, NT, E]),
                                           ALU.mult, ALU.mult))
            step(dve.tensor_copy(fl(m16), fl(mask)))
            for j in range(1, NT):
                step(TT(c16[:, j, :], c16[:, j - 1, :], m16[:, j - 1, :], ALU.add))
            dve.sem_inc(e_m16.sem, 1)
            for _ in rest[0]:
                pass
            rest[0] = shared(2, 4)
            e_pos.wait(dve, 1)
            chain(dve.scalar_tensor_tensor(fl(tmp), ps[:, POSITION, :], float(CAP), fl(mask), ALU.is_lt, ALU.mult))
            chain(TT(fl(wv), fl(wv), fl(tmp), ALU.mult))
            dve.sem_inc(e_wv.sem, 1)
            chain(dve.scalar_tensor_tensor(fl(masked), ps[:, POSITION, :], -BIG, fl(tmp), ALU.add, ALU.mult))
            chain(dve.tensor_scalar(fl(pv16), fl(masked), BIG, None, ALU.add))
            for j in range(NT):
                if j >= 2:
                    e_a2.wait(dve, j - 1)
                TT(oneh[:, j % 2, :, :], ioS[:, :, :], pv16[:, j, :].unsqueeze(1).to_broadcast([P, CAP, E]),
                   ALU.is_equal).then_inc(e_oh.sem, 1)
                for _ in range({3: 2, 5: 2, 7: 4, 9: 1 + LATE, 11: 2, 13: 2}.get(j, 0)):
                    next(rest[0])
            for _ in rest[0]:
                pass
            dve.wait_ge(s_ia, 16)
            chain(dve.tensor_scalar(ib[:, :], ia[:, :], 0.0, None, ALU.is_equal))
            chain(dve.tensor_scalar(ib[:, :], ib[:, :], sio[0:CAP, 0:1], None, ALU.mult))
            chain(dve.scalar_tensor_tensor(ib[:, :], ia[:, :], float(T), ib[:, :], ALU.add, ALU.add))
            dve.tensor_copy(idx[:, :], ib[:, :]).then_inc(e_idx.sem, 1)

            def rows(n, u, count):
                m_xt.wait(dve, n)
                dve.tensor_copy(xgt[u % 2].rearrange("p c s -> p (c s)"), ps[:, 6, 0:NC * CAP]).then_inc(m_xc.sem, 1)
                dve.wait_ge(s_g[u], count)
                m_yf.wait(dve, n - RING)
                dve.tensor_copy(wc[u][:, :], xg[u][:, bass.ds(n - 1 + D, 1)]).then_inc(m_w.sem, 1)

            def hidden(n, u):
                gu = ps[0:CAP, 7 if u % 2 == 0 else 0, :]
                m_e.wait(dve, n)
                m_ht.wait(dve, n - 1)
                dve.scalar_tensor_tensor(hh, eg, 1.0, gu[:, 0:I], ALU.add, ALU.mult).then_inc(m_t.sem, 1)
                m_t.wait(dve, n)
                dve.scalar_tensor_tensor(hh, hh, 0.5, gu[:, I:2 * I], ALU.mult, ALU.mult).then_inc(m_h.sem, 1)
                m_ht.wait(dve, n)
                dve.tensor_copy(ht[u % 2].rearrange("p c s -> p (c s)"), ps[:, 1, 0:2 * CAP]).then_inc(m_hc.sem, 1)

            rows(1, 0, 16)
            rows(2, 1, 16)

            def experts(o, last):
                for k in range(RING):
                    n = o * RING + k + 1
                    hidden(n, k)
                    if not (last and k >= RING - 2):
                        rows(n + 2, (k + 2) % RING, o * 16 + (16 if k < 2 else 32))

            with dve.Fori(0, E // RING - 1) as o:
                experts(o, False)
            experts(E // RING - 1, True)

        @block.tensor
        def _(pe):
            s_first.wait(pe, N_FIRST)
            PARTS = ((0, 0), (0, 1), (1, 0))

            def product(out_, lhs, rhs, chunks):
                steps = [(c, a, z) for c in range(chunks) for a, z in PARTS]
                for k, (c, a, z) in enumerate(steps):
                    mm = pe.matmul(out_, lhs(a, c), rhs(z, c), start=(k == 0), stop=(k == len(steps) - 1))
                return mm

            link.wait(pe, 1)
            with pe.Fori(0, NT // 4) as bk:
                for u in range(4):
                    m = pe.snap(bk * 4 + u + 1)
                    (e_xs if u % 2 == 0 else e_xsp).wait(pe, bk * 2 + u // 2 + 1)
                    copied(pe, bk - 1, u)
                    for a in range(2):
                        for c in range(NC):
                            tr = pe.transpose(turned_parts(u)[:, a * NC + c, :], xs[:, u, a, c * P:(c + 1) * P], ident[:, :])
                    tr.then_inc(e_xt.sem, 1)
                for u in range(4):
                    j = bk * 4 + u
                    copied(pe, bk, u)
                    product(ps[:, ROUTER, bass.ds(j * E, E)], lambda a, c: x2t[:, a, c, bass.ds(j * P, P)],
                            lambda z, c: rwt[:, z, c * E:(c + 1) * E], NC)
            pe.drain().then_inc(e_r.sem, 1)

            def slots_of(j, half):
                e_oh.wait(pe, j + 1)
                flat = oneh[:, half, :, :].rearrange("p s e -> p (s e)")
                for k in range(CAP * E // 512):
                    row, bank = slot_row(k)
                    mm = pe.matmul(ps[row:row + 1, bank, :], tok[:, j:j + 1], flat[:, k * 512:(k + 1) * 512],
                                   start=(j == 0), stop=(j == NT - 1))
                mm.then_inc(e_a2.sem, 1)

            def shared(bk, slots):
                for it in range(NI):
                    n = bk * NI + it + 1
                    f_lo.wait(pe, n - 2)
                    for w, bank in ((SG, it % 2), (SU, 2 + it % 2)):
                        mm = product(ps[:, bank, :], lambda a, c: swt[:, w, a, c * D + it * P:c * D + (it + 1) * P],
                                     lambda z, c: x2t[:, z, c, bass.ds(bk * 512, 512)], NC)
                    mm.then_inc(f_gu.sem, 1)
                    for j in slots[2 * it:2 * it + 2]:
                        slots_of(j, j % 2)
                f_lo.wait(pe, bk * NI + NI)
                for q in range(4):
                    n = bk * 4 + q + 1
                    f_ac.wait(pe, n - 2)
                    product(ps[:, 4 + q % 2, :], lambda a, c: hs[:, a, c, q * P:(q + 1) * P],
                            lambda z, c: swt[:, SD, z, c * D:(c + 1) * D], NI).then_inc(f_dn.sem, 1)

            wlo.wait(pe, 3)
            with pe.Fori(0, 2) as bk:
                shared(bk, ())
            s_const.wait(pe, N_CONST)
            e_m16.wait(pe, 1)
            flat = lambda t: t[:, :, :].rearrange("p j e -> p (j e)")
            pe.matmul(ps[:, POSITION, :], before[:, :], flat(m16), start=True, stop=False)
            pe.matmul(ps[:, POSITION, :], ones16[:, :], flat(c16), start=False, stop=True).then_inc(e_pos.sem, 1)
            shared(2, range(8))
            shared(3, range(8, NT))
            e_a2.wait(pe, NT)
            pe.sem_inc(e_a.sem, 1)

            def turn_rows(n, u, count):
                pe.wait_ge(s_g[u], count)
                m_xc.wait(pe, n - 1)
                for c in range(NC):
                    tr = pe.transpose(ps[:, 6, c * CAP:(c + 1) * CAP], xg[u][:, c * P:(c + 1) * P], identf[0:CAP, 0:CAP])
                tr.then_inc(m_xt.sem, 1)

            def gate_up(n, u, count):
                pe.wait_ge(s_ring[u], count)
                m_xc.wait(pe, n)
                m_h.wait(pe, n - 2)
                for c in range(NC):
                    mm = pe.matmul(ps[0:CAP, 7 if u % 2 == 0 else 0, :], xgt[u % 2][:, c, :], wring[:, u, c * 512:(c + 1) * 512],
                                   start=(c == 0), stop=(c == NC - 1))
                mm.then_inc(m_gu.sem, 1)

            def turn_hidden(n):
                m_h.wait(pe, n)
                m_hc.wait(pe, n - 1)
                for c in range(2):
                    tr = pe.transpose(ps[:, 1, c * CAP:(c + 1) * CAP], hh[:, c * P:(c + 1) * P], identf[0:CAP, 0:CAP])
                tr.then_inc(m_ht.sem, 1)

            def down(n, u):
                m_hc.wait(pe, n)
                m_yf.wait(pe, n - 2)
                for c in range(2):
                    mm = pe.matmul(ps[0:CAP, 2 + u % 2, :], ht[u % 2][:, c, :], wring[:, u, 2048 + c * D:2048 + (c + 1) * D],
                                   start=(c == 0), stop=(c == 1))
                mm.then_inc(m_y.sem, 1)

            f_ac.wait(pe, NT)
            e_ar.wait(pe, 1)
            turn_rows(1, 0, 16)
            turn_rows(2, 1, 16)
            gate_up(1, 0, 16)

            def experts(o, last):
                for k in range(RING):
                    n = o * RING + k + 1
                    if not (last and k == RING - 1):
                        gate_up(n + 1, (k + 1) % RING, o * 16 + (16 if k < RING - 1 else 32))
                    turn_hidden(n)
                    if not (last and k >= RING - 2):
                        turn_rows(n + 2, (k + 2) % RING, o * 16 + (16 if k < 2 else 32))
                    down(n, k)

            with pe.Fori(0, E // RING - 1) as o:
                experts(o, False)
            experts(E // RING - 1, True)


def lay_ffn(inputs):
    f = {k[len("L0_ffn_"):]: np.asarray(v) for k, v in inputs.items() if k.startswith("L0_ffn_")}

    def chunks(w):
        k, n = w.shape
        return w.reshape(k // P, P, n).transpose(1, 0, 2).reshape(P, -1)
    w3 = np.stack([chunks(f["shared_gate"].T), chunks(f["shared_up"].T), chunks(f["shared_down"].T)])
    gu = np.concatenate([f["W_gate"], f["W_up"]], axis=2).reshape(E, NC, P, 2 * I).transpose(0, 2, 1, 3).reshape(E, P, -1)
    dn = f["W_down"].reshape(E, 2, P, D).transpose(0, 2, 1, 3).reshape(E, P, -1)
    return {"rw": chunks(f["router_w"].T), "ebias": f["e_bias"], "w3": w3, "wx": np.concatenate([gu, dn], axis=2)}


def build(nc, d, out):
    x1_dram = nc.dram_tensor("x1", (T, D), F32).ap()
    table = nc.dram_tensor("table", (T + DUMMY, TROW), F32).ap()
    attention_program(nc, d, x1_dram)
    ffn_program(nc, d, x1_dram, table, out)


def kernel(**inputs):
    import concourse.bacc as bacc
    from concourse.bass_utils import run_bass_kernel_spmd

    arrays = {**lay_attention(inputs), **lay_ffn(inputs)}
    arrays = {f"in_{n}": np.ascontiguousarray(a) for n, a in arrays.items()}
    nc = bacc.Bacc("TRN2", target_bir_lowering=False, num_devices=1)
    d = {n[3:]: nc.dram_tensor(n, a.shape, mybir.dt.from_np(a.dtype), kind="ExternalInput").ap()
         for n, a in arrays.items()}
    out = nc.dram_tensor("out", (T + DUMMY, D), F32, kind="ExternalOutput").ap()
    build(nc, d, out)
    result = run_bass_kernel_spmd(nc, [arrays], core_ids=[0]).results[0]["out"]
    return result[:T].reshape(B, L, D)
```
